# Optimizing a Trainium2 kernel written in Bass

```python
import numpy as np
import jax
import jax.numpy as jnp

def _softmax(x, axis=-1):
    return jax.nn.softmax(x, axis=axis)

def _gelu(x):
    return jax.nn.gelu(x, approximate=True)

def _silu(x):
    return jax.nn.silu(x)

def _sigmoid(x):
    return jax.nn.sigmoid(x)

def _layernorm(x, axis=-1, eps=1e-05):
    m = jnp.mean(x, axis=axis, keepdims=True)
    v = jnp.var(x, axis=axis, keepdims=True)
    return (x - m) / jnp.sqrt(v + eps)

def _scatter_add(tgt, idx, src, axis=0):
    return tgt.at[idx].add(src)

def _segment_sum(src, seg, n):
    return jax.ops.segment_sum(src, seg, n)
kernel_name = 'mk_flamingo_gated_d2_seqx_r8_7b5e3c'

def setup_inputs(seed: int=0):
    np.random.seed(seed)
    _w = jnp.asarray

    def _rec_inputs():
        import jax
        import jax.numpy as jnp
        _rk = jax.random.key(seed)
        x = -0.0002928 + 1 * jax.random.normal(jax.random.fold_in(_rk, 1), (128, 64, 128), jnp.float32)
        _lenS = 64 - jax.random.randint(jax.random.fold_in(_rk, 7), (128,), 0, max(1, 64 // 4) + 1, jnp.int32)
        _lenS2 = 64 - jax.random.randint(jax.random.fold_in(_rk, 8), (128,), 0, max(1, 64 // 4) + 1, jnp.int32)
        _ctx_1024P = jax.random.normal(jax.random.fold_in(_rk, 11), (128, 16, 128), jnp.float32)
        _ctx_1024c = jax.random.dirichlet(jax.random.fold_in(_rk, 511), 0.3 * jnp.ones((16,), jnp.float32), (128, 64))
        _ctx_1024t = jnp.einsum('bsk,bkd->bsd', _ctx_1024c, _ctx_1024P)
        _ctx_1024t = _ctx_1024t * jax.lax.rsqrt(jnp.mean(jnp.square(_ctx_1024t)) + 1e-12) * 0.953939
        ctx_1024 = -1.39393e-06 + 0.999914 * (_ctx_1024t + 0.3 * jax.random.normal(jax.random.fold_in(_rk, 611), (128, 64, 128), jnp.float32))
        _g = jax.random.normal(jax.random.fold_in(_rk, 9001), (2, 2), jnp.float32)
        _g = jnp.sign(_g) * jnp.maximum(jnp.abs(_g), 1.0) + (_g == 0) * 1.0
        g_xattn = _g[0]
        g_ffn = _g[1]
        return (x, ctx_1024, g_xattn, g_ffn)
    x, ctx_1024, g_xattn, g_ffn = _rec_inputs()

    def _L0_xattn_setup():
        import jax, jax.numpy as jnp
        import numpy as np
        import math
        D_MODEL = 128
        N_HEADS = 16
        D_HEAD = D_MODEL // N_HEADS
        key = jax.random.key(seed)
        ks = jax.random.split(key, 11)
        N, L, S = (2, 256, 256)
        inp = {'queries': jax.random.normal(ks[0], (N, L, D_MODEL), dtype=jnp.float32), 'keys': jax.random.normal(ks[1], (N, S, D_MODEL), dtype=jnp.float32), 'values': jax.random.normal(ks[2], (N, S, D_MODEL), dtype=jnp.float32), 'Wq': jax.random.normal(ks[3], (D_MODEL, N_HEADS * D_HEAD), dtype=jnp.float32) / math.sqrt(D_MODEL), 'bq': jnp.zeros((N_HEADS * D_HEAD,), dtype=jnp.float32), 'Wk': jax.random.normal(ks[4], (D_MODEL, N_HEADS * D_HEAD), dtype=jnp.float32) / math.sqrt(D_MODEL), 'bk': jnp.zeros((N_HEADS * D_HEAD,), dtype=jnp.float32), 'Wv': jax.random.normal(ks[5], (D_MODEL, N_HEADS * D_HEAD), dtype=jnp.float32) / math.sqrt(D_MODEL), 'bv': jnp.zeros((N_HEADS * D_HEAD,), dtype=jnp.float32), 'Wo': jax.random.normal(ks[6], (N_HEADS * D_HEAD, D_MODEL), dtype=jnp.float32) / math.sqrt(N_HEADS * D_HEAD), 'bo': jnp.zeros((D_MODEL,), dtype=jnp.float32)}
        return inp
    _L0_xattn_all = _L0_xattn_setup()
    _L0_xattn_in = {k: v for k, v in _L0_xattn_all.items() if k in ('Wq', 'bq', 'Wk', 'bk', 'Wv', 'bv', 'Wo', 'bo')}
    del _L0_xattn_all

    def _L0_ffn_setup():
        import jax, jax.numpy as jnp
        import numpy as np
        B, SEQ, D, E, F = (4, 128, 128, 8, 512)
        CAPACITY = 2
        key = jax.random.key(seed)
        ks = jax.random.split(key, 8)
        x = jax.random.normal(ks[0], (B, SEQ, D), jnp.float32)
        gate_weight = jax.random.normal(ks[1], (E, D), jnp.float32) * 0.006
        W1 = jax.random.normal(ks[2], (E, D, F), jnp.float32) * (1.0 / np.sqrt(D))
        b1 = jnp.zeros((E, F), jnp.float32)
        W2 = jax.random.normal(ks[3], (E, F, D), jnp.float32) * (1.0 / np.sqrt(F))
        b2 = jnp.zeros((E, D), jnp.float32)
        Ws1 = jax.random.normal(ks[4], (D, F), jnp.float32) * (1.0 / np.sqrt(D))
        bs1 = jnp.zeros((F,), jnp.float32)
        Ws2 = jax.random.normal(ks[5], (F, D), jnp.float32) * (1.0 / np.sqrt(F))
        bs2 = jnp.zeros((D,), jnp.float32)
        return {'x': x, 'gate_weight': gate_weight, 'W1': W1, 'b1': b1, 'W2': W2, 'b2': b2, 'Ws1': Ws1, 'bs1': bs1, 'Ws2': Ws2, 'bs2': bs2}
    _L0_ffn_all = _L0_ffn_setup()
    _L0_ffn_in = {k: v for k, v in _L0_ffn_all.items() if k in ('gate_weight', 'W1', 'b1', 'W2', 'b2', 'Ws1', 'bs1', 'Ws2', 'bs2')}
    del _L0_ffn_all

    def _L1_xattn_setup():
        import jax, jax.numpy as jnp
        import numpy as np
        from functools import partial
        FACTOR = 5
        N_HEADS = 16

        def _time_delay_agg(values, corr):
            B, H, L, C = values.shape
            top_k = int(FACTOR * np.log(L + 1)) if L > 1 else 1
            top_k = max(1, min(top_k, L))
            mean_value = corr.mean(axis=1).mean(axis=1)
            mean_across_batch = mean_value.mean(axis=0)
            actual_k = min(top_k, C)
            _, indices = jax.lax.top_k(mean_across_batch, actual_k)
            selected = mean_value[:, indices]
            weights = jax.nn.softmax(selected, axis=-1)
            t = jnp.arange(L)

            def body(acc, inp):
                d, w = inp
                idx = (t + d) % L
                acc = acc + values[:, :, idx, :] * w[:, None, None, None]
                return (acc, None)
            agg, _ = jax.lax.scan(body, jnp.zeros_like(values), (indices, weights.T))
            return agg
        key = jax.random.key(seed)
        ks = jax.random.split(key, 8)
        B, L, D = (4, 512, 128)
        scale = 0.02
        return {'q': jax.random.normal(ks[0], (B, L, D), jnp.float32), 'k': jax.random.normal(ks[1], (B, L, D), jnp.float32), 'v': jax.random.normal(ks[2], (B, L, D), jnp.float32), 'Wq': jax.random.normal(ks[3], (D, D), jnp.float32) * scale, 'bq': jnp.zeros((D,), jnp.float32), 'Wk': jax.random.normal(ks[4], (D, D), jnp.float32) * scale, 'bk': jnp.zeros((D,), jnp.float32), 'Wv': jax.random.normal(ks[5], (D, D), jnp.float32) * scale, 'bv': jnp.zeros((D,), jnp.float32), 'Wo': jax.random.normal(ks[6], (D, D), jnp.float32) * scale, 'bo': jnp.zeros((D,), jnp.float32)}
    _L1_xattn_all = _L1_xattn_setup()
    _L1_xattn_in = {k: v for k, v in _L1_xattn_all.items() if k in ('Wq', 'bq', 'Wk', 'bk', 'Wv', 'bv', 'Wo', 'bo')}
    del _L1_xattn_all

    def _L1_ffn_setup():
        import jax, jax.numpy as jnp
        import numpy as np
        H = 128
        I = 64
        E = 32
        TOP_K = 6
        N_GROUP = 8
        TOPK_GROUP = 4
        SCALE = 2.5
        N_SHARED = 2
        SI = I * N_SHARED
        B, S = (2, 128)
        key = jax.random.key(seed)
        ks = jax.random.split(key, 8)
        x = jax.random.normal(ks[0], (B, S, H), jnp.float32)
        gate_weight = jax.random.normal(ks[1], (E, H), jnp.float32) * 0.02
        e_score_correction_bias = jax.random.normal(ks[2], (E,), jnp.float32) * 0.01
        experts_gate_up = jax.random.normal(ks[3], (E, 2 * I, H), jnp.float32) * 0.02
        experts_down = jax.random.normal(ks[4], (E, H, I), jnp.float32) * 0.02
        shared_gate_w = jax.random.normal(ks[5], (SI, H), jnp.float32) * 0.02
        shared_up_w = jax.random.normal(ks[6], (SI, H), jnp.float32) * 0.02
        shared_down_w = jax.random.normal(ks[7], (H, SI), jnp.float32) * 0.02
        return {'x': x, 'gate_weight': gate_weight, 'e_score_correction_bias': e_score_correction_bias, 'experts_gate_up': experts_gate_up, 'experts_down': experts_down, 'shared_gate_w': shared_gate_w, 'shared_up_w': shared_up_w, 'shared_down_w': shared_down_w}
    _L1_ffn_all = _L1_ffn_setup()
    _L1_ffn_in = {k: v for k, v in _L1_ffn_all.items() if k in ('gate_weight', 'e_score_correction_bias', 'experts_gate_up', 'experts_down', 'shared_gate_w', 'shared_up_w', 'shared_down_w')}
    del _L1_ffn_all
    return {'x': x, 'ctx_1024': ctx_1024, 'g_xattn': g_xattn, 'g_ffn': g_ffn, 'L0_xattn_Wq': _L0_xattn_in['Wq'], 'L0_xattn_bq': _L0_xattn_in['bq'], 'L0_xattn_Wk': _L0_xattn_in['Wk'], 'L0_xattn_bk': _L0_xattn_in['bk'], 'L0_xattn_Wv': _L0_xattn_in['Wv'], 'L0_xattn_bv': _L0_xattn_in['bv'], 'L0_xattn_Wo': _L0_xattn_in['Wo'], 'L0_xattn_bo': _L0_xattn_in['bo'], 'L0_ffn_gate_weight': _L0_ffn_in['gate_weight'], 'L0_ffn_W1': _L0_ffn_in['W1'], 'L0_ffn_b1': _L0_ffn_in['b1'], 'L0_ffn_W2': _L0_ffn_in['W2'], 'L0_ffn_b2': _L0_ffn_in['b2'], 'L0_ffn_Ws1': _L0_ffn_in['Ws1'], 'L0_ffn_bs1': _L0_ffn_in['bs1'], 'L0_ffn_Ws2': _L0_ffn_in['Ws2'], 'L0_ffn_bs2': _L0_ffn_in['bs2'], 'L1_xattn_Wq': _L1_xattn_in['Wq'], 'L1_xattn_bq': _L1_xattn_in['bq'], 'L1_xattn_Wk': _L1_xattn_in['Wk'], 'L1_xattn_bk': _L1_xattn_in['bk'], 'L1_xattn_Wv': _L1_xattn_in['Wv'], 'L1_xattn_bv': _L1_xattn_in['bv'], 'L1_xattn_Wo': _L1_xattn_in['Wo'], 'L1_xattn_bo': _L1_xattn_in['bo'], 'L1_ffn_gate_weight': _L1_ffn_in['gate_weight'], 'L1_ffn_e_score_correction_bias': _L1_ffn_in['e_score_correction_bias'], 'L1_ffn_experts_gate_up': _L1_ffn_in['experts_gate_up'], 'L1_ffn_experts_down': _L1_ffn_in['experts_down'], 'L1_ffn_shared_gate_w': _L1_ffn_in['shared_gate_w'], 'L1_ffn_shared_up_w': _L1_ffn_in['shared_up_w'], 'L1_ffn_shared_down_w': _L1_ffn_in['shared_down_w']}

def reference(x, ctx_1024, g_xattn, g_ffn, L0_xattn_Wq, L0_xattn_bq, L0_xattn_Wk, L0_xattn_bk, L0_xattn_Wv, L0_xattn_bv, L0_xattn_Wo, L0_xattn_bo, L0_ffn_gate_weight, L0_ffn_W1, L0_ffn_b1, L0_ffn_W2, L0_ffn_b2, L0_ffn_Ws1, L0_ffn_bs1, L0_ffn_Ws2, L0_ffn_bs2, L1_xattn_Wq, L1_xattn_bq, L1_xattn_Wk, L1_xattn_bk, L1_xattn_Wv, L1_xattn_bv, L1_xattn_Wo, L1_xattn_bo, L1_ffn_gate_weight, L1_ffn_e_score_correction_bias, L1_ffn_experts_gate_up, L1_ffn_experts_down, L1_ffn_shared_gate_w, L1_ffn_shared_up_w, L1_ffn_shared_down_w):
    import jax
    import jax.numpy as jnp

    def _L0_xattn_ref(queries, keys, values, Wq, bq, Wk, bk, Wv, bv, Wo, bo):
        import jax, jax.numpy as jnp
        import numpy as np
        import math
        D_MODEL = 128
        N_HEADS = 16
        D_HEAD = D_MODEL // N_HEADS
        N, L, _ = queries.shape
        S = keys.shape[1]
        H, D = (N_HEADS, D_HEAD)
        q = (queries @ Wq + bq).reshape(N, L, H, D)
        k = (keys @ Wk + bk).reshape(N, S, H, D)
        v = (values @ Wv + bv).reshape(N, S, H, D)
        sm = jnp.einsum('nlhd,nshd->nlhs', q, k) / math.sqrt(D)
        sm = jax.nn.softmax(sm, axis=1)
        attn = jnp.einsum('nlhs,nshd->nlhd', sm, v).reshape(N, L, H * D)
        return attn @ Wo + bo

    def _L0_ffn_ref(x, gate_weight, W1, b1, W2, b2, Ws1, bs1, Ws2, bs2):
        import jax, jax.numpy as jnp
        import numpy as np
        B, SEQ, D, E, F = (4, 128, 128, 8, 512)
        CAPACITY = 2
        Bb, s, Dd = x.shape
        Ee = gate_weight.shape[0]
        xf = x.reshape(-1, Dd)
        S = xf.shape[0]
        logits = xf @ gate_weight.T
        scores = jax.nn.softmax(logits, axis=-1).T
        k = S * CAPACITY
        vals, idx = jax.lax.top_k(scores.reshape(-1), k)
        eidx = idx // S
        tidx = idx % S
        gate = jnp.zeros((Ee, S), x.dtype).at[eidx, tidx].add(vals)
        h = jax.nn.gelu(jnp.einsum('sd,edf->esf', xf, W1) + b1[:, None, :], approximate=True)
        y = jnp.einsum('esf,efd->esd', h, W2) + b2[:, None, :]
        out = jnp.einsum('es,esd->sd', gate, y)
        shared = jax.nn.gelu(xf @ Ws1 + bs1, approximate=True) @ Ws2 + bs2
        out = out + shared
        return out.reshape(Bb, s, Dd)

    def _L1_xattn_ref(q, k, v, Wq, bq, Wk, bk, Wv, bv, Wo, bo):
        import jax, jax.numpy as jnp
        import numpy as np
        from functools import partial
        FACTOR = 5
        N_HEADS = 16

        def _time_delay_agg(values, corr):
            B, H, L, C = values.shape
            top_k = int(FACTOR * np.log(L + 1)) if L > 1 else 1
            top_k = max(1, min(top_k, L))
            mean_value = corr.mean(axis=1).mean(axis=1)
            mean_across_batch = mean_value.mean(axis=0)
            actual_k = min(top_k, C)
            _, indices = jax.lax.top_k(mean_across_batch, actual_k)
            selected = mean_value[:, indices]
            weights = jax.nn.softmax(selected, axis=-1)
            t = jnp.arange(L)

            def body(acc, inp):
                d, w = inp
                idx = (t + d) % L
                acc = acc + values[:, :, idx, :] * w[:, None, None, None]
                return (acc, None)
            agg, _ = jax.lax.scan(body, jnp.zeros_like(values), (indices, weights.T))
            return agg
        B, L, D = q.shape
        H = N_HEADS
        dk = D // H

        def proj(x, W, b):
            y = x @ W.T + b
            return y.reshape(B, L, H, dk).transpose(0, 2, 1, 3)
        Q = proj(q, Wq, bq).astype(jnp.float32)
        K = proj(k, Wk, bk).astype(jnp.float32)
        V = proj(v, Wv, bv).astype(jnp.float32)
        Qf = jnp.fft.rfft(Q, axis=2)
        Kf = jnp.fft.rfft(K, axis=2)
        R = jnp.fft.irfft(Qf * jnp.conj(Kf), n=L, axis=2)
        V_agg = _time_delay_agg(V, R)
        V_agg = V_agg.transpose(0, 2, 1, 3).reshape(B, L, D)
        return V_agg @ Wo.T + bo

    def _L1_ffn_ref(x, gate_weight, e_score_correction_bias, experts_gate_up, experts_down, shared_gate_w, shared_up_w, shared_down_w):
        import jax, jax.numpy as jnp
        import numpy as np
        H = 128
        I = 64
        E = 32
        TOP_K = 6
        N_GROUP = 8
        TOPK_GROUP = 4
        SCALE = 2.5
        N_SHARED = 2
        SI = I * N_SHARED
        B, S = (2, 128)
        b, s, h = x.shape
        xf = x.reshape(-1, h)
        T = xf.shape[0]
        logits = xf.astype(jnp.float32) @ gate_weight.astype(jnp.float32).T
        scores = jax.nn.sigmoid(logits)
        sfc = scores + e_score_correction_bias[None, :]
        gs = E // N_GROUP
        group_scores = sfc.reshape(T, N_GROUP, gs).max(axis=-1)
        _, gidx = jax.lax.top_k(group_scores, TOPK_GROUP)
        gmask = jnp.zeros((T, N_GROUP), bool).at[jnp.arange(T)[:, None], gidx].set(True)
        smask = jnp.repeat(gmask, gs, axis=1)
        masked = jnp.where(smask, sfc, 0.0)
        _, topk_idx = jax.lax.top_k(masked, TOP_K)
        tw = jnp.take_along_axis(scores, topk_idx, axis=1)
        tw = tw / (tw.sum(-1, keepdims=True) + 1e-20)
        tw = (tw * SCALE).astype(xf.dtype)
        combine = jnp.zeros((T, E), xf.dtype).at[jnp.arange(T)[:, None], topk_idx].add(tw)

        def expert_step(acc, inp):
            gu, dn, c = inp
            g = xf @ gu[:I].T
            u = xf @ gu[I:].T
            o = jax.nn.silu(g) * u @ dn.T
            return (acc + c[:, None] * o, None)
        routed, _ = jax.lax.scan(expert_step, jnp.zeros_like(xf), (experts_gate_up, experts_down, combine.T))
        sh = jax.nn.silu(xf @ shared_gate_w.T) * (xf @ shared_up_w.T)
        shared_out = sh @ shared_down_w.T
        return (routed + shared_out).reshape(b, s, h)
    x = x + jnp.tanh(g_xattn[0]) * _L0_xattn_ref(_layernorm(x, axis=-1), ctx_1024, ctx_1024, L0_xattn_Wq, L0_xattn_bq, L0_xattn_Wk, L0_xattn_bk, L0_xattn_Wv, L0_xattn_bv, L0_xattn_Wo, L0_xattn_bo)
    x = x + jnp.tanh(g_ffn[0]) * _L0_ffn_ref(_layernorm(x, axis=-1), L0_ffn_gate_weight, L0_ffn_W1, L0_ffn_b1, L0_ffn_W2, L0_ffn_b2, L0_ffn_Ws1, L0_ffn_bs1, L0_ffn_Ws2, L0_ffn_bs2)
    x = x + jnp.tanh(g_xattn[1]) * _L1_xattn_ref(_layernorm(x, axis=-1), ctx_1024, ctx_1024, L1_xattn_Wq, L1_xattn_bq, L1_xattn_Wk, L1_xattn_bk, L1_xattn_Wv, L1_xattn_bv, L1_xattn_Wo, L1_xattn_bo)
    x = x + jnp.tanh(g_ffn[1]) * _L1_ffn_ref(_layernorm(x, axis=-1), L1_ffn_gate_weight, L1_ffn_e_score_correction_bias, L1_ffn_experts_gate_up, L1_ffn_experts_down, L1_ffn_shared_gate_w, L1_ffn_shared_up_w, L1_ffn_shared_down_w)
    return x

_drawn_inputs = setup_inputs


def setup_inputs(seed=0):
    import zlib

    import numpy as np

    out = dict(_drawn_inputs(seed))
    spreads = {'g_ffn': (-1.0, 0.6),
     'L0_xattn_bq': (0.0, 0.8),
     'L0_xattn_bk': (0.0, 0.1),
     'L0_xattn_bv': (0.0, 0.1),
     'L0_xattn_bo': (0.0, 0.1),
     'L0_ffn_b1': (0.0, 0.8),
     'L0_ffn_b2': (0.0, 0.704),
     'L0_ffn_bs1': (0.0, 0.1),
     'L0_ffn_bs2': (0.0, 0.1),
     'L1_xattn_bq': (0.0, 0.8),
     'L1_xattn_bk': (0.0, 0.8),
     'L1_xattn_bv': (0.0, 0.583),
     'L1_xattn_bo': (0.0, 0.1)}
    factors = {'L1_xattn_Wq': 8.0,
     'L1_xattn_Wk': 8.0,
     'L1_ffn_gate_weight': 8.0,
     'L1_ffn_e_score_correction_bias': 8.0,
     'L1_ffn_experts_gate_up': 8.0,
     'L1_ffn_experts_down': 8.0,
     'L1_ffn_shared_gate_w': 8.0,
     'L1_ffn_shared_up_w': 8.0,
     'L1_ffn_shared_down_w': 8.0}
    for name, (base, spread) in spreads.items():
        noise = np.random.default_rng([zlib.crc32(name.encode()), seed]).standard_normal(out[name].shape)
        drawn = base * np.exp(spread * noise) if base else spread * noise
        out[name] = jnp.asarray(drawn.astype(out[name].dtype))
    for name, factor in factors.items():
        out[name] = (out[name] * factor).astype(out[name].dtype)
    return out
```

```python
import concourse.bass as bass
from concourse import mybir
from contextlib import ExitStack
import math

F32 = mybir.dt.float32
F32R = mybir.dt.float32r
F16 = mybir.dt.float16
I32 = mybir.dt.int32
ALU = mybir.AluOpType
ACT = mybir.ActivationFunctionType
AX = mybir.AxisListType

NB, L, D = 128, 64, 128
T = NB * L
TG = 512
G = T // TG
TPG = TG // 128
NBG = TG // L
H, DH = 16, 8
QG, HQ = 4, 4
NVAR = 3
EPS = 1e-5
E0, F0 = 8, 512
FC = F0 // 128
WC0 = F0 + FC * D
RC0 = WC0 + FC + 1
KTOP = 2 * T
NT = T // 128
E1, I1 = 32, 64
PAIRS = E1 // 2 + 1
NG1, GS1, TOPG1, TOPK1 = 8, 4, 4, 6
SCALE1 = 2.5


def need(eng, sem, n):
    if isinstance(n, int) and n <= 0:
        return
    eng.wait_ge(sem, n)


def group(i):
    return bass.ds(i * TG, TG)


def skewed(eng, lead, lag):
    lead(0, 0)
    with eng.Fori(0, G // 2 - 1) as r:
        lead(2 * r + 1, 1)
        lag(2 * r, 0)
        lead(2 * r + 2, 0)
        lag(2 * r + 1, 1)
    lead(G - 1, 1)
    lag(G - 2, 0)
    lag(G - 1, 1)


def attention(nc, sem, P, W, XH, XL, SC, xT, ctxT, scratch, x1_dram):
    with ExitStack() as ctx:
        def sb(name, shape, dt):
            return ctx.enter_context(nc.sbuf_tensor(name, shape, dt))

        xg = sb("xg", [128, 2, TG], F32)
        cg = sb("cg", [128, 2, TG], F32)
        xc1 = sb("xc1", [128, TG], F32)
        sq1 = sb("sq1", [128, TG], F32)
        xn1 = sb("xn1", [128, TG], F32)
        xc2 = sb("xc2", [128, TG], F32)
        sq2 = sb("sq2", [128, TG], F32)
        xn2 = sb("xn2", [128, TG], F32)
        x1s = sb("x1s", [128, 2, TG], F32)
        qk32 = sb("qk32", [128, 2, TG], F32)
        qkh = sb("qkh", [128, 2, TG], F16)
        qkl = sb("qkl", [128, 2, TG], F16)
        v32 = sb("v32", [128, 2, TPG, 128], F32)
        QM = sb("QM", [96, 2, QG, HQ, TG], F16)
        KS = sb("KS", [96, 2, QG, TG], F16)
        ES = sb("ES", [128, 2, H, L], F32)
        EH = sb("EH", [128, 2, H, L], F16)
        EL = sb("EL", [128, 2, H, L], F16)
        mx = sb("mx", [128, 2, H], F32)
        zh = sb("zh", [128, 2, H, L // 2], F32)
        zz = sb("zz", [128, 2, H], F32)
        rz = sb("rz", [128, 2, H], F32)
        vz = sb("vz", [128, 2, 128], F32)
        VH = sb("VH", [128, 2, H, 128], F16)
        VL = sb("VL", [128, 2, H, 128], F16)
        OS = sb("OS", [128, TPG, 2, L], F32)

        loaded = [sem("xc_loaded0"), sem("xc_loaded1")]
        zeroed = sem("zeroed")
        mean1, centred1, squared1 = sem("mean1"), sem("centred1"), sem("squared1")
        var1, log1, rstd1, normed1 = sem("var1"), sem("log1"), sem("rstd1"), sem("normed1")
        mean2, centred2, squared2 = sem("mean2"), sem("centred2"), sem("squared2")
        var2, log2, rstd2, normed2 = sem("var2"), sem("log2"), sem("rstd2"), sem("normed2")
        hi2, lo2 = sem("hi2"), sem("lo2")
        q_done, k_done, v_done = sem("q_done"), sem("k_done"), sem("v_done")
        q_out, k_out, v_out = sem("q_out"), sem("k_out"), sem("v_out")
        qk_hi, qk_lo, qk_stored = sem("qk_hi"), sem("qk_lo"), sem("qk_stored")
        stacked = [sem("stacked0"), sem("stacked1")]
        scored, maxed, shifted = sem("scored"), sem("maxed"), sem("shifted")
        exped, exped16, halved, summed = sem("exped"), sem("exped16"), sem("halved"), sem("summed")
        inverted, v_scaled, v_hi, v_lo = sem("inverted"), sem("v_scaled"), sem("v_hi"), sem("v_lo")
        e_lo, pv_done, o_out = sem("exp_lo"), sem("pv_done"), sem("o_out")
        projected, x1_done = sem("projected"), sem("x1_done")
        x1_stored = [sem("x1_stored0"), sem("x1_stored1")]
        routed, logits_out = sem("routed"), sem("logits_out")
        STACK = 16 * (NVAR * HQ + NVAR)

        S = [P[:, 0:2, :], P[:, 2:4, :]]
        BO, BA, BB, BC = P[:, 4, 0:128], P[:, 5, :], P[:, 6, :], P[:, 7, :]
        block = ctx.enter_context(nc.Block())

        def groups(eng, body):
            body(0, 0, True, False)
            with eng.Fori(0, G // 2 - 1) as r:
                body(2 * r + 1, 1, True, True)
                body(2 * r + 2, 0, True, True)
            body(G - 1, 1, False, True)

        @block.sync
        def _(sp):
            def load(i, p, again=True):
                if again:
                    sp.wait_ge(x1_done, i - 1)
                    sp.wait_ge(v_done, i - 1)
                    sp.wait_ge(k_done, i - 1)
                nc.sync.dma_start(xg[:, p, :], xT[:, group(i)]).then_inc(loaded[p], 16)
                nc.sync.dma_start(cg[:, p, :], ctxT[:, group(i)]).then_inc(loaded[p], 16)

            def store(i, p):
                sp.wait_ge(x1_done, i + 1)
                nc.sync.dma_start(x1_dram[:, group(i)], x1s[:, p, :]).then_inc(x1_stored[p], 16)

            def stack(i, p):
                sp.wait_ge(qk_lo, 2 * i + 2)
                for c in range(2):
                    nc.sync.dma_start(scratch[p, c, 0], qkh[:, c, :]).then_inc(qk_stored, 16)
                    nc.sync.dma_start(scratch[p, c, 1], qkl[:, c, :]).then_inc(qk_stored, 16)
                sp.wait_ge(qk_stored, 64 * i + 64)
                for var, half in enumerate((0, 1, 0)):
                    src = scratch[p, 0, half].rearrange("(g h d) t -> h d g t", g=QG, h=HQ)
                    for hh in range(HQ):
                        a = 32 * var + DH * hh
                        nc.sync.dma_start(QM[a:a + DH, p, :, hh, :], src[hh]).then_inc(stacked[p], 16)
                for var, half in enumerate((0, 0, 1)):
                    src = scratch[p, 1, half].rearrange("(g r) t -> r g t", g=QG)
                    nc.sync.dma_start(KS[32 * var:32 * var + 32, p, :, :], src).then_inc(stacked[p], 16)

            def body(i, p):
                stack(i + 1, 1 - p)
                store(i, p)
                load(i + 2, p)

            load(0, 0, False)
            load(1, 1, False)
            sp.wait_ge(zeroed, 3)
            stack(0, 0)
            stack(1, 1)
            store(0, 0)
            load(2, 0)
            with sp.Fori(0, G // 2 - 2) as r:
                body(2 * r + 1, 1)
                body(2 * r + 2, 0)
            body(G - 3, 1)
            stack(G - 1, 1)
            store(G - 2, 0)
            store(G - 1, 1)
            for p in range(2):
                sp.wait_ge(x1_stored[p], 16 * G // 2)

        @block.gpsimd
        def _(pool):
            nc.gpsimd.memset(VH[:], 0.0).then_inc(zeroed, 1)
            nc.gpsimd.memset(VL[:], 0.0).then_inc(zeroed, 1)

            def body(i, p, front, tail):
                for t in range(TPG):
                    b, n = t % 2, TPG * i + t
                    pool.wait_ge(exped, n + 1)
                    need(pool, summed, n - 1)
                    nc.gpsimd.tensor_tensor(zh[:, b], ES[:, b, :, 0:L // 2], ES[:, b, :, L // 2:L],
                                            ALU.add).then_inc(halved, 1)

            groups(pool, body)

        def v_slot(V, b, u, a):
            flat = V[64 * u:64 * u + 64, b, 8 * a:8 * a + 8, :].rearrange("p h c -> p (h c)")
            return bass.AP(flat.tensor, flat.offset + 64 * u, [list(flat.ap[0]), [136, 8], [1, DH]])

        def v_from(u, b, a):
            return vz[64 * u:64 * u + 64, b, 64 * a:64 * a + 64].rearrange("p (h d) -> p h d", h=8)

        @block.vector
        def _(dve):
            flat = QM[:].rearrange("p a b c d -> p (a b c d)").bitcast(I32)
            nc.vector.memset(flat, 0).then_inc(zeroed, 1)

            def centre1(i, p):
                if isinstance(i, int):
                    dve.wait_ge(loaded[p], 32)
                else:
                    dve.wait_ge(loaded[p], 16 * (i - p) + 32)
                dve.wait_ge(mean1, i + 1)
                need(dve, normed1, i)
                need(dve, squared1, i)
                nc.vector.tensor_tensor(xc1[:], xg[:, p, :], BA, ALU.subtract).then_inc(centred1, 1)

            def norm1(i):
                dve.wait_ge(rstd1, i + 1)
                need(dve, q_done, i)
                nc.vector.tensor_tensor(xn1[:], xc1[:], sq1[:], ALU.mult).then_inc(normed1, 1)

            def split_qk(i, c):
                dve.wait_ge(q_out if c == 0 else k_out, i + 1)
                need(dve, qk_stored, 64 * i)
                nc.vector.tensor_copy(qkh[:, c, :], qk32[:, c, :]).then_inc(qk_hi, 1)
                dve.wait_ge(qk_hi, 2 * i + 1 + c)
                nc.vector.tensor_tensor(qkl[:, c, :], qk32[:, c, :], qkh[:, c, :],
                                        ALU.subtract).then_inc(qk_lo, 1)

            def v_evac(i, p):
                dve.wait_ge(v_done, i + 1)
                need(dve, v_scaled, TPG * (i - 1) if isinstance(i, int) else TPG * i - TPG)
                nc.vector.tensor_tensor(v32[:, p], BA.rearrange("p (t c) -> p t c", t=TPG),
                                        W["bv0"][:].unsqueeze(1).to_broadcast([128, TPG, 128]),
                                        ALU.add).then_inc(v_out, 1)

            def soft(i, t):
                b, n = t % 2, TPG * i + t
                s = S[b].rearrange("p a (h l) -> p (a h) l", l=L)
                dve.wait_ge(scored, n + 1)
                nc.vector.tensor_reduce(mx[:, b], s, AX.X, ALU.max).then_inc(maxed, 1)
                dve.wait_ge(maxed, n + 1)
                nc.vector.tensor_tensor(s, s, mx[:, b].unsqueeze(2).to_broadcast([128, H, L]),
                                        ALU.subtract).then_inc(shifted, 1)

            def values(i, p, t):
                b, n = t % 2, TPG * i + t
                dve.wait_ge(halved, n + 1)
                nc.vector.tensor_reduce(zz[:, b], zh[:, b], AX.X, ALU.add).then_inc(summed, 1)
                dve.wait_ge(exped16, n + 1)
                need(dve, pv_done, n - 1)
                nc.vector.tensor_tensor(EL[:, b], ES[:, b], EH[:, b], ALU.subtract).then_inc(e_lo, 1)
                dve.wait_ge(summed, n + 1)
                nc.vector.reciprocal(rz[:, b], zz[:, b]).then_inc(inverted, 1)
                dve.wait_ge(inverted, n + 1)
                dve.wait_ge(v_out, i + 1)
                nc.vector.tensor_tensor(vz[:, b].rearrange("p (h d) -> p h d", h=H),
                                        v32[:, p, t].rearrange("p (h d) -> p h d", h=H),
                                        rz[:, b].unsqueeze(2).to_broadcast([128, H, DH]),
                                        ALU.mult).then_inc(v_scaled, 1)
                dve.wait_ge(v_hi, 4 * n + 4)
                dve.wait_ge(v_scaled, n + 1)
                for u in range(2):
                    for a in range(2):
                        nc.vector.tensor_tensor(v_slot(VL, b, u, a), v_from(u, b, a), v_slot(VH, b, u, a),
                                                ALU.subtract).then_inc(v_lo, 1)

            def x1(i, p):
                dve.wait_ge(projected, i + 1)
                if not isinstance(i, int) or i >= 2:
                    dve.wait_ge(x1_stored[p], 16 * (i // 2) if isinstance(i, int) else 8 * (i - p))
                    dve.wait_ge(centred2, i - 1)
                nc.vector.scalar_tensor_tensor(out=x1s[:, p, :], in0=BC, scalar=W["bo0"][:, 0:1],
                                               in1=xg[:, p, :], op0=ALU.add,
                                               op1=ALU.add).then_inc(x1_done, 1)

            def centre2(i, p):
                dve.wait_ge(mean2, i + 1)
                need(dve, normed2, i)
                nc.vector.tensor_tensor(xc2[:], x1s[:, p, :], BB, ALU.subtract).then_inc(centred2, 1)

            def norm2(i):
                dve.wait_ge(rstd2, i + 1)
                need(dve, routed, i)
                need(dve, lo2, i)
                nc.vector.tensor_tensor(xn2[:], xc2[:], sq2[:], ALU.mult).then_inc(normed2, 1)
                dve.wait_ge(normed2, i + 1)
                nc.vector.tensor_copy(XH[:, group(i)], xn2[:]).then_inc(hi2, 1)
                dve.wait_ge(hi2, i + 1)
                nc.vector.tensor_tensor(XL[:, group(i)], xn2[:], XH[:, group(i)].bitcast(F32),
                                        ALU.subtract).then_inc(lo2, 1)

            centre1(0, 0)
            norm1(0)
            v_evac(0, 0)
            split_qk(0, 0)
            split_qk(0, 1)

            def body(i, p, front, tail):
                soft(i, 0)
                if tail:
                    centre2(i - 1, 1 - p)
                if front:
                    centre1(i + 1, 1 - p)
                soft(i, 1)
                values(i, p, 0)
                if tail:
                    norm2(i - 1)
                if front:
                    norm1(i + 1)
                soft(i, 2)
                values(i, p, 1)
                if front:
                    v_evac(i + 1, 1 - p)
                soft(i, 3)
                if front:
                    split_qk(i + 1, 0)
                values(i, p, 2)
                if front:
                    split_qk(i + 1, 1)
                values(i, p, 3)
                x1(i, p)

            groups(dve, body)
            centre2(G - 1, 1)
            norm2(G - 1)

        @block.scalar
        def _(act):
            def square(i, xc, sq, centred, squared, normed):
                act.wait_ge(centred, i + 1)
                need(act, normed, i)
                nc.scalar.activation(sq[:], xc[:], ACT.Square).then_inc(squared, 1)

            def rstd(i, bank, sq, var, log, rst):
                act.wait_ge(var, i + 1)
                nc.scalar.activation(sq[:], bank, ACT.Ln, bias=W["eps"][:, 0:1]).then_inc(log, 1)
                act.wait_ge(log, i + 1)
                nc.scalar.activation(sq[:], sq[:], ACT.Exp, scale=-0.5).then_inc(rst, 1)

            def exps(i, t):
                b, n = t % 2, TPG * i + t
                s = S[b].rearrange("p a (h l) -> p (a h) l", l=L)
                act.wait_ge(shifted, n + 1)
                need(act, e_lo, n - 1)
                need(act, halved, n - 1)
                nc.scalar.activation(ES[:, b], s, ACT.Exp, scale=DH ** -0.5).then_inc(exped, 1)
                need(act, pv_done, n - 1)
                nc.scalar.activation(EH[:, b], s, ACT.Exp, scale=DH ** -0.5).then_inc(exped16, 1)

            def v_high(i, t):
                b, n = t % 2, TPG * i + t
                act.wait_ge(v_scaled, n + 1)
                if isinstance(i, int) and i == 0 and t == 0:
                    act.wait_ge(zeroed, 3)
                need(act, pv_done, n - 1)
                for u in range(2):
                    for a in range(2):
                        nc.scalar.activation(v_slot(VH, b, u, a), v_from(u, b, a),
                                             ACT.Copy).then_inc(v_hi, 1)

            def o_evac(i, t):
                n = TPG * i + t
                act.wait_ge(pv_done, n + 1)
                need(act, projected, i)
                nc.scalar.activation(OS[:, t].rearrange("p a l -> p (a l)"), BO,
                                     ACT.Copy).then_inc(o_out, 1)

            def qk_evac(i, c):
                act.wait_ge(k_done if c else q_done, i + 1)
                need(act, qk_lo, 2 * i - 1 + c if not isinstance(i, int) else (2 * i - 1 + c if i else 0))
                nc.scalar.activation(qk32[:, c, :], BC if c else BB, ACT.Identity,
                                     bias=W["bk0" if c else "bq0"][:, 0:1]).then_inc(k_out if c else q_out, 1)

            def logit_evac(i):
                act.wait_ge(routed, i + 1)
                nc.scalar.activation(SC[:, :, bass.ds(i * TPG, TPG)].rearrange("p e t -> p t e"),
                                     BC[:, 0:TPG * E0].rearrange("p (t e) -> p t e", e=E0),
                                     ACT.Copy).then_inc(logits_out, 1)

            first = (xc1, sq1, centred1, squared1, normed1)
            second = (xc2, sq2, centred2, squared2, normed2)
            root1 = (BA, sq1, var1, log1, rstd1)
            root2 = (BB, sq2, var2, log2, rstd2)
            square(0, *first)
            rstd(0, *root1)
            qk_evac(0, 0)
            qk_evac(0, 1)

            def body(i, p, front, tail):
                exps(i, 0)
                if tail:
                    square(i - 1, *second)
                if front:
                    square(i + 1, *first)
                exps(i, 1)
                if tail:
                    rstd(i - 1, *root2)
                if front:
                    rstd(i + 1, *root1)
                v_high(i, 0)
                exps(i, 2)
                o_evac(i, 0)
                if tail:
                    logit_evac(i - 1)
                if front:
                    qk_evac(i + 1, 0)
                v_high(i, 1)
                exps(i, 3)
                o_evac(i, 1)
                if front:
                    qk_evac(i + 1, 1)
                v_high(i, 2)
                o_evac(i, 2)
                v_high(i, 3)
                o_evac(i, 3)

            groups(act, body)
            square(G - 1, *second)
            rstd(G - 1, *root2)
            logit_evac(G - 1)

        @block.tensor
        def _(pe):
            def mean_1(i, p):
                if isinstance(i, int):
                    pe.wait_ge(loaded[p], 32)
                else:
                    pe.wait_ge(loaded[p], 16 * (i - p) + 32)
                need(pe, v_out, i)
                nc.tensor.matmul(BA, W["mean"][:], xg[:, p, :], start=True, stop=True).then_inc(mean1, 1)

            def var_1(i):
                pe.wait_ge(squared1, i + 1)
                pe.wait_ge(centred1, i + 1)
                nc.tensor.matmul(BA, W["mean"][:], sq1[:], start=True, stop=True).then_inc(var1, 1)

            def mean_2(i, p):
                pe.wait_ge(x1_done, i + 1)
                pe.wait_ge(q_out, i + 2 if not isinstance(i, int) or i < G - 1 else G)
                nc.tensor.matmul(BB, W["mean"][:], x1s[:, p, :], start=True, stop=True).then_inc(mean2, 1)

            def var_2(i):
                pe.wait_ge(squared2, i + 1)
                pe.wait_ge(centred2, i + 1)
                nc.tensor.matmul(BB, W["mean"][:], sq2[:], start=True, stop=True).then_inc(var2, 1)

            def q_proj(i):
                pe.wait_ge(normed1, i + 1)
                need(pe, log2, i - 1)
                nc.tensor.matmul(BB, W["wq0"][:], xn1[:], start=True, stop=True).then_inc(q_done, 1)

            def k_proj(i, p):
                need(pe, logits_out, i - 1)
                need(pe, x1_done, i - 1)
                nc.tensor.matmul(BC, W["wk0"][:], cg[:, p, :], start=True, stop=True).then_inc(k_done, 1)

            def v_proj(i, p):
                pe.wait_ge(log1, i + 1)
                for t in range(TPG):
                    last = nc.tensor.matmul(BA[:, 128 * t:128 * t + 128], cg[:, p, 128 * t:128 * t + 128],
                                            W["wv0"][:], start=True, stop=True)
                last.then_inc(v_done, 1)

            def score(i, p, t):
                b, n = t % 2, TPG * i + t
                if t == 0:
                    if isinstance(i, int):
                        pe.wait_ge(stacked[p], STACK * (i // 2 + 1))
                    else:
                        pe.wait_ge(stacked[p], STACK // 2 * (i - p) + STACK)
                need(pe, exped16, n - 1)
                for u in range(2):
                    c0 = 128 * t + 64 * u
                    for g in range(QG):
                        last = nc.tensor.matmul(
                            S[b][64 * u:64 * u + 64, g // 2, 256 * (g % 2):256 * (g % 2) + 256],
                            KS[:, p, g, c0:c0 + 64], QM[:, p, g, :, c0:c0 + 64], start=True, stop=True)
                last.then_inc(scored, 1)

            def pv(i, t):
                b, n = t % 2, TPG * i + t
                pe.wait_ge(v_lo, 4 * n + 4)
                pe.wait_ge(e_lo, n + 1)
                need(pe, o_out, n)
                for a in range(2):
                    for h in range(8):
                        for k, (v, e) in enumerate(((VH, EH), (VL, EH), (VH, EL))):
                            last = nc.tensor.matmul(BO[:, 64 * a:64 * a + 64], v[:, b, 8 * a + h, :],
                                                    e[:, b, 8 * a + h, :],
                                                    start=(h == 0 and k == 0), stop=(h == 7 and k == 2))
                last.then_inc(pv_done, 1)

            def project(i):
                pe.wait_ge(o_out, TPG * i + TPG)
                pe.wait_ge(k_out, i + 2 if not isinstance(i, int) or i < G - 1 else G)
                out = BC.rearrange("p (t u l) -> p u t l", t=TPG, u=2)
                for u in range(2):
                    for a in range(2):
                        last = nc.tensor.matmul(out[:, u], W["wo0"][:, u, a, :], OS[:, :, a, :],
                                                start=(a == 0), stop=(a == 1))
                last.then_inc(projected, 1)

            def logits(i):
                pe.wait_ge(normed2, i + 1)
                pe.wait_ge(x1_done, i + 1)
                for t in range(TPG):
                    last = nc.tensor.matmul(BC[:, E0 * t:E0 * t + E0], xn2[:, 128 * t:128 * t + 128],
                                            W["gw0"][:], start=True, stop=True)
                last.then_inc(routed, 1)

            mean_1(0, 0)
            var_1(0)
            v_proj(0, 0)
            q_proj(0)
            k_proj(0, 0)

            def body(i, p, front, tail):
                if tail:
                    mean_2(i - 1, 1 - p)
                score(i, p, 0)
                if front:
                    mean_1(i + 1, 1 - p)
                if tail:
                    var_2(i - 1)
                score(i, p, 1)
                if front:
                    var_1(i + 1)
                pv(i, 0)
                if tail:
                    logits(i - 1)
                score(i, p, 2)
                if front:
                    v_proj(i + 1, 1 - p)
                    q_proj(i + 1)
                pv(i, 1)
                score(i, p, 3)
                if front:
                    k_proj(i + 1, 1 - p)
                pv(i, 2)
                pv(i, 3)
                project(i)

            groups(pe, body)
            mean_2(G - 1, 1)
            var_2(G - 1)
            logits(G - 1)


def first_ffn(nc, sem, P, W, X, XH, XL, SC, experts, x1_dram, gate_dram):
    with ExitStack() as ctx:
        def sb(name, shape, dt):
            return ctx.enter_context(nc.sbuf_tensor(name, shape, dt))

        WR = sb("WR", [128, 2, RC0], F32)
        WH = sb("WH", [128, 2, WC0], F32R)
        WL = sb("WL", [128, 2, WC0], F32R)
        HS = sb("HS", [128, 2, FC, TG], F32)
        HH = sb("HH", [128, 2, FC, TG], F32R)
        HL = sb("HL", [128, 2, FC, TG], F32R)
        GB = sb("GB", [128, 2, TG], F32)
        YB = sb("YB", [128, 2, TG], F32)
        cmp_ = sb("cmp_", [128, E0 * NT], F32)
        cnt = sb("cnt", [128, 1], F32)
        thr = sb("thr", [128, 1], I32)
        bit = sb("bit", [128, 1], I32)
        trial = sb("trial", [128, 1], I32)
        keep = sb("keep", [128, 1], I32)

        scores_ready = sem("scores_ready")
        x_loaded = sem("x_loaded")
        w_loaded = [sem("w_loaded0"), sem("w_loaded1")]
        w_hi, w_lo = sem("w_hi"), sem("w_lo")
        h_done, gelu_done = sem("h_done"), sem("gelu_done")
        h_hi, h_lo = [sem("h_hi0"), sem("h_hi1")], [sem("h_lo0"), sem("h_lo1")]
        y_done, y_out = [sem("y_done0"), sem("y_done1")], [sem("y_out0"), sem("y_out1")]
        added = [sem("added0"), sem("added1")]
        gates_loaded = [sem("gates_loaded0"), sem("gates_loaded1")]
        counted, totalled, stepped = sem("counted"), sem("totalled"), sem("stepped")
        BT, BY = P[:, 6, 0:1], [P[:, 4, :], P[:, 5, :]]
        NQ = E0 + 1
        HG = G // 2

        flat = SC[:].rearrange("p e j -> p (e j)")
        by_token = SC[:].rearrange("p e j -> p j e")
        peak = cmp_[:, 0:NT]
        with nc.Block() as block:
            @block.vector
            def _(dve):
                nc.vector.tensor_reduce(peak, by_token, AX.X, ALU.max).then_inc(scores_ready, 1)
                dve.wait_ge(scores_ready, 1)
                nc.vector.tensor_tensor(SC[:], SC[:], peak.unsqueeze(1).to_broadcast([128, E0, NT]),
                                        ALU.subtract).then_inc(scores_ready, 1)
                dve.wait_ge(scores_ready, 3)
                nc.vector.tensor_reduce(peak, by_token, AX.X, ALU.add).then_inc(scores_ready, 1)
                dve.wait_ge(scores_ready, 4)
                nc.vector.reciprocal(peak, peak).then_inc(scores_ready, 1)
                dve.wait_ge(scores_ready, 5)
                nc.vector.tensor_tensor(SC[:], SC[:], peak.unsqueeze(1).to_broadcast([128, E0, NT]),
                                        ALU.mult).then_inc(scores_ready, 1)
                nc.vector.memset(thr[:], 0).then_inc(scores_ready, 1)
                nc.vector.memset(bit[:], 1 << 29).then_inc(scores_ready, 1)
                nc.vector.memset(trial[:], 1 << 29).then_inc(scores_ready, 1)

            @block.scalar
            def _(act):
                act.wait_ge(scores_ready, 2)
                nc.scalar.activation(flat, flat, ACT.Exp).then_inc(scores_ready, 1)

            @block.sync
            def _(sp):
                nc.sync.dma_start(WR[:, 0], experts[0]).then_inc(w_loaded[0], 16)
                nc.sync.dma_start(WR[:, 1], experts[1]).then_inc(w_loaded[1], 16)
                nc.sync.dma_start(X[:], x1_dram).then_inc(x_loaded, 16)

        def w1(pe, q, w, b, u, first=False):
            if not first:
                pe.wait_ge(w_lo, q + 1)
            for c in range(FC):
                if not first:
                    pe.wait_ge(gelu_done, FC * (G * q + b - 1) + c + 1)
                wc = slice(128 * c, 128 * c + 128)
                for k, (a, x) in enumerate(((WH, XH), (WL, XH), (WH, XL))):
                    last = nc.tensor.matmul(P[:, c, :], a[:, w, wc], x[:, group(b)],
                                            start=(k == 0), stop=(k == 2))
                last.then_inc(h_done, 1)

        def total(pe, n):
            pe.wait_ge(counted, n + 1)
            nc.tensor.matmul(BT, W["ones"][:], cnt[:], start=True, stop=True).then_inc(totalled, 1)

        def w2(pe, w, u, n):
            need(pe, y_out[u], n)
            for half in range(2):
                pe.wait_ge(h_lo[u], 2 * n + half + 1)
                for c in (2 * half, 2 * half + 1):
                    wc = slice(F0 + 128 * c, F0 + 128 * c + 128)
                    for k, (a, h) in enumerate(((WH, HH), (WL, HH), (WH, HL))):
                        last = nc.tensor.matmul(BY[u], a[:, w, wc], h[:, u, c, :],
                                                start=(c == 0 and k == 0), stop=(c == FC - 1 and k == 2))
            last.then_inc(y_done[u], 1)

        def gelus(act, q, w, b, u, n):
            for c in range(FC):
                act.wait_ge(h_done, FC * (G * q + b) + c + 1)
                if c % 2 == 0:
                    need(act, h_lo[u], 2 * n)
                nc.scalar.activation(HS[:, u, c, :], P[:, c, :], ACT.Gelu_apprx_tanh,
                                     bias=WR[:, w, WC0 + c:WC0 + c + 1]).then_inc(gelu_done, 1)

        def split(dve, q, b, u, n):
            for half in range(2):
                hs = slice(2 * half, 2 * half + 2)
                dve.wait_ge(gelu_done, FC * (G * q + b) + 2 * half + 2)
                need(dve, y_done[u], n)
                nc.vector.tensor_copy(HH[:, u, hs], HS[:, u, hs]).then_inc(h_hi[u], 1)
                dve.wait_ge(h_hi[u], 2 * n + half + 1)
                nc.vector.tensor_tensor(HL[:, u, hs], HS[:, u, hs], HH[:, u, hs].bitcast(F32),
                                        ALU.subtract).then_inc(h_lo[u], 1)

        def gated(dve, w, u, n, shared):
            dve.wait_ge(y_done[u], n + 1)
            need(dve, added[u], n)
            b2 = WR[:, w, WC0 + FC:WC0 + FC + 1]
            if shared:
                nc.vector.tensor_scalar(YB[:, u, :], BY[u], b2, W["gf"][:, 0:1], ALU.add,
                                        ALU.mult).then_inc(y_out[u], 1)
            else:
                dve.wait_ge(gates_loaded[u], 16 * (n + 1) - 16 * HG)
                nc.vector.scalar_tensor_tensor(out=YB[:, u, :], in0=BY[u], scalar=b2, in1=GB[:, u, :],
                                               op0=ALU.add, op1=ALU.mult).then_inc(y_out[u], 1)

        def split_weights(dve, q, w, kq):
            dve.wait_ge(w_loaded[w], 16 * kq + 16)
            nc.vector.tensor_copy(WH[:, w], WR[:, w, 0:WC0]).then_inc(w_hi, 1)
            dve.wait_ge(w_hi, q + 1)
            nc.vector.tensor_tensor(WL[:, w], WR[:, w, 0:WC0], WH[:, w].bitcast(F32),
                                    ALU.subtract).then_inc(w_lo, 1)

        def add(pool, b, u, n):
            pool.wait_ge(y_out[u], n + 1)
            need(pool, added[1 - u], n + u)
            nc.gpsimd.tensor_tensor(X[:, group(b)], X[:, group(b)], YB[:, u, :],
                                    ALU.add).then_inc(added[u], 1)

        def over_groups(eng, q, ahead, here, last_ahead):
            with eng.Fori(0, HG - 1) as r:
                ahead(2 * r + 1, 1, HG * q + r)
                here(2 * r, 0, HG * q + r)
                ahead(2 * r + 2, 0, HG * q + r + 1)
                here(2 * r + 1, 1, HG * q + r)
            ahead(G - 1, 1, HG * q + HG - 1)
            here(G - 2, 0, HG * q + HG - 1)
            last_ahead()
            here(G - 1, 1, HG * q + HG - 1)

        def over_experts(eng, expert):
            with eng.Fori(0, E0 // 2 - 1) as r:
                expert(2 * r + 1, 1, r, False)
                expert(2 * r + 2, 0, r + 1, False)
            expert(E0 - 1, 1, E0 // 2 - 1, False)
            expert(E0, 0, E0 // 2, True)

        with nc.Block() as block:
            @block.tensor
            def _(pe):
                pe.wait_ge(w_lo, 1)
                w1(pe, 0, 0, 0, 0, first=True)

                def ahead(b, u, n):
                    w1(pe, 0, 0, b, u)

                def here(b, u, n):
                    total(pe, 2 * b)
                    w2(pe, 0, u, n)
                    total(pe, 2 * b + 1)

                over_groups(pe, 0, ahead, here, lambda: w1(pe, 1, 1, 0, 0))

            @block.scalar
            def _(act):
                with act.Fori(0, HG) as r:
                    gelus(act, 0, 0, 2 * r, 0, r)
                    gelus(act, 0, 0, 2 * r + 1, 1, r)

            @block.gpsimd
            def _(pool):
                pool.wait_ge(x_loaded, 16)
                with pool.Fori(0, HG) as r:
                    add(pool, 2 * r, 0, r)
                    add(pool, 2 * r + 1, 1, r)

            @block.vector
            def _(dve):
                split_weights(dve, 0, 0, 0)
                split(dve, 0, 0, 0, 0)

                def count(n):
                    dve.wait_ge(stepped, 4 * n)
                    need(dve, totalled, n)
                    nc.vector.tensor_scalar(cmp_[:], flat, trial[:].bitcast(F32), 0.0, ALU.is_ge, ALU.add,
                                            accum_out=cnt[:]).then_inc(counted, 1)

                def step(n):
                    dve.wait_ge(totalled, n + 1)
                    nc.vector.scalar_tensor_tensor(out=keep[:], in0=BT, scalar=float(KTOP), in1=bit[:],
                                                   op0=ALU.is_ge, op1=ALU.mult).then_inc(stepped, 1)
                    dve.wait_ge(stepped, 4 * n + 1)
                    nc.vector.tensor_scalar(bit[:], bit[:], 1, None,
                                            ALU.logical_shift_right).then_inc(stepped, 1)
                    nc.vector.tensor_tensor(thr[:], thr[:], keep[:], ALU.bitwise_or).then_inc(stepped, 1)
                    dve.wait_ge(stepped, 4 * n + 3)
                    nc.vector.tensor_tensor(trial[:], thr[:], bit[:], ALU.bitwise_or).then_inc(stepped, 1)

                count(0)

                def ahead(b, u, n):
                    split(dve, 0, b, u, n)

                def here(b, u, n):
                    step(2 * b)
                    count(2 * b + 1)
                    gated(dve, 0, u, n, True)
                    step(2 * b + 1)
                    if not (isinstance(b, int) and b == G - 1):
                        count(2 * b + 2)

                over_groups(dve, 0, ahead, here, lambda: split_weights(dve, 1, 1, 0))

        above = HS[:, 0, 0, :]
        on = HS[:, 0, 1, :]
        before = HS[:, 0, 2, :]
        rank = HS[:, 0, 3, :]
        gates = HS[:, 1, 0, :]
        gt = HS[:, 1, 1, :]
        left = cnt
        TRI = GB[:, 0, 0:128]
        ident = GB[:, 0, 128:256]
        chosen, made, stored = sem("chosen"), sem("gate_masks"), sem("gates_stored")
        gt_sems = sem("gate_products")
        with nc.Block() as block:
            @block.gpsimd
            def _(pool):
                nc.gpsimd.memset(GB[:, 0, 0:256], 1.0).then_inc(made, 1)
                pool.wait_ge(made, 1)
                nc.gpsimd.affine_select(out=TRI, in_=TRI, compare_op=ALU.is_gt, fill=0.0, base=0,
                                        pattern=[[1, 128]], channel_multiplier=-1).then_inc(made, 1)
                nc.gpsimd.affine_select(out=ident, in_=ident, compare_op=ALU.is_equal, fill=0.0, base=0,
                                        pattern=[[1, 128]], channel_multiplier=-1).then_inc(made, 1)

            @block.vector
            def _(dve):
                n = [0]

                def step(instruction):
                    instruction.then_inc(chosen, 1)
                    n[0] += 1
                    dve.wait_ge(chosen, n[0])

                t32 = thr[:].bitcast(F32)
                step(nc.vector.tensor_scalar(on, flat, t32, None, ALU.is_equal))
                step(nc.vector.tensor_scalar(above, flat, t32, 0.0, ALU.is_gt, ALU.add, accum_out=cnt[:]))
                dve.wait_ge(gt_sems, 1)
                step(nc.vector.tensor_scalar(left[:], BT, -1.0, float(KTOP), ALU.mult, ALU.add))
                dve.wait_ge(gt_sems, 2)
                step(nc.vector.tensor_copy(before, P[:, 5, :]))
                step(nc.vector.tensor_tensor_scan(rank, W["one_row"][:], before, 0.0, ALU.mult, ALU.add))
                step(nc.vector.tensor_tensor(rank, rank, before, ALU.subtract))
                step(nc.vector.tensor_tensor(rank, rank, P[:, 4, :], ALU.add))
                step(nc.vector.tensor_scalar(rank, rank, left[:], None, ALU.is_lt))
                step(nc.vector.tensor_tensor(rank, rank, on, ALU.mult))
                step(nc.vector.tensor_tensor(rank, rank, above, ALU.add))
                step(nc.vector.tensor_scalar(gates, flat, W["gf"][:, 0:1], None, ALU.mult))
                nc.vector.tensor_tensor(gates, gates, rank, ALU.mult).then_inc(made, 1)
                dve.wait_ge(gt_sems, 3)
                nc.vector.tensor_copy(gt, P[:, 7, :]).then_inc(made, 1)

            @block.tensor
            def _(pe):
                pe.wait_ge(chosen, 2)
                nc.tensor.matmul(BT, W["ones"][:], cnt[:], start=True, stop=True).then_inc(gt_sems, 1)
                pe.wait_ge(made, 3)
                nc.tensor.matmul(P[:, 4, :], TRI, on, start=True, stop=True)
                nc.tensor.matmul(P[:, 5, :], W["ones"][:], on, start=True, stop=True).then_inc(gt_sems, 1)
                pe.wait_ge(made, 4)
                for k in range(4):
                    last = nc.tensor.transpose(P[:, 7, 128 * k:128 * k + 128], gates[:, 128 * k:128 * k + 128],
                                               ident)
                last.then_inc(gt_sems, 1)

            @block.sync
            def _(sp):
                sp.wait_ge(made, 5)
                nc.sync.dma_start(gate_dram.rearrange("(k e) (j p) -> (e j) k p", e=2, p=128),
                                  gt.rearrange("r (k p) -> r k p", k=4)).then_inc(stored, 16)
                sp.wait_ge(stored, 16)

        with nc.Block() as block:
            @block.sync
            def _(sp):
                def gate_load(q, b, u, n):
                    sp.wait_ge(y_out[u], n)
                    nc.sync.dma_start(GB[:, u, :], gate_dram[q - 1, group(b)].partition_broadcast(128)
                                      ).then_inc(gates_loaded[u], 16)

                def expert(q, w, kq, last):
                    with sp.Fori(0, HG) as r:
                        gate_load(q, 2 * r, 0, HG * q + r)
                        gate_load(q, 2 * r + 1, 1, HG * q + r)

                def weights(q, w):
                    sp.wait_ge(y_out[0], HG * (q - 1))
                    sp.wait_ge(y_out[1], HG * (q - 1))
                    nc.sync.dma_start(WR[:, w], experts[q]).then_inc(w_loaded[w], 16)

                weights(2, 0)
                with sp.Fori(0, E0 // 2 - 1) as r:
                    expert(2 * r + 1, 1, r, False)
                    weights(2 * r + 3, 1)
                    expert(2 * r + 2, 0, r + 1, False)
                    weights(2 * r + 4, 0)
                expert(E0 - 1, 1, 0, False)
                expert(E0, 0, 0, True)

            @block.tensor
            def _(pe):
                def expert(q, w, kq, last):
                    over_groups(pe, q, lambda b, u, n: w1(pe, q, w, b, u), lambda b, u, n: w2(pe, w, u, n),
                                (lambda: None) if last else (lambda: w1(pe, q + 1, 1 - w, 0, 0)))
                over_experts(pe, expert)

            @block.scalar
            def _(act):
                def expert(q, w, kq, last):
                    act.wait_ge(w_loaded[w], 16 * kq + 16)
                    with act.Fori(0, HG) as r:
                        gelus(act, q, w, 2 * r, 0, HG * q + r)
                        gelus(act, q, w, 2 * r + 1, 1, HG * q + r)
                over_experts(act, expert)

            @block.gpsimd
            def _(pool):
                def expert(q, w, kq, last):
                    with pool.Fori(0, HG) as r:
                        add(pool, 2 * r, 0, HG * q + r)
                        add(pool, 2 * r + 1, 1, HG * q + r)
                over_experts(pool, expert)

            @block.vector
            def _(dve):
                split(dve, 1, 0, 0, HG)

                def expert(q, w, kq, last):
                    def last_ahead():
                        if not last:
                            split_weights(dve, q + 1, 1 - w, kq + w)
                            split(dve, q + 1, 0, 0, HG * q + HG)
                    over_groups(dve, q, lambda b, u, n: split(dve, q, b, u, n),
                                lambda b, u, n: gated(dve, w, u, n, False), last_ahead)
                over_experts(dve, expert)


def delay_weights(nc, sem, P, W, X, ctxT, ins, we_dram):
    with ExitStack() as ctx:
        def sb(name, shape, dt):
            return ctx.enter_context(nc.sbuf_tensor(name, shape, dt))

        cg = sb("d_cg", [128, 2, TG], F32)
        xc = sb("d_xc", [128, 2, TG], F32)
        sq = sb("d_sq", [128, 2, TG], F32)
        xn = sb("d_xn", [128, TG], F32)
        sx = sb("sx", [128, NB], F32)
        sc = sb("sc", [128, NB], F32)
        wqT = sb("wq1T", [128, 128], F32)
        wkT = sb("wk1T", [128, 128], F32)
        wv = sb("wv1", [128, 128], F32)
        woT = sb("wo1T", [128, 128], F32)
        bqB = sb("bq1B", [128, 128], F32)
        bkB = sb("bk1B", [128, 128], F32)
        bv = sb("bv1", [128, 1], F32)
        bo = sb("bo1", [128, 1], F32)
        qs = sb("qs", [128, 128], F32)
        ks = sb("ks", [128, 128], F32)
        corr = sb("corr", [128, DH], F32)
        peak = sb("d_peak", [128, 1], F32)
        total = sb("d_total", [128, 1], F32)
        WE = sb("WE", [128, 2 * L], F32)

        w_loaded, c_loaded = sem("d_w_loaded"), [sem("d_c_loaded0"), sem("d_c_loaded1")]
        mean, centred, squared, var = sem("d_mean"), sem("d_centred"), sem("d_squared"), sem("d_var")
        log, rstd, normed, summed, c_summed = sem("d_log"), sem("d_rstd"), sem("d_normed"), sem("d_summed"), sem("d_c_summed")
        multiplied, chain, exped, stored = sem("d_multiplied"), sem("d_chain"), sem("d_exped"), sem("d_stored")
        banks_mean = [P[:, 0, :], P[:, 1, :]]
        banks_var = [P[:, 2, :], P[:, 3, :]]
        with nc.Block() as block:
            @block.sync
            def _(sp):
                for dst, name in ((wqT, "wq1T"), (wkT, "wk1T"), (wv, "L1_xattn_Wv"), (woT, "wo1T")):
                    nc.sync.dma_start(dst[:], ins[name]).then_inc(w_loaded, 16)
                for dst, name in ((bqB, "L1_xattn_bq"), (bkB, "L1_xattn_bk")):
                    nc.sync.dma_start(dst[:], ins[name].partition_broadcast(128)).then_inc(w_loaded, 16)
                for dst, name in ((bv, "L1_xattn_bv"), (bo, "L1_xattn_bo")):
                    nc.sync.dma_start(dst[:], ins[name].rearrange("(p a) -> p a", a=1)).then_inc(w_loaded, 16)
                with sp.Fori(0, G // 2) as r:
                    for p in range(2):
                        sp.wait_ge(c_summed, 2 * r)
                        nc.sync.dma_start(cg[:, p, :], ctxT[:, group(2 * r + p)]).then_inc(c_loaded[p], 16)
                sp.wait_ge(chain, 1)
                nc.sync.dma_start(we_dram, WE[:]).then_inc(stored, 16)
                sp.wait_ge(stored, 16)

            @block.tensor
            def _(pe):
                def lead(i, p):
                    need(pe, centred, i - 1)
                    nc.tensor.matmul(banks_mean[p], W["mean"][:], X[:, group(i)],
                                     start=True, stop=True).then_inc(mean, 1)

                def lag(i, p):
                    pe.wait_ge(squared, i + 1)
                    nc.tensor.matmul(banks_var[p], W["mean"][:], sq[:, p, :],
                                     start=True, stop=True).then_inc(var, 1)

                skewed(pe, lead, lag)
                pe.wait_ge(w_loaded, 128)
                nc.tensor.matmul(P[:, 6, 0:128], wv[:], woT[:], start=True, stop=True).then_inc(multiplied, 1)
                nc.tensor.matmul(P[:, 7, 0:1], woT[:], bv[:], start=True, stop=True).then_inc(multiplied, 1)
                pe.wait_ge(summed, G)
                pe.wait_ge(c_summed, G)
                nc.tensor.matmul(P[:, 4, 0:128], sx[:], wqT[:], start=True, stop=True).then_inc(multiplied, 1)
                nc.tensor.matmul(P[:, 5, 0:128], sc[:], wkT[:], start=True, stop=True).then_inc(multiplied, 1)

            @block.scalar
            def _(act):
                def lead(i, p):
                    act.wait_ge(centred, i + 1)
                    need(act, normed, i - 1)
                    nc.scalar.activation(sq[:, p, :], xc[:, p, :], ACT.Square).then_inc(squared, 1)

                def lag(i, p):
                    act.wait_ge(var, i + 1)
                    nc.scalar.activation(sq[:, p, :], banks_var[p], ACT.Ln, bias=W["eps"][:, 0:1]).then_inc(log, 1)
                    act.wait_ge(log, i + 1)
                    nc.scalar.activation(sq[:, p, :], sq[:, p, :], ACT.Exp, scale=-0.5).then_inc(rstd, 1)

                skewed(act, lead, lag)
                act.wait_ge(exped, 1)
                nc.scalar.activation(corr[:], corr[:], ACT.Exp, accum_out=total[:]).then_inc(exped, 1)

            @block.vector
            def _(dve):
                def lead(i, p):
                    dve.wait_ge(mean, i + 1)
                    need(dve, normed, i - 1)
                    nc.vector.tensor_tensor(xc[:, p, :], X[:, group(i)], banks_mean[p],
                                            ALU.subtract).then_inc(centred, 1)

                def lag(i, p):
                    dve.wait_ge(rstd, i + 1)
                    need(dve, summed, i)
                    nc.vector.tensor_tensor(xn[:], xc[:, p, :], sq[:, p, :], ALU.mult).then_inc(normed, 1)
                    if isinstance(i, int):
                        dve.wait_ge(c_loaded[p], 16 * (i // 2 + 1))
                    else:
                        dve.wait_ge(c_loaded[p], 8 * (i - p) + 16)
                    nc.vector.tensor_reduce(sc[:, bass.ds(i * NBG, NBG)], cg[:, p, :].rearrange("p (n l) -> p n l", l=L),
                                            AX.X, ALU.add).then_inc(c_summed, 1)
                    dve.wait_ge(normed, i + 1)
                    nc.vector.tensor_reduce(sx[:, bass.ds(i * NBG, NBG)], xn[:].rearrange("p (n l) -> p n l", l=L),
                                            AX.X, ALU.add).then_inc(summed, 1)

                skewed(dve, lead, lag)
                n = [0]
                steps = sem("d_steps")

                def step(instruction):
                    instruction.then_inc(steps, 1)
                    n[0] += 1
                    dve.wait_ge(steps, n[0])

                step(nc.vector.memset(WE[:], 0.0))
                dve.wait_ge(multiplied, 2)
                step(nc.vector.tensor_scalar(W["wvo1"][:], P[:, 6, 0:128], W["gx"][:, 1:2], None, ALU.mult))
                step(nc.vector.tensor_tensor(W["bvo1"][:], P[:, 7, 0:1], bo[:], ALU.add))
                step(nc.vector.tensor_scalar(W["bvo1"][:], W["bvo1"][:], W["gx"][:, 1:2], None, ALU.mult))
                dve.wait_ge(multiplied, 4)
                step(nc.vector.scalar_tensor_tensor(out=qs[:], in0=bqB[:], scalar=float(L), in1=P[:, 4, 0:128],
                                                    op0=ALU.mult, op1=ALU.add))
                step(nc.vector.scalar_tensor_tensor(out=ks[:], in0=bkB[:], scalar=float(L), in1=P[:, 5, 0:128],
                                                    op0=ALU.mult, op1=ALU.add))
                step(nc.vector.tensor_tensor(qs[:], qs[:], ks[:], ALU.mult))
                step(nc.vector.tensor_reduce(corr[:], qs[:].rearrange("p (h c) -> p c h", h=H), AX.X, ALU.add))
                step(nc.vector.tensor_scalar(corr[:], corr[:], 1.0 / (H * L), None, ALU.mult))
                step(nc.vector.tensor_reduce(peak[:], corr[:], AX.X, ALU.max))
                nc.vector.tensor_scalar(corr[:], corr[:], peak[:], None, ALU.subtract).then_inc(exped, 1)
                dve.wait_ge(exped, 2)
                step(nc.vector.reciprocal(total[:], total[:]))
                step(nc.vector.tensor_scalar(corr[:], corr[:], total[:], None, ALU.mult))
                for d in range(DH):
                    step(nc.vector.tensor_copy(WE[:, L - d:L - d + 1], corr[:, d:d + 1]))
                    if d:
                        step(nc.vector.tensor_copy(WE[:, 2 * L - d:2 * L - d + 1], corr[:, d:d + 1]))
                nc.vector.tensor_copy(peak[:], total[:]).then_inc(chain, 1)


def delays_and_routes(nc, sem, P, W, X, XH, XL, WFH, WFL, ins, we_dram, c_dram):
    with ExitStack() as ctx:
        def sb(name, shape, dt):
            return ctx.enter_context(nc.sbuf_tensor(name, shape, dt))

        WRAW = sb("WRAW", [128, 2, 3 * 128], F32)
        cn = sb("cn", [128, 2, TPG, 128], F32)
        CM = sb("CM", [128, 2, TPG, 128], F32)
        ag = sb("ag", [128, TG], F32)
        xc = sb("e_xc", [128, 2, TG], F32)
        sq = sb("e_sq", [128, 2, TG], F32)
        xn = sb("e_xn", [128, TG], F32)
        ident = sb("ident", [128, 128], F32)
        biasB = sb("biasB", [128, E1], F32)
        gw = sb("gw1", [128, E1], F32)
        seg = [sb("seg_g", [128, TPG, NG1], F32), sb("seg_e", [128, TPG, E1], F32)]
        R = {n: sb("r_" + n, [128, TPG, k], F32) for n, k in {
            "exp": E1, "score": E1, "choice": E1, "group": NG1, "top": 8, "above": E1, "on": E1,
            "rank": E1, "count": 1, "pick_g": NG1, "pick_e": E1, "weight": E1, "sum": 1, "comb": E1, "idle": 1}.items()}
        ct = sb("ct", [E1, 2, TG], F32)

        w_loaded, raw_loaded = sem("e_w_loaded"), sem("e_raw_loaded")
        wf_hi, wf_lo, ready = sem("e_wf_hi"), sem("e_wf_lo"), sem("e_ready")
        with nc.Block() as block:
            @block.sync
            def _(sp):
                nc.sync.dma_start(gw[:], ins["gate1T"]).then_inc(w_loaded, 16)
                nc.sync.dma_start(biasB[:], ins["L1_ffn_e_score_correction_bias"].partition_broadcast(128)
                                  ).then_inc(w_loaded, 16)
                with sp.Fori(0, PAIRS) as r:
                    sp.wait_ge(wf_lo, r)
                    nc.sync.dma_start(WRAW[:, 0], ins["experts1"][:, r]).then_inc(raw_loaded, 16)

            @block.vector
            def _(dve):
                nc.vector.memset(CM[:], 0.0).then_inc(ready, 1)
                for s in seg:
                    nc.vector.memset(s[:], 1.0).then_inc(ready, 1)
                dve.wait_ge(ready, 3)
                for s in seg:
                    nc.vector.memset(s[:, :, 0:1], 0.0).then_inc(ready, 1)
                with dve.Fori(0, PAIRS) as r:
                    dve.wait_ge(raw_loaded, 16 * r + 16)
                    nc.vector.tensor_copy(WFH[:, r], WRAW[:, 0]).then_inc(wf_hi, 1)
                    dve.wait_ge(wf_hi, r + 1)
                    nc.vector.tensor_tensor(WFL[:, r], WRAW[:, 0], WFH[:, r].bitcast(F32),
                                            ALU.subtract).then_inc(wf_lo, 1)
                dve.wait_ge(ready, 5)

            @block.gpsimd
            def _(pool):
                made = sem("e_ident")
                nc.gpsimd.memset(ident[:], 1.0).then_inc(made, 1)
                pool.wait_ge(made, 1)
                nc.gpsimd.affine_select(out=ident[:], in_=ident[:], compare_op=ALU.is_equal, fill=0.0, base=0,
                                        pattern=[[1, 128]], channel_multiplier=-1).then_inc(made, 1)
                pool.wait_ge(made, 2)

        loaded = [sem("e_loaded0"), sem("e_loaded1")]
        agg, agg_out, projected, x3 = sem("e_agg"), sem("e_agg_out"), sem("e_projected"), sem("e_x3")
        mean, centred, squared, var = sem("e_mean"), sem("e_centred"), sem("e_squared"), sem("e_var")
        log, rstd, normed, hi, lo = sem("e_log"), sem("e_rstd"), sem("e_normed"), sem("e_hi"), sem("e_lo")
        logits, exped, chosen, turned, turned_out = (sem("e_logits"), sem("e_exped"), sem("e_chosen"),
                                                     sem("e_turned"), sem("e_turned_out"))
        stored = [sem("e_stored0"), sem("e_stored1")]
        steps = sem("e_steps")
        BAG, BPR, BL, BTR = P[:, 0, :], P[:, 1, :], P[:, 6, 0:TPG * E1], P[0:E1, 7, :]
        banks_mean, banks_var = [P[:, 2, :], P[:, 3, :]], [P[:, 4, :], P[:, 5, :]]
        block = ctx.enter_context(nc.Block())

        @block.sync
        def _(sp):
            we = we_dram.rearrange("n j -> (n j)")
            ctx_n = ins["ctxN"].rearrange("(g j p) d -> g p j d", j=TPG, p=128)

            def load(i, p):
                need(sp, agg, i - 1)
                nc.sync.dma_start(cn[:, p], ctx_n[i]).then_inc(loaded[p], 16)
                for u in range(2):
                    at = we[bass.ds((i * NBG + u) * 2 * L + 1, 1)]
                    src = bass.AP(at.tensor, at.offset, [[1, L], [4 * L, TPG], [1, L]])
                    nc.sync.dma_start(CM[64 * u:64 * u + 64, p, :, 64 * u:64 * u + 64], src).then_inc(loaded[p], 16)

            def store(i, p):
                sp.wait_ge(turned_out, i + 1)
                nc.sync.dma_start(c_dram[:, group(i)], ct[:, p, :]).then_inc(stored[p], 16)

            load(0, 0)
            load(1, 1)
            with sp.Fori(0, G // 2 - 1) as r:
                for p in range(2):
                    load(2 * r + 2 + p, p)
                    store(2 * r + p, p)
            store(G - 2, 0)
            store(G - 1, 1)
            for p in range(2):
                sp.wait_ge(stored[p], 8 * G)

        @block.tensor
        def _(pe):
            def lead(i, p):
                if isinstance(i, int):
                    pe.wait_ge(loaded[p], 48 * (i // 2 + 1))
                else:
                    pe.wait_ge(loaded[p], 24 * (i - p) + 48)
                need(pe, agg_out, i)
                for t in range(TPG):
                    last = nc.tensor.matmul(BAG[:, 128 * t:128 * t + 128], cn[:, p, t, :], CM[:, p, t, :],
                                            start=True, stop=True)
                last.then_inc(agg, 1)
                pe.wait_ge(agg_out, i + 1)
                need(pe, x3, i)
                nc.tensor.matmul(BPR, W["wvo1"][:], ag[:], start=True, stop=True).then_inc(projected, 1)
                pe.wait_ge(x3, i + 1)
                need(pe, centred, i - 1)
                nc.tensor.matmul(banks_mean[p], W["mean"][:], X[:, group(i)], start=True, stop=True).then_inc(mean, 1)

            def lag(i, p):
                pe.wait_ge(squared, i + 1)
                nc.tensor.matmul(banks_var[p], W["mean"][:], sq[:, p, :], start=True, stop=True).then_inc(var, 1)
                pe.wait_ge(normed, i + 1)
                need(pe, exped, i)
                for t in range(TPG):
                    last = nc.tensor.matmul(BL[:, E1 * t:E1 * t + E1], xn[:, 128 * t:128 * t + 128], gw[:],
                                            start=True, stop=True)
                last.then_inc(logits, 1)
                pe.wait_ge(chosen, i + 1)
                need(pe, turned_out, i)
                for t in range(TPG):
                    last = nc.tensor.transpose(BTR[:, 128 * t:128 * t + 128], R["comb"][:, t, :], ident[:])
                last.then_inc(turned, 1)

            pe.wait_ge(w_loaded, 32)
            skewed(pe, lead, lag)

        @block.scalar
        def _(act):
            def lead(i, p):
                act.wait_ge(agg, i + 1)
                need(act, projected, i)
                nc.scalar.activation(ag[:], BAG, ACT.Copy).then_inc(agg_out, 1)
                act.wait_ge(centred, i + 1)
                need(act, normed, i - 1)
                nc.scalar.activation(sq[:, p, :], xc[:, p, :], ACT.Square).then_inc(squared, 1)

            def lag(i, p):
                act.wait_ge(var, i + 1)
                nc.scalar.activation(sq[:, p, :], banks_var[p], ACT.Ln, bias=W["eps"][:, 0:1]).then_inc(log, 1)
                act.wait_ge(log, i + 1)
                nc.scalar.activation(sq[:, p, :], sq[:, p, :], ACT.Exp, scale=-0.5).then_inc(rstd, 1)
                act.wait_ge(logits, i + 1)
                need(act, chosen, i)
                nc.scalar.activation(R["exp"][:].rearrange("p t e -> p (t e)"), BL, ACT.Exp,
                                     scale=-1.0).then_inc(exped, 1)
                act.wait_ge(turned, i + 1)
                if not isinstance(i, int) or i >= 2:
                    act.wait_ge(stored[p], 8 * (i - p))
                nc.scalar.activation(ct[:, p, :], BTR, ACT.Copy).then_inc(turned_out, 1)

            skewed(act, lead, lag)

        @block.vector
        def _(dve):
            def lead(i, p):
                dve.wait_ge(projected, i + 1)
                nc.vector.scalar_tensor_tensor(out=X[:, group(i)], in0=BPR, scalar=W["bvo1"][:, 0:1],
                                               in1=X[:, group(i)], op0=ALU.add, op1=ALU.add).then_inc(x3, 1)
                dve.wait_ge(mean, i + 1)
                need(dve, normed, i - 1)
                nc.vector.tensor_tensor(xc[:, p, :], X[:, group(i)], banks_mean[p], ALU.subtract).then_inc(centred, 1)

            def route(i):
                k = [0]

                def step(instruction):
                    instruction.then_inc(steps, 1)
                    k[0] += 1
                    dve.wait_ge(steps, NSTEPS * i + k[0])

                flat = {x: R[x][:].rearrange("p t e -> p (t e)") for x in R}

                def top_mask(v, n, keep, pick, start):
                    above = flat["above"][:, 0:TPG * n].rearrange("p (t e) -> p t e", t=TPG)
                    on = flat["on"][:, 0:TPG * n].rearrange("p (t e) -> p t e", t=TPG)
                    rank = flat["rank"][:, 0:TPG * n].rearrange("p (t e) -> p t e", t=TPG)
                    nc.vector.memset(R["idle"][:], 0.0)
                    for t in range(TPG):
                        ins_ = nc.vector.max(R["top"][:, t, :], v[:, t, :])
                        if t < TPG - 1:
                            ins_.then_inc(steps, 1)
                            k[0] += 1
                    step(ins_)
                    least = R["top"][:, :, keep - 1:keep].to_broadcast([128, TPG, n])
                    nc.vector.tensor_tensor(on, v[:], least, ALU.is_equal).then_inc(steps, 1)
                    k[0] += 1
                    step(nc.vector.tensor_tensor(above, v[:], least, ALU.is_gt))
                    nc.vector.tensor_reduce(R["count"][:, :, 0], above, AX.X, ALU.add).then_inc(steps, 1)
                    k[0] += 1
                    step(nc.vector.tensor_tensor_scan(flat["rank"][:, 0:TPG * n],
                                                      start[:].rearrange("p t e -> p (t e)"),
                                                      flat["on"][:, 0:TPG * n], 0.0, ALU.mult, ALU.add))
                    step(nc.vector.tensor_tensor(rank, rank, R["count"][:].to_broadcast([128, TPG, n]), ALU.add))
                    step(nc.vector.scalar_tensor_tensor(out=flat["rank"][:, 0:TPG * n], in0=flat["rank"][:, 0:TPG * n],
                                                        scalar=float(keep), in1=flat["on"][:, 0:TPG * n],
                                                        op0=ALU.is_le, op1=ALU.mult))
                    step(nc.vector.tensor_tensor(pick[:], rank, above, ALU.add))

                dve.wait_ge(exped, i + 1)
                step(nc.vector.tensor_scalar(flat["score"], flat["exp"], 1.0, None, ALU.add))
                step(nc.vector.reciprocal(flat["score"], flat["score"]))
                step(nc.vector.tensor_tensor(R["choice"][:], R["score"][:],
                                             biasB[:].unsqueeze(1).to_broadcast([128, TPG, E1]), ALU.add))
                step(nc.vector.tensor_reduce(flat["group"], flat["choice"].rearrange("p (g s) -> p g s", s=GS1),
                                             AX.X, ALU.max))
                top_mask(R["group"], NG1, TOPG1, R["pick_g"], seg[0])
                step(nc.vector.tensor_tensor(flat["choice"].rearrange("p (g s) -> p g s", s=GS1),
                                             flat["choice"].rearrange("p (g s) -> p g s", s=GS1),
                                             flat["pick_g"].unsqueeze(2).to_broadcast([128, TPG * NG1, GS1]),
                                             ALU.mult))
                top_mask(R["choice"], E1, TOPK1, R["pick_e"], seg[1])
                step(nc.vector.tensor_tensor(R["weight"][:], R["score"][:], R["pick_e"][:], ALU.mult))
                step(nc.vector.tensor_reduce(R["sum"][:, :, 0], R["weight"][:], AX.X, ALU.add))
                step(nc.vector.tensor_scalar(flat["sum"], flat["sum"], 1e-20, None, ALU.add))
                step(nc.vector.reciprocal(flat["sum"], flat["sum"]))
                step(nc.vector.tensor_scalar(flat["sum"], flat["sum"], SCALE1, None, ALU.mult))
                need(dve, turned, i)
                nc.vector.tensor_tensor(R["comb"][:], R["weight"][:], R["sum"][:].to_broadcast([128, TPG, E1]),
                                        ALU.mult).then_inc(chosen, 1)
                assert k[0] == NSTEPS, k[0]

            NSTEPS = 32

            def lag(i, p):
                dve.wait_ge(rstd, i + 1)
                need(dve, logits, i)
                need(dve, lo, i)
                nc.vector.tensor_tensor(xn[:], xc[:, p, :], sq[:, p, :], ALU.mult).then_inc(normed, 1)
                dve.wait_ge(normed, i + 1)
                nc.vector.tensor_copy(XH[:, group(i)], xn[:]).then_inc(hi, 1)
                dve.wait_ge(hi, i + 1)
                nc.vector.tensor_tensor(XL[:, group(i)], xn[:], XH[:, group(i)].bitcast(F32),
                                        ALU.subtract).then_inc(lo, 1)
                route(i)

            skewed(dve, lead, lag)


def second_ffn(nc, sem, P, W, X, XH, XL, WFH, WFL, c_dram, out):
    with ExitStack() as ctx:
        def sb(name, shape, dt):
            return ctx.enter_context(nc.sbuf_tensor(name, shape, dt))

        CQ = 4
        NC = (PAIRS - 1) // CQ
        CB = sb("CB", [128, 2, CQ, TG], F32)
        sg = sb("f_silu", [128, 2, TG], F32)
        au = sb("f_au", [128, 2, TG], F32)
        ac = sb("f_ac", [128, 2, TG], F32)
        hh = sb("f_hh", [128, 2, TG], F32R)
        hl = sb("f_hl", [128, 2, TG], F32R)
        o32 = sb("f_out", [128, 2, TG], F32)
        g_done, u_done, silu_done, gated = sem("f_g"), sem("f_u"), sem("f_silu_done"), sem("f_gated")
        weighted, hi, lo, summed = sem("f_weighted"), sem("f_hi"), sem("f_lo"), sem("f_summed")
        y_done, y_out = sem("f_y"), sem("f_y_out")
        c_loaded, stored = [sem("f_c0"), sem("f_c1")], [sem("f_stored0"), sem("f_stored1")]
        BG, BU, BY = [P[:, 0, :], P[:, 1, :]], [P[:, 2, :], P[:, 3, :]], [P[:, 4, :], P[:, 5, :]]
        N2 = 2 * PAIRS
        block = ctx.enter_context(nc.Block())

        def pair(n):
            return n // PAIRS % 2, n % PAIRS

        @block.sync
        def _(sp):
            c_view = c_dram.rearrange("(k e) t -> k e t", e=2)

            def load(r, b, j):
                q = (NC * b + j) % 2
                n = NC * b + j - 2
                done = (n // NC) * (PAIRS - 1) + (n % NC + 1) * CQ
                if done > 0 or not isinstance(r, int):
                    need(sp, weighted, 2 * (PAIRS - 1) * r + done)
                for e in range(2):
                    src = c_view[CQ * j:CQ * j + CQ, e, group(2 * r + b)]
                    nc.sync.dma_start(CB[64 * e:64 * e + 64, q], src.partition_broadcast(64)
                                      ).then_inc(c_loaded[q], 16)

            def store(i, b, r):
                sp.wait_ge(y_out, i + 1)
                nc.sync.dma_start(out[:, group(i)], o32[:, b, :]).then_inc(stored[b], 16)

            def body(r):
                for b in range(2):
                    for j in range(NC):
                        load(r, b, j)
                    if b == 1:
                        store(2 * r, 0, r)
                    elif not isinstance(r, int):
                        store(2 * r - 1, 1, r)

            body(0)
            with sp.Fori(1, G // 2) as r:
                body(r)
            store(G - 1, 1, 0)
            for b in range(2):
                sp.wait_ge(stored[b], 8 * G)

        @block.tensor
        def _(pe):
            def up(r, n):
                b, k = pair(n)
                s = n % 2
                g = group(2 * r + n // PAIRS)
                for bank, col, done, freed in ((BG[s], 0, g_done, silu_done), (BU[s], 128, u_done, gated)):
                    if not (isinstance(r, int) and n < 2 and r == 0):
                        need(pe, freed, N2 * r + n - 1)
                    for m, (w, x) in enumerate(((WFH, XH), (WFL, XH), (WFH, XL))):
                        last = nc.tensor.matmul(bank, w[:, k, col:col + 128], x[:, g],
                                                start=(m == 0), stop=(m == 2))
                    last.then_inc(done, 1)

            def down(r, n):
                b, k = pair(n)
                s = n % 2
                if k == 0:
                    need(pe, y_out, 2 * r + b - 1) if not isinstance(r, int) else None
                pe.wait_ge(lo, N2 * r + n + 1)
                for m, (w, h) in enumerate(((WFH, hh), (WFL, hh), (WFH, hl))):
                    last = nc.tensor.matmul(BY[b], w[:, k, 256:384], h[:, s, :],
                                            start=(k == 0 and m == 0), stop=(k == PAIRS - 1 and m == 2))
                last.then_inc(summed, 1)

            def step(r, last):
                for n in range(N2):
                    if n + 2 < N2 or not last:
                        up(r, n + 2)
                    down(r, n)

            up(0, 0)
            up(0, 1)
            step(0, False)
            with pe.Fori(1, G // 2 - 1) as r:
                step(r, False)
            step(G // 2 - 1, True)

        @block.scalar
        def _(act):
            def body(r):
                for n in range(N2):
                    s = n % 2
                    act.wait_ge(g_done, N2 * r + n + 1)
                    if not (isinstance(r, int) and n < 2):
                        need(act, gated, N2 * r + n - 1)
                    nc.scalar.activation(sg[:, s, :], BG[s], ACT.Silu).then_inc(silu_done, 1)

            body(0)
            with act.Fori(1, G // 2) as r:
                body(r)

        @block.gpsimd
        def _(pool):
            def body(r):
                m = 0
                for n in range(N2):
                    b, k = pair(n)
                    s = n % 2
                    if k == PAIRS - 1:
                        continue
                    j = NC * b + k // CQ
                    if k % CQ == 0:
                        pool.wait_ge(c_loaded[j % 2], 32 * (NC * r + j // 2 + 1))
                    pool.wait_ge(gated, N2 * r + n + 1)
                    if not (isinstance(r, int) and n < 2):
                        need(pool, lo, N2 * r + n - 1)
                    nc.gpsimd.tensor_tensor(ac[:, s, :], au[:, s, :], CB[:, j % 2, k % CQ, :],
                                            ALU.mult).then_inc(weighted, 1)

            body(0)
            with pool.Fori(1, G // 2) as r:
                body(r)

        @block.vector
        def _(dve):
            def gate(r, n):
                s = n % 2
                dve.wait_ge(silu_done, N2 * r + n + 1)
                dve.wait_ge(u_done, N2 * r + n + 1)
                if not (isinstance(r, int) and n < 2):
                    need(dve, lo, N2 * r + n - 1)
                nc.vector.tensor_tensor(au[:, s, :], sg[:, s, :], BU[s], ALU.mult).then_inc(gated, 1)

            def split(r, n):
                b, k = pair(n)
                s = n % 2
                shared = k == PAIRS - 1
                src = au if shared else ac
                if shared:
                    dve.wait_ge(gated, N2 * r + n + 1)
                else:
                    dve.wait_ge(weighted, 2 * (PAIRS - 1) * r + b * (PAIRS - 1) + k + 1)
                if not (isinstance(r, int) and n < 2):
                    need(dve, summed, N2 * r + n - 1)
                nc.vector.tensor_copy(hh[:, s, :], src[:, s, :]).then_inc(hi, 1)
                dve.wait_ge(hi, N2 * r + n + 1)
                nc.vector.tensor_tensor(hl[:, s, :], src[:, s, :], hh[:, s, :].bitcast(F32),
                                        ALU.subtract).then_inc(lo, 1)

            def result(r, b):
                i = 2 * r + b
                dve.wait_ge(summed, N2 * r + PAIRS * (b + 1))
                if not isinstance(r, int):
                    dve.wait_ge(stored[b], 16 * r)
                nc.vector.scalar_tensor_tensor(out=o32[:, b, :], in0=BY[b], scalar=W["gf"][:, 1:2],
                                               in1=X[:, group(i)], op0=ALU.mult, op1=ALU.add).then_inc(y_out, 1)

            def body(r):
                for n in range(N2):
                    gate(r, n)
                    if n:
                        split(r, n - 1)
                    if n == PAIRS + 3:
                        result(r, 0)
                split(r, N2 - 1)
                result(r, 1)

            body(0)
            with dve.Fori(1, G // 2) as r:
                body(r)


def shared_constants(nc, sem, W, ins):
    loaded, done = sem("const_loaded"), sem("const_done")
    with ExitStack() as ctx:
        block = ctx.enter_context(nc.Block())
        dmas = []

        @block.sync
        def _(sp):
            def load(dst, src):
                nc.sync.dma_start(dst, src).then_inc(loaded, 16)
                dmas.append(1)

            def column(v):
                return v.rearrange("(p a) -> p a", a=1)

            load(W["wq0"][:], ins["L0_xattn_Wq"])
            load(W["wk0"][:], ins["L0_xattn_Wk"])
            load(W["wv0"][:], ins["L0_xattn_Wv"])
            sp.wait_ge(done, 1)
            for u in range(2):
                load(W["wo0"][64 * u:64 * u + 64, u], ins["L0_xattn_Wo"].rearrange("(a r) d -> r a d", a=2))
            load(W["gw0"][:], ins["gate0T"])
            load(W["bq0"][:], column(ins["L0_xattn_bq"]))
            load(W["bk0"][:], column(ins["L0_xattn_bk"]))
            load(W["bo0"][:], column(ins["L0_xattn_bo"]))
            load(W["bv0"][:], ins["L0_xattn_bv"].partition_broadcast(128))
            load(W["gx"][:], ins["g_xattn"].partition_broadcast(128))
            load(W["gf"][:], ins["g_ffn"].partition_broadcast(128))

        n_loaded = 16 * len(dmas)

        @block.vector
        def _(dve):
            nc.vector.memset(W["wo0"][:], 0.0).then_inc(done, 1)
            nc.vector.memset(W["mean"][:], 1.0 / D).then_inc(done, 1)
            nc.vector.memset(W["ones"][:], 1.0).then_inc(done, 1)
            nc.vector.memset(W["one_row"][:], 1.0).then_inc(done, 1)
            nc.vector.memset(W["eps"][:], EPS).then_inc(done, 1)
            dve.wait_ge(done, 7)
            dve.wait_ge(loaded, n_loaded)
            nc.vector.tensor_scalar(W["wo0"][:].rearrange("p u a d -> p (u a d)"),
                                    W["wo0"][:].rearrange("p u a d -> p (u a d)"),
                                    W["gx"][:, 0:1], None, ALU.mult).then_inc(done, 1)
            nc.vector.tensor_scalar(W["bo0"][:], W["bo0"][:], W["gx"][:, 0:1], None, ALU.mult).then_inc(done, 1)

        @block.scalar
        def _(act):
            act.wait_ge(loaded, n_loaded)
            nc.scalar.activation(W["gx"][:], W["gx"][:], ACT.Tanh).then_inc(done, 1)
            nc.scalar.activation(W["gf"][:], W["gf"][:], ACT.Tanh).then_inc(done, 1)


def program(nc, ins, out, stop="all"):
    with ExitStack() as ctx:
        ctx.enter_context(nc.allow_low_precision(reason="operands split in halves"))
        def sem(name):
            return ctx.enter_context(nc.semaphore(name))

        def sb(name, shape, dt):
            return ctx.enter_context(nc.sbuf_tensor(name, shape, dt))

        P = ctx.enter_context(nc.psum_tensor("P", [128, 8, TG], F32))
        W = {n: sb("w_" + n, s, F32) for n, s in {
            "wq0": [128, 128], "wk0": [128, 128], "wv0": [128, 128], "wo0": [128, 2, 2, 128],
            "gw0": [128, E0], "bq0": [128, 1], "bk0": [128, 1], "bo0": [128, 1], "bv0": [128, 128],
            "gx": [128, 2], "gf": [128, 2], "mean": [128, 128], "ones": [128, 128], "eps": [128, 1],
            "one_row": [128, TG], "wvo1": [128, 128], "bvo1": [128, 1],
        }.items()}
        XH = sb("XH", [128, T], F32R)
        XL = sb("XL", [128, T], F32R)
        SC = sb("SC", [128, E0, NT], F32)
        scratch = nc.dram_tensor("qk_scratch", [2, 2, 2, 128, TG], F16)
        x1_dram = nc.dram_tensor("x1_dram", [128, T], F32)
        shared_constants(nc, sem, W, ins)
        attention(nc, sem, P, W, XH, XL, SC, ins["xT"], ins["ctxT"], scratch.ap(), x1_dram.ap())
        if stop == "A":
            with nc.Block() as block:
                s = sem("dbg")
                @block.sync
                def _(sp):
                    nc.sync.dma_start(out, x1_dram.ap()).then_inc(s, 16)
                    dbg = nc.dram_tensor("dbg_sc", [128, E0, NT], F32)
                    nc.sync.dma_start(dbg.ap(), SC[:]).then_inc(s, 16)
                    sp.wait_ge(s, 32)
            return
        gate_dram = nc.dram_tensor("gate_dram", [E0, T], F32)
        X = sb("X", [128, T], F32)
        first_ffn(nc, sem, P, W, X, XH, XL, SC, ins["experts0"], x1_dram.ap(), gate_dram.ap())
        if stop == "C":
            with nc.Block() as block:
                s = sem("dbg")
                @block.sync
                def _(sp):
                    nc.sync.dma_start(out, X[:]).then_inc(s, 16)
                    sp.wait_ge(s, 16)
            return
        we_dram = nc.dram_tensor("we_dram", [NB, 2 * L], F32)
        c_dram = nc.dram_tensor("c_dram", [E1, T], F32)
        delay_weights(nc, sem, P, W, X, ins["ctxT"], ins, we_dram.ap())
        WFH = sb("WFH", [128, PAIRS, 3 * 128], F32R)
        WFL = sb("WFL", [128, PAIRS, 3 * 128], F32R)
        delays_and_routes(nc, sem, P, W, X, XH, XL, WFH, WFL, ins, we_dram.ap(), c_dram.ap())
        if stop == "E":
            with nc.Block() as block:
                s = sem("dbg")
                @block.sync
                def _(sp):
                    nc.sync.dma_start(out, X[:]).then_inc(s, 16)
                    dbg = nc.dram_tensor("dbg_a", [E1, T], F32)
                    nc.sync.dma_start(dbg.ap(), c_dram.ap()).then_inc(s, 16)
                    sp.wait_ge(s, 32)
            return
        second_ffn(nc, sem, P, W, X, XH, XL, WFH, WFL, c_dram.ap(), out)


def kernel(**inputs):
    import numpy as np
    import concourse.bacc as bacc
    from concourse.bass_utils import run_bass_kernel_spmd as run

    a = {k: np.asarray(v) for k, v in inputs.items()}
    laid = {k: a[k] for k in ("g_xattn", "g_ffn", "L0_xattn_Wq", "L0_xattn_bq", "L0_xattn_Wk", "L0_xattn_bk",
                              "L0_xattn_Wv", "L0_xattn_bv", "L0_xattn_Wo", "L0_xattn_bo")}
    laid["xT"] = a["x"].reshape(T, D).T
    laid["ctxT"] = a["ctx_1024"].reshape(T, D).T
    laid["gate0T"] = a["L0_ffn_gate_weight"].T
    laid["ctxN"] = a["ctx_1024"][:, ::-1, :].reshape(T, D)
    laid["wq1T"] = a["L1_xattn_Wq"].T
    laid["wk1T"] = a["L1_xattn_Wk"].T
    laid["wo1T"] = a["L1_xattn_Wo"].T
    laid["gate1T"] = a["L1_ffn_gate_weight"].T
    laid.update({k: a[k] for k in ("L1_xattn_Wv", "L1_xattn_bq", "L1_xattn_bk", "L1_xattn_bv", "L1_xattn_bo",
                                   "L1_ffn_e_score_correction_bias")})
    gu = np.concatenate([a["L1_ffn_experts_gate_up"].reshape(E1 // 2, 2, 2, I1, D).transpose(0, 2, 1, 3, 4),
                         np.stack([a["L1_ffn_shared_gate_w"], a["L1_ffn_shared_up_w"]]).reshape(1, 2, 2, I1, D)])
    down = np.concatenate([a["L1_ffn_experts_down"].transpose(0, 2, 1).reshape(E1 // 2, 2 * I1, D),
                           a["L1_ffn_shared_down_w"].T[None]])
    laid["experts1"] = np.concatenate([gu.reshape(PAIRS, 4 * I1, D).transpose(2, 0, 1), down.transpose(1, 0, 2)],
                                      axis=2)

    def rows(w1, b1, w2, b2):
        e = w1.shape[0]
        w2c = w2.reshape(e, FC, 128, D).transpose(0, 2, 1, 3).reshape(e, 128, FC * D)
        b1c = b1.reshape(e, FC, 128).transpose(0, 2, 1)
        return np.concatenate([w1, w2c, b1c, b2[:, :, None]], axis=2)

    laid["experts0"] = np.concatenate([
        rows(a["L0_ffn_Ws1"][None], a["L0_ffn_bs1"][None], a["L0_ffn_Ws2"][None], a["L0_ffn_bs2"][None]),
        rows(a["L0_ffn_W1"], a["L0_ffn_b1"], a["L0_ffn_W2"], a["L0_ffn_b2"])])
    nc = bacc.Bacc("TRN2", target_bir_lowering=False, num_devices=1)
    arrays, ins = {}, {}
    for name, v in laid.items():
        v = np.ascontiguousarray(v)
        arrays[f"in_{name}"] = v
        ins[name] = nc.dram_tensor(f"in_{name}", v.shape, mybir.dt.from_np(v.dtype), kind="ExternalInput").ap()
    out = nc.dram_tensor("out_T", [D, T], F32, kind="ExternalOutput")
    program(nc, ins, out.ap(), STOP)
    r = run(nc, [arrays], core_ids=[0])
    return np.ascontiguousarray(r.results[0]["out_T"].T).reshape(NB, L, D)


STOP = "all"
```

```python
import concourse.bass as bass
from concourse import mybir
from contextlib import ExitStack
import math

F32 = mybir.dt.float32
F32R = mybir.dt.float32r
F16 = mybir.dt.float16
I32 = mybir.dt.int32
ALU = mybir.AluOpType
ACT = mybir.ActivationFunctionType
AX = mybir.AxisListType

NB, L, D = 128, 64, 128
T = NB * L
TG = 512
G = T // TG
TPG = TG // 128
NBG = TG // L
H, DH = 16, 8
QG, HQ = 4, 4
NVAR = 3
EPS = 1e-5
TABLES = "natural_log_exp_and_others"
E0, F0 = 8, 512
FC = F0 // 128
WC0 = F0 + FC * D
RC0 = WC0 + FC + 1
KTOP = 2 * T
NT = T // 128
E1, I1 = 32, 64
PAIRS = E1 // 2 + 1
NG1, GS1, TOPG1, TOPK1 = 8, 4, 4, 6
SCALE1 = 2.5
START = 1
SEMAPHORES = """
x_loaded0 x_loaded1 ctx_loaded0 ctx_loaded1 residual_loaded0 residual_loaded1 zeroed mean1 centred1 squared1 var1 log1 rstd1 normed1 mean2 centred2 squared2
var2 log2 rstd2 normed2 hi2 lo2 q_done k_done v_done q_out k_out v_out qk_hi qk_lo qk_stored
stacked0 stacked1 scored maxed shifted exped exped16 halved summed inverted v_scaled v_hi v_lo
exp_lo pv_done o_out projected x1_done x1_stored0 x1_stored1 routed logits_out scores_ready x_loaded
w_loaded0 w_loaded1 w_hi w_lo h_done gelu_done h_hi0 h_hi1 h_lo0 h_lo1 y_done0 y_done1 y_out0 y_out1
added0 added1 gates_loaded0 gates_loaded1 counted totalled stepped chosen gate_masks gates_stored
gate_products d_w_loaded d_c_loaded0 d_c_loaded1 d_mean d_centred d_squared d_var d_log d_rstd
d_normed d_summed d_c_summed d_multiplied d_chain d_exped d_stored d_steps e_w_loaded e_raw_loaded
e_wf_hi e_wf_lo e_ready e_ident e_loaded0 e_loaded1 e_agg e_agg_out e_projected e_x3 e_mean
e_centred e_squared e_var e_log e_rstd e_normed e_hi e_lo e_logits e_exped e_chosen e_turned
e_turned_out e_stored0 e_stored1 e_steps f_g f_u f_silu_done f_gated f_weighted f_hi f_lo f_summed
f_y f_y_out f_c0 f_c1 f_stored0 f_stored1
""".split()


def need(eng, sem, n):
    if isinstance(n, int) and n <= START:
        return
    eng.wait_ge(sem, n)


def group(i):
    return bass.ds(i * TG, TG)


def skewed(eng, lead, lag):
    lead(0, 0)
    with eng.Fori(0, G // 2 - 1) as r:
        lead(2 * r + 1, 1)
        lag(2 * r, 0)
        lead(2 * r + 2, 0)
        lag(2 * r + 1, 1)
    lead(G - 1, 1)
    lag(G - 2, 0)
    lag(G - 1, 1)


def attention(nc, sem, P, W, XH, XL, SC, xT, ctxT, scratch, x1_dram):
    with ExitStack() as ctx:
        def sb(name, shape, dt):
            return ctx.enter_context(nc.sbuf_tensor(name, shape, dt))

        xg = sb("xg", [128, 2, TG], F32)
        cg = sb("cg", [128, 2, TG], F32)
        xc1 = sb("xc1", [128, TG], F32)
        sq1 = sb("sq1", [128, TG], F32)
        xn1 = sb("xn1", [128, TG], F32)
        xc2 = sb("xc2", [128, TG], F32)
        sq2 = sb("sq2", [128, TG], F32)
        xn2 = sb("xn2", [128, TG], F32)
        x1s = sb("x1s", [128, 2, TG], F32)
        qk32 = sb("qk32", [128, 2, TG], F32)
        qk16 = sb("qk16", [128, 2, 2, TG], F16)
        v32 = sb("v32", [128, 2, TPG, 128], F32)
        QM = sb("QM", [96, 2, QG, HQ, TG], F16)
        KS = sb("KS", [96, 2, QG, TG], F16)
        ES = sb("ES", [128, 2, H, L], F32)
        EH = sb("EH", [128, 2, H, L], F16)
        EL = sb("EL", [128, 2, H, L], F16)
        mx = sb("mx", [128, 2, H], F32)
        zh = sb("zh", [128, 2, H, L // 2], F32)
        zz = sb("zz", [128, 2, H], F32)
        rz = sb("rz", [128, 2, H], F32)
        vz = sb("vz", [128, 2, 128], F32)
        VH = sb("VH", [128, 2, H, 128], F16)
        VL = sb("VL", [128, 2, H, 128], F16)
        OS = sb("OS", [128, TPG, 2, L], F32)

        x_loaded = [sem("x_loaded0"), sem("x_loaded1")]
        c_loaded = [sem("ctx_loaded0"), sem("ctx_loaded1")]
        r_loaded = [sem("residual_loaded0"), sem("residual_loaded1")]
        zeroed = sem("zeroed")
        mean1, centred1, squared1 = sem("mean1"), sem("centred1"), sem("squared1")
        var1, log1, rstd1, normed1 = sem("var1"), sem("log1"), sem("rstd1"), sem("normed1")
        mean2, centred2, squared2 = sem("mean2"), sem("centred2"), sem("squared2")
        var2, log2, rstd2, normed2 = sem("var2"), sem("log2"), sem("rstd2"), sem("normed2")
        hi2, lo2 = sem("hi2"), sem("lo2")
        q_done, k_done, v_done = sem("q_done"), sem("k_done"), sem("v_done")
        q_out, k_out, v_out = sem("q_out"), sem("k_out"), sem("v_out")
        qk_hi, qk_lo, qk_stored = sem("qk_hi"), sem("qk_lo"), sem("qk_stored")
        stacked = [sem("stacked0"), sem("stacked1")]
        scored, maxed, shifted = sem("scored"), sem("maxed"), sem("shifted")
        exped, exped16, halved, summed = sem("exped"), sem("exped16"), sem("halved"), sem("summed")
        inverted, v_scaled, v_hi, v_lo = sem("inverted"), sem("v_scaled"), sem("v_hi"), sem("v_lo")
        e_lo, pv_done, o_out = sem("exp_lo"), sem("pv_done"), sem("o_out")
        projected, x1_done = sem("projected"), sem("x1_done")
        x1_stored = [sem("x1_stored0"), sem("x1_stored1")]
        routed, logits_out = sem("routed"), sem("logits_out")
        STACK = 16 * (NVAR * HQ + NVAR)

        S = [P[:, 0:2, :], P[:, 2:4, :]]
        BO, BA, BB, BC = P[:, 4, 0:128], P[:, 5, :], P[:, 6, :], P[:, 7, :]
        block = ctx.enter_context(nc.Block())

        def has(j):
            return not isinstance(j, int) or 0 <= j < G

        def groups(eng, body, ahead=2, before=None):
            body(-2, 0)
            if before:
                before()
            for i in range(-1, 2):
                body(i, i % 2)
            with eng.Fori(1, (G - ahead) // 2) as r:
                body(2 * r, 0)
                body(2 * r + 1, 1)
            for i in range(G - ahead, G + 2):
                body(i, i % 2)

        def back(i, p, t, k):
            return (i, p, t - k) if t >= k else (i - 1, 1 - p, t - k + TPG)

        @block.sync
        def _(sp):
            def load_ctx(j, p):
                need(sp, v_done, START + (j - 1))
                nc.sync.dma_start(cg[:, p, :], ctxT[:, group(j)]).then_inc(c_loaded[p], 16)

            def load_x(j, p):
                need(sp, centred1, START + (j - 1))
                nc.sync.dma_start(xg[:, p, :], xT[:, group(j)]).then_inc(x_loaded[p], 16)

            def load_residual(j, p):
                need(sp, x1_stored[p], START + 8 * (j - p))
                nc.sync.dma_start(x1s[:, p, :], xT[:, group(j)]).then_inc(r_loaded[p], 16)

            def store(j, p):
                sp.wait_ge(centred2, START + j + 1)
                nc.sync.dma_start(x1_dram[:, group(j)], x1s[:, p, :]).then_inc(x1_stored[p], 16)

            def stack(j, p):
                for c in range(2):
                    sp.wait_ge(qk_lo, START + 2 * j + 1 + c)
                    nc.sync.dma_start(scratch[p, c].rearrange("h w t -> w h t"), qk16[:, c]
                                      ).then_inc(qk_stored, 16)
                sp.wait_ge(qk_stored, START + 32 * j + 32)
                for var, half in enumerate((0, 1, 0)):
                    src = scratch[p, 0, half].rearrange("(g h d) t -> h d g t", g=QG, h=HQ)
                    for hh in range(HQ):
                        a = 32 * var + DH * hh
                        nc.sync.dma_start(QM[a:a + DH, p, :, hh, :], src[hh]).then_inc(stacked[p], 16)
                for var, half in enumerate((0, 0, 1)):
                    src = scratch[p, 1, half].rearrange("(g r) t -> r g t", g=QG)
                    nc.sync.dma_start(KS[32 * var:32 * var + 32, p, :, :], src).then_inc(stacked[p], 16)

            def body(i, p):
                if has(i + 3):
                    load_x(i + 3, 1 - p)
                if has(i + 2):
                    load_ctx(i + 2, p)
                if has(i):
                    load_residual(i, p)
                if has(i + 1):
                    if isinstance(i, int) and i == -1:
                        sp.wait_ge(zeroed, START + 3)
                    stack(i + 1, 1 - p)
                if has(i - 1):
                    store(i - 1, 1 - p)

            body(-3, 1)
            groups(sp, body, 4)
            for p in range(2):
                sp.wait_ge(x1_stored[p], START + 8 * G)

        @block.gpsimd
        def _(pool):
            nc.gpsimd.memset(VH[:], 0.0).then_inc(zeroed, 1)
            nc.gpsimd.memset(VL[:], 0.0).then_inc(zeroed, 1)

            def halves(i, t):
                b, n = t % 2, TPG * i + t
                pool.wait_ge(exped, START + n + 1)
                need(pool, summed, START + (n - 1))
                nc.gpsimd.tensor_tensor(zh[:, b], ES[:, b, :, 0:L // 2], ES[:, b, :, L // 2:L],
                                        ALU.add).then_inc(halved, 1)
                pool.wait_ge(exped16, START + n + 1)
                need(pool, pv_done, START + (n - 1))
                nc.gpsimd.tensor_tensor(EL[:, b], ES[:, b], EH[:, b], ALU.subtract).then_inc(e_lo, 1)

            def x_low(j):
                pool.wait_ge(hi2, START + j + 1)
                nc.gpsimd.tensor_tensor(XL[:, group(j)], xn2[:], XH[:, group(j)].bitcast(F32),
                                        ALU.subtract).then_inc(lo2, 1)

            def body(i, p):
                for t in range(TPG):
                    if has(i):
                        halves(i, t)
                    if t == 3 and has(i - 2):
                        x_low(i - 2)

            groups(pool, body)

        def v_slot(V, b, u, a):
            flat = V[64 * u:64 * u + 64, b, 8 * a:8 * a + 8, :].rearrange("p h c -> p (h c)")
            return bass.AP(flat.tensor, flat.offset + 64 * u, [list(flat.ap[0]), [136, 8], [1, DH]])

        def v_from(u, b, a):
            return vz[64 * u:64 * u + 64, b, 64 * a:64 * a + 64].rearrange("p (h d) -> p h d", h=8)

        @block.vector
        def _(dve):
            def centre1(j, p):
                dve.wait_ge(x_loaded[p], START + 8 * (j - p) + 16)
                dve.wait_ge(mean1, START + j + 1)
                need(dve, squared1, START + j)
                nc.vector.tensor_tensor(xc1[:], xg[:, p, :], BA, ALU.subtract).then_inc(centred1, 1)

            def norm1(j):
                dve.wait_ge(rstd1, START + j + 1)
                need(dve, q_done, START + j)
                nc.vector.tensor_tensor(xn1[:], xc1[:], sq1[:], ALU.mult).then_inc(normed1, 1)

            def split_qk(j, c):
                dve.wait_ge(q_out if c == 0 else k_out, START + j + 1)
                need(dve, qk_stored, START + 32 * j)
                nc.vector.tensor_copy(qk16[:, c, 0], qk32[:, c, :]).then_inc(qk_hi, 1)
                dve.wait_ge(qk_hi, START + 2 * j + 1 + c)
                nc.vector.tensor_tensor(qk16[:, c, 1], qk32[:, c, :], qk16[:, c, 0],
                                        ALU.subtract).then_inc(qk_lo, 1)

            def v_evac(j, p):
                dve.wait_ge(v_done, START + j + 1)
                need(dve, v_scaled, START + (TPG * j - TPG))
                nc.vector.tensor_tensor(v32[:, p], BA.rearrange("p (t c) -> p t c", t=TPG),
                                        W["bv0"][:].unsqueeze(1).to_broadcast([128, TPG, 128]),
                                        ALU.add).then_inc(v_out, 1)

            def soft(i, t):
                b, n = t % 2, TPG * i + t
                s = S[b].rearrange("p a (h l) -> p (a h) l", l=L)
                dve.wait_ge(scored, START + n + 1)
                nc.vector.tensor_reduce(mx[:, b], s, AX.X, ALU.max).then_inc(maxed, 1)
                dve.wait_ge(maxed, START + n + 1)
                nc.vector.tensor_tensor(s, s, mx[:, b].unsqueeze(2).to_broadcast([128, H, L]),
                                        ALU.subtract).then_inc(shifted, 1)

            def scale_v(j, p, t):
                b, n = t % 2, TPG * j + t
                dve.wait_ge(halved, START + n + 1)
                nc.vector.tensor_reduce(zz[:, b], zh[:, b], AX.X, ALU.add).then_inc(summed, 1)
                dve.wait_ge(summed, START + n + 1)
                nc.vector.reciprocal(rz[:, b], zz[:, b]).then_inc(inverted, 1)
                dve.wait_ge(inverted, START + n + 1)
                dve.wait_ge(v_out, START + j + 1)
                nc.vector.tensor_tensor(vz[:, b].rearrange("p (h d) -> p h d", h=H),
                                        v32[:, p, t].rearrange("p (h d) -> p h d", h=H),
                                        rz[:, b].unsqueeze(2).to_broadcast([128, H, DH]),
                                        ALU.mult).then_inc(v_scaled, 1)

            def v_low(j, t):
                b, n = t % 2, TPG * j + t
                dve.wait_ge(v_hi, START + 4 * n + 4)
                for u in range(2):
                    for a in range(2):
                        nc.vector.tensor_tensor(v_slot(VL, b, u, a), v_from(u, b, a), v_slot(VH, b, u, a),
                                                ALU.subtract).then_inc(v_lo, 1)

            def x1(j, p):
                dve.wait_ge(projected, START + j + 1)
                dve.wait_ge(r_loaded[p], START + 8 * (j - p) + 16)
                nc.vector.scalar_tensor_tensor(out=x1s[:, p, :], in0=BC, scalar=W["bo0"][:, 0:1],
                                               in1=x1s[:, p, :], op0=ALU.add,
                                               op1=ALU.add).then_inc(x1_done, 1)

            def centre2(j, p):
                dve.wait_ge(mean2, START + j + 1)
                need(dve, squared2, START + j)
                nc.vector.tensor_tensor(xc2[:], x1s[:, p, :], BB, ALU.subtract).then_inc(centred2, 1)

            def norm2(j):
                dve.wait_ge(rstd2, START + j + 1)
                need(dve, routed, START + j)
                need(dve, lo2, START + j)
                nc.vector.tensor_tensor(xn2[:], xc2[:], sq2[:], ALU.mult).then_inc(normed2, 1)

            def split2(j):
                dve.wait_ge(normed2, START + j + 1)
                nc.vector.tensor_copy(XH[:, group(j)], xn2[:]).then_inc(hi2, 1)

            def body(i, p):
                for t in range(TPG):
                    if has(i):
                        soft(i, t)
                    j, pj, tj = back(i, p, t, 1)
                    if t == 1 and has(i + 1):
                        v_evac(i + 1, 1 - p)
                    if t == 3 and has(i + 2):
                        norm1(i + 2)
                    if has(j):
                        scale_v(j, pj, tj)
                    if t == 0 and has(i + 1):
                        split_qk(i + 1, 0)
                        split_qk(i + 1, 1)
                    if t == 1 and has(i - 2):
                        norm2(i - 2)
                    if t == 3 and has(i - 2):
                        split2(i - 2)
                    if t == 3 and has(i - 1):
                        centre2(i - 1, 1 - p)
                    if has(j):
                        v_low(j, tj)
                    if t == 1 and has(i + 2):
                        centre1(i + 2, p)
                    if t == 2 and has(i - 1):
                        x1(i - 1, 1 - p)

            def zero_stack():
                flat = QM[:].rearrange("p a b c d -> p (a b c d)").bitcast(I32)
                nc.vector.memset(flat, 0).then_inc(zeroed, 1)

            groups(dve, body, before=zero_stack)

        @block.scalar
        def _(act):
            def square(j, xc, sq, centred, squared, normed):
                act.wait_ge(centred, START + j + 1)
                need(act, normed, START + j)
                nc.scalar.activation(sq[:], xc[:], ACT.Square).then_inc(squared, 1)

            def rstd(j, bank, sq, var, log, rst):
                act.wait_ge(var, START + j + 1)
                nc.scalar.activation(sq[:], bank, ACT.Ln, bias=W["eps"][:, 0:1]).then_inc(log, 1)
                act.wait_ge(log, START + j + 1)
                nc.scalar.activation(sq[:], sq[:], ACT.Exp, scale=-0.5).then_inc(rst, 1)

            def exps(i, t):
                b, n = t % 2, TPG * i + t
                s = S[b].rearrange("p a (h l) -> p (a h) l", l=L)
                act.wait_ge(shifted, START + n + 1)
                need(act, e_lo, START + (n - 1))
                nc.scalar.activation(ES[:, b], s, ACT.Exp, scale=DH ** -0.5).then_inc(exped, 1)
                need(act, pv_done, START + (n - 1))
                nc.scalar.activation(EH[:, b], s, ACT.Exp, scale=DH ** -0.5).then_inc(exped16, 1)

            def v_high(j, t):
                b, n = t % 2, TPG * j + t
                act.wait_ge(v_scaled, START + n + 1)
                if isinstance(j, int) and j == 0 and t == 0:
                    act.wait_ge(zeroed, START + 3)
                need(act, pv_done, START + (n - 1))
                for u in range(2):
                    for a in range(2):
                        nc.scalar.activation(v_slot(VH, b, u, a), v_from(u, b, a),
                                             ACT.Copy).then_inc(v_hi, 1)

            def o_evac(j, t):
                act.wait_ge(pv_done, START + TPG * j + t + 1)
                need(act, projected, START + j)
                nc.scalar.activation(OS[:, t].rearrange("p a l -> p (a l)"), BO,
                                     ACT.Copy).then_inc(o_out, 1)

            def qk_evac(j, c):
                act.wait_ge(k_done if c else q_done, START + j + 1)
                need(act, qk_lo, START + (2 * j - 1 + c))
                nc.scalar.activation(qk32[:, c, :], BC if c else BA, ACT.Identity,
                                     bias=W["bk0" if c else "bq0"][:, 0:1]).then_inc(k_out if c else q_out, 1)

            def logit_evac(j):
                act.wait_ge(routed, START + j + 1)
                nc.scalar.activation(SC[:, :, bass.ds(j * TPG, TPG)].rearrange("p e t -> p t e"),
                                     BC[:, 0:TPG * E0].rearrange("p (t e) -> p t e", e=E0),
                                     ACT.Copy).then_inc(logits_out, 1)

            first = (xc1, sq1, centred1, squared1, normed1)
            second = (xc2, sq2, centred2, squared2, normed2)
            root1 = (BA, sq1, var1, log1, rstd1)
            root2 = (BB, sq2, var2, log2, rstd2)
            nc.scalar.preload_act_table_set(TABLES)

            def body(i, p):
                for t in range(TPG):
                    if t == 2 and has(i + 2):
                        square(i + 2, *first)
                    if t == 0 and has(i - 2):
                        square(i - 2, *second)
                    if has(i):
                        exps(i, t)
                    j, _, tj = back(i, p, t, 1)
                    if has(j):
                        v_high(j, tj)
                    j, _, tj = back(i, p, t, 2)
                    if has(j):
                        o_evac(j, tj)
                    if t == 2 and has(i + 2):
                        rstd(i + 2, *root1)
                    if t == 3 and has(i + 2):
                        qk_evac(i + 2, 0)
                        qk_evac(i + 2, 1)
                    if t == 0 and has(i - 2):
                        rstd(i - 2, *root2)
                    if t == 1 and has(i - 2):
                        logit_evac(i - 2)

            groups(act, body)

        @block.tensor
        def _(pe):
            def mean_1(j, p):
                pe.wait_ge(x_loaded[p], START + 8 * (j - p) + 16)
                need(pe, v_out, START + j)
                nc.tensor.matmul(BA, W["mean"][:], xg[:, p, :], start=True, stop=True).then_inc(mean1, 1)

            def var_1(j):
                pe.wait_ge(squared1, START + j + 1)
                nc.tensor.matmul(BA, W["mean"][:], sq1[:], start=True, stop=True).then_inc(var1, 1)

            def mean_2(j, p):
                pe.wait_ge(x1_done, START + j + 1)
                need(pe, log2, START + j)
                nc.tensor.matmul(BB, W["mean"][:], x1s[:, p, :], start=True, stop=True).then_inc(mean2, 1)

            def var_2(j):
                pe.wait_ge(squared2, START + j + 1)
                nc.tensor.matmul(BB, W["mean"][:], sq2[:], start=True, stop=True).then_inc(var2, 1)

            def q_proj(j):
                pe.wait_ge(normed1, START + j + 1)
                nc.tensor.matmul(BA, W["wq0"][:], xn1[:], start=True, stop=True).then_inc(q_done, 1)

            def k_proj(j, p):
                pe.wait_ge(c_loaded[p], START + 8 * (j - p) + 16)
                need(pe, x1_done, START + (j - 2))
                nc.tensor.matmul(BC, W["wk0"][:], cg[:, p, :], start=True, stop=True).then_inc(k_done, 1)

            def v_proj(j, p):
                pe.wait_ge(q_out, START + j + 1)
                for t in range(TPG):
                    last = nc.tensor.matmul(BA[:, 128 * t:128 * t + 128], cg[:, p, 128 * t:128 * t + 128],
                                            W["wv0"][:], start=True, stop=True)
                last.then_inc(v_done, 1)

            def score(i, p, t):
                b, n = t % 2, TPG * i + t
                if t == 0:
                    pe.wait_ge(stacked[p], START + STACK // 2 * (i - p) + STACK)
                need(pe, exped16, START + (n - 1))
                for u in range(2):
                    c0 = 128 * t + 64 * u
                    for g in range(QG):
                        last = nc.tensor.matmul(
                            S[b][64 * u:64 * u + 64, g // 2, 256 * (g % 2):256 * (g % 2) + 256],
                            KS[:, p, g, c0:c0 + 64], QM[:, p, g, :, c0:c0 + 64], start=True, stop=True)
                last.then_inc(scored, 1)

            def pv(j, t):
                b, n = t % 2, TPG * j + t
                pe.wait_ge(v_lo, START + 4 * n + 4)
                pe.wait_ge(e_lo, START + n + 1)
                need(pe, o_out, START + n)
                for a in range(2):
                    for h in range(8):
                        for k, (v, e) in enumerate(((VH, EH), (VL, EH), (VH, EL))):
                            last = nc.tensor.matmul(BO[:, 64 * a:64 * a + 64], v[:, b, 8 * a + h, :],
                                                    e[:, b, 8 * a + h, :],
                                                    start=(h == 0 and k == 0), stop=(h == 7 and k == 2))
                last.then_inc(pv_done, 1)

            def project(j):
                pe.wait_ge(o_out, START + TPG * j + TPG)
                pe.wait_ge(k_out, START + (min(j + 3, G) if isinstance(j, int) else j + 3))
                need(pe, logits_out, START + j)
                out = BC.rearrange("p (t u l) -> p u t l", t=TPG, u=2)
                for u in range(2):
                    for a in range(2):
                        last = nc.tensor.matmul(out[:, u], W["wo0"][:, u, a, :], OS[:, :, a, :],
                                                start=(a == 0), stop=(a == 1))
                last.then_inc(projected, 1)

            def logits(j):
                pe.wait_ge(normed2, START + j + 1)
                pe.wait_ge(k_out, START + (min(j + 4, G) if isinstance(j, int) else j + 4))
                for t in range(TPG):
                    last = nc.tensor.matmul(BC[:, E0 * t:E0 * t + E0], xn2[:, 128 * t:128 * t + 128],
                                            W["gw0"][:], start=True, stop=True)
                last.then_inc(routed, 1)

            def body(i, p):
                for t in range(TPG):
                    j, _, tj = back(i, p, t, 2)
                    if has(j):
                        pv(j, tj)
                    if t < TPG - 1 and has(i):
                        score(i, p, t + 1)
                    if t == TPG - 1 and has(i + 1):
                        score(i + 1, 1 - p, 0)
                    if t == 0 and has(i + 1):
                        v_proj(i + 1, 1 - p)
                    if t == 0 and has(i - 2):
                        var_2(i - 2)
                    if t == 1 and has(i + 2):
                        mean_1(i + 2, p)
                    if t == 1 and has(i - 2):
                        logits(i - 2)
                    if t == 2 and has(i - 1):
                        project(i - 1)
                    if t == 2 and has(i + 2):
                        var_1(i + 2)
                    if t == 3 and has(i - 1):
                        mean_2(i - 1, 1 - p)
                    if t == 3 and has(i + 2):
                        q_proj(i + 2)
                        k_proj(i + 2, p)

            groups(pe, body)


def first_ffn(nc, sem, P, W, X, XH, XL, SC, experts, x1_dram, gate_dram):
    with ExitStack() as ctx:
        def sb(name, shape, dt):
            return ctx.enter_context(nc.sbuf_tensor(name, shape, dt))

        WR = sb("WR", [128, 2, RC0], F32)
        WH = sb("WH", [128, 2, WC0], F32R)
        WL = sb("WL", [128, 2, WC0], F32R)
        HS = sb("HS", [128, 2, FC, TG], F32)
        HH = sb("HH", [128, 2, FC, TG], F32R)
        HL = sb("HL", [128, 2, FC, TG], F32R)
        GB = sb("GB", [128, 2, TG], F32)
        YB = sb("YB", [128, 2, TG], F32)
        cmp_ = sb("cmp_", [128, E0 * NT], F32)
        cnt = sb("cnt", [128, 1], F32)
        thr = sb("thr", [128, 1], I32)
        bit = sb("bit", [128, 1], I32)
        trial = sb("trial", [128, 1], I32)
        keep = sb("keep", [128, 1], I32)

        scores_ready = sem("scores_ready")
        x_loaded = sem("x_loaded")
        w_loaded = [sem("w_loaded0"), sem("w_loaded1")]
        w_hi, w_lo = sem("w_hi"), sem("w_lo")
        h_done, gelu_done = sem("h_done"), sem("gelu_done")
        h_hi, h_lo = [sem("h_hi0"), sem("h_hi1")], [sem("h_lo0"), sem("h_lo1")]
        y_done, y_out = [sem("y_done0"), sem("y_done1")], [sem("y_out0"), sem("y_out1")]
        added = [sem("added0"), sem("added1")]
        gates_loaded = [sem("gates_loaded0"), sem("gates_loaded1")]
        counted, totalled, stepped = sem("counted"), sem("totalled"), sem("stepped")
        BT, BY = P[:, 6, 0:1], [P[:, 4, :], P[:, 5, :]]
        NQ = E0 + 1
        HG = G // 2

        flat = SC[:].rearrange("p e j -> p (e j)")
        by_token = SC[:].rearrange("p e j -> p j e")
        peak = cmp_[:, 0:NT]
        with nc.Block() as block:
            @block.vector
            def _(dve):
                nc.vector.tensor_reduce(peak, by_token, AX.X, ALU.max).then_inc(scores_ready, 1)
                dve.wait_ge(scores_ready, START + 1)
                nc.vector.tensor_tensor(SC[:], SC[:], peak.unsqueeze(1).to_broadcast([128, E0, NT]),
                                        ALU.subtract).then_inc(scores_ready, 1)
                dve.wait_ge(scores_ready, START + 3)
                nc.vector.tensor_reduce(peak, by_token, AX.X, ALU.add).then_inc(scores_ready, 1)
                dve.wait_ge(scores_ready, START + 4)
                nc.vector.reciprocal(peak, peak).then_inc(scores_ready, 1)
                dve.wait_ge(scores_ready, START + 5)
                nc.vector.tensor_tensor(SC[:], SC[:], peak.unsqueeze(1).to_broadcast([128, E0, NT]),
                                        ALU.mult).then_inc(scores_ready, 1)
                nc.vector.memset(thr[:], 0).then_inc(scores_ready, 1)
                nc.vector.memset(bit[:], 1 << 29).then_inc(scores_ready, 1)
                nc.vector.memset(trial[:], 1 << 29).then_inc(scores_ready, 1)

            @block.scalar
            def _(act):
                act.wait_ge(scores_ready, START + 2)
                nc.scalar.activation(flat, flat, ACT.Exp).then_inc(scores_ready, 1)

            @block.sync
            def _(sp):
                nc.sync.dma_start(WR[:, 0], experts[0]).then_inc(w_loaded[0], 16)
                nc.sync.dma_start(WR[:, 1], experts[1]).then_inc(w_loaded[1], 16)
                nc.sync.dma_start(X[:], x1_dram).then_inc(x_loaded, 16)

        def w1(pe, q, w, b, u, first=False):
            if not first:
                pe.wait_ge(w_lo, START + q + 1)
            for c in range(FC):
                if not first:
                    pe.wait_ge(gelu_done, START + FC * (G * q + b - 1) + c + 1)
                wc = slice(128 * c, 128 * c + 128)
                for k, (a, x) in enumerate(((WH, XH), (WL, XH), (WH, XL))):
                    last = nc.tensor.matmul(P[:, c, :], a[:, w, wc], x[:, group(b)],
                                            start=(k == 0), stop=(k == 2))
                last.then_inc(h_done, 1)

        def total(pe, n):
            pe.wait_ge(counted, START + n + 1)
            nc.tensor.matmul(BT, W["ones"][:], cnt[:], start=True, stop=True).then_inc(totalled, 1)

        def w2(pe, w, u, n):
            need(pe, y_out[u], START + (n))
            for half in range(2):
                pe.wait_ge(h_lo[u], START + 2 * n + half + 1)
                for c in (2 * half, 2 * half + 1):
                    wc = slice(F0 + 128 * c, F0 + 128 * c + 128)
                    for k, (a, h) in enumerate(((WH, HH), (WL, HH), (WH, HL))):
                        last = nc.tensor.matmul(BY[u], a[:, w, wc], h[:, u, c, :],
                                                start=(c == 0 and k == 0), stop=(c == FC - 1 and k == 2))
            last.then_inc(y_done[u], 1)

        def gelus(act, q, w, b, u, n):
            for c in range(FC):
                act.wait_ge(h_done, START + FC * (G * q + b) + c + 1)
                if c % 2 == 0:
                    need(act, h_lo[u], START + (2 * n))
                nc.scalar.activation(HS[:, u, c, :], P[:, c, :], ACT.Gelu_apprx_tanh,
                                     bias=WR[:, w, WC0 + c:WC0 + c + 1]).then_inc(gelu_done, 1)

        def split(dve, q, b, u, n):
            for half in range(2):
                hs = slice(2 * half, 2 * half + 2)
                dve.wait_ge(gelu_done, START + FC * (G * q + b) + 2 * half + 2)
                need(dve, y_done[u], START + (n))
                nc.vector.tensor_copy(HH[:, u, hs], HS[:, u, hs]).then_inc(h_hi[u], 1)
                dve.wait_ge(h_hi[u], START + 2 * n + half + 1)
                nc.vector.tensor_tensor(HL[:, u, hs], HS[:, u, hs], HH[:, u, hs].bitcast(F32),
                                        ALU.subtract).then_inc(h_lo[u], 1)

        def gated(dve, w, u, n, shared):
            dve.wait_ge(y_done[u], START + n + 1)
            need(dve, added[u], START + (n))
            b2 = WR[:, w, WC0 + FC:WC0 + FC + 1]
            if shared:
                nc.vector.tensor_scalar(YB[:, u, :], BY[u], b2, W["gf"][:, 0:1], ALU.add,
                                        ALU.mult).then_inc(y_out[u], 1)
            else:
                dve.wait_ge(gates_loaded[u], START + 16 * (n + 1) - 16 * HG)
                nc.vector.scalar_tensor_tensor(out=YB[:, u, :], in0=BY[u], scalar=b2, in1=GB[:, u, :],
                                               op0=ALU.add, op1=ALU.mult).then_inc(y_out[u], 1)

        def split_weights(dve, q, w, kq):
            dve.wait_ge(w_loaded[w], START + 16 * kq + 16)
            nc.vector.tensor_copy(WH[:, w], WR[:, w, 0:WC0]).then_inc(w_hi, 1)
            dve.wait_ge(w_hi, START + q + 1)
            nc.vector.tensor_tensor(WL[:, w], WR[:, w, 0:WC0], WH[:, w].bitcast(F32),
                                    ALU.subtract).then_inc(w_lo, 1)

        def add(pool, b, u, n):
            pool.wait_ge(y_out[u], START + n + 1)
            need(pool, added[1 - u], START + (n + u))
            nc.gpsimd.tensor_tensor(X[:, group(b)], X[:, group(b)], YB[:, u, :],
                                    ALU.add).then_inc(added[u], 1)

        def over_groups(eng, q, ahead, here, last_ahead):
            with eng.Fori(0, HG - 1) as r:
                ahead(2 * r + 1, 1, HG * q + r)
                here(2 * r, 0, HG * q + r)
                ahead(2 * r + 2, 0, HG * q + r + 1)
                here(2 * r + 1, 1, HG * q + r)
            ahead(G - 1, 1, HG * q + HG - 1)
            here(G - 2, 0, HG * q + HG - 1)
            last_ahead()
            here(G - 1, 1, HG * q + HG - 1)

        def over_experts(eng, expert):
            with eng.Fori(0, E0 // 2 - 1) as r:
                expert(2 * r + 1, 1, r, False)
                expert(2 * r + 2, 0, r + 1, False)
            expert(E0 - 1, 1, E0 // 2 - 1, False)
            expert(E0, 0, E0 // 2, True)

        with nc.Block() as block:
            @block.tensor
            def _(pe):
                pe.wait_ge(w_lo, START + 1)
                w1(pe, 0, 0, 0, 0, first=True)

                def ahead(b, u, n):
                    w1(pe, 0, 0, b, u)

                def here(b, u, n):
                    total(pe, 2 * b)
                    w2(pe, 0, u, n)
                    total(pe, 2 * b + 1)

                over_groups(pe, 0, ahead, here, lambda: w1(pe, 1, 1, 0, 0))

            @block.scalar
            def _(act):
                with act.Fori(0, HG) as r:
                    gelus(act, 0, 0, 2 * r, 0, r)
                    gelus(act, 0, 0, 2 * r + 1, 1, r)

            @block.gpsimd
            def _(pool):
                pool.wait_ge(x_loaded, START + 16)
                with pool.Fori(0, HG) as r:
                    add(pool, 2 * r, 0, r)
                    add(pool, 2 * r + 1, 1, r)

            @block.vector
            def _(dve):
                split_weights(dve, 0, 0, 0)
                split(dve, 0, 0, 0, 0)

                def count(n):
                    dve.wait_ge(stepped, START + 4 * n)
                    need(dve, totalled, START + (n))
                    nc.vector.tensor_scalar(cmp_[:], flat, trial[:].bitcast(F32), 0.0, ALU.is_ge, ALU.add,
                                            accum_out=cnt[:]).then_inc(counted, 1)

                def step(n):
                    dve.wait_ge(totalled, START + n + 1)
                    nc.vector.scalar_tensor_tensor(out=keep[:], in0=BT, scalar=float(KTOP), in1=bit[:],
                                                   op0=ALU.is_ge, op1=ALU.mult).then_inc(stepped, 1)
                    dve.wait_ge(stepped, START + 4 * n + 1)
                    nc.vector.tensor_scalar(bit[:], bit[:], 1, None,
                                            ALU.logical_shift_right).then_inc(stepped, 1)
                    nc.vector.tensor_tensor(thr[:], thr[:], keep[:], ALU.bitwise_or).then_inc(stepped, 1)
                    dve.wait_ge(stepped, START + 4 * n + 3)
                    nc.vector.tensor_tensor(trial[:], thr[:], bit[:], ALU.bitwise_or).then_inc(stepped, 1)

                count(0)

                def ahead(b, u, n):
                    split(dve, 0, b, u, n)

                def here(b, u, n):
                    step(2 * b)
                    count(2 * b + 1)
                    gated(dve, 0, u, n, True)
                    step(2 * b + 1)
                    if not (isinstance(b, int) and b == G - 1):
                        count(2 * b + 2)

                over_groups(dve, 0, ahead, here, lambda: split_weights(dve, 1, 1, 0))

        above = HS[:, 0, 0, :]
        on = HS[:, 0, 1, :]
        before = HS[:, 0, 2, :]
        rank = HS[:, 0, 3, :]
        gates = HS[:, 1, 0, :]
        gt = HS[:, 1, 1, :]
        left = cnt
        TRI = GB[:, 0, 0:128]
        ident = GB[:, 0, 128:256]
        chosen, made, stored = sem("chosen"), sem("gate_masks"), sem("gates_stored")
        gt_sems = sem("gate_products")
        with nc.Block() as block:
            @block.gpsimd
            def _(pool):
                nc.gpsimd.memset(GB[:, 0, 0:256], 1.0).then_inc(made, 1)
                pool.wait_ge(made, START + 1)
                nc.gpsimd.affine_select(out=TRI, in_=TRI, compare_op=ALU.is_gt, fill=0.0, base=0,
                                        pattern=[[1, 128]], channel_multiplier=-1).then_inc(made, 1)
                nc.gpsimd.affine_select(out=ident, in_=ident, compare_op=ALU.is_equal, fill=0.0, base=0,
                                        pattern=[[1, 128]], channel_multiplier=-1).then_inc(made, 1)

            @block.vector
            def _(dve):
                n = [0]

                def step(instruction):
                    instruction.then_inc(chosen, 1)
                    n[0] += 1
                    dve.wait_ge(chosen, START + n[0])

                t32 = thr[:].bitcast(F32)
                step(nc.vector.tensor_scalar(on, flat, t32, None, ALU.is_equal))
                step(nc.vector.tensor_scalar(above, flat, t32, 0.0, ALU.is_gt, ALU.add, accum_out=cnt[:]))
                dve.wait_ge(gt_sems, START + 1)
                step(nc.vector.tensor_scalar(left[:], BT, -1.0, float(KTOP), ALU.mult, ALU.add))
                dve.wait_ge(gt_sems, START + 2)
                step(nc.vector.tensor_copy(before, P[:, 5, :]))
                step(nc.vector.tensor_tensor_scan(rank, W["one_row"][:], before, 0.0, ALU.mult, ALU.add))
                step(nc.vector.tensor_tensor(rank, rank, before, ALU.subtract))
                step(nc.vector.tensor_tensor(rank, rank, P[:, 4, :], ALU.add))
                step(nc.vector.tensor_scalar(rank, rank, left[:], None, ALU.is_lt))
                step(nc.vector.tensor_tensor(rank, rank, on, ALU.mult))
                step(nc.vector.tensor_tensor(rank, rank, above, ALU.add))
                step(nc.vector.tensor_scalar(gates, flat, W["gf"][:, 0:1], None, ALU.mult))
                nc.vector.tensor_tensor(gates, gates, rank, ALU.mult).then_inc(made, 1)
                dve.wait_ge(gt_sems, START + 3)
                nc.vector.tensor_copy(gt, P[:, 7, :]).then_inc(made, 1)

            @block.tensor
            def _(pe):
                pe.wait_ge(chosen, START + 2)
                nc.tensor.matmul(BT, W["ones"][:], cnt[:], start=True, stop=True).then_inc(gt_sems, 1)
                pe.wait_ge(made, START + 3)
                nc.tensor.matmul(P[:, 4, :], TRI, on, start=True, stop=True)
                nc.tensor.matmul(P[:, 5, :], W["ones"][:], on, start=True, stop=True).then_inc(gt_sems, 1)
                pe.wait_ge(made, START + 4)
                for k in range(4):
                    last = nc.tensor.transpose(P[:, 7, 128 * k:128 * k + 128], gates[:, 128 * k:128 * k + 128],
                                               ident)
                last.then_inc(gt_sems, 1)

            @block.sync
            def _(sp):
                sp.wait_ge(made, START + 5)
                nc.sync.dma_start(gate_dram.rearrange("(k e) (j p) -> (e j) k p", e=2, p=128),
                                  gt.rearrange("r (k p) -> r k p", k=4)).then_inc(stored, 16)
                sp.wait_ge(stored, START + 16)

        with nc.Block() as block:
            @block.sync
            def _(sp):
                def gate_load(q, b, u, n):
                    sp.wait_ge(y_out[u], START + n)
                    nc.sync.dma_start(GB[:, u, :], gate_dram[q - 1, group(b)].partition_broadcast(128)
                                      ).then_inc(gates_loaded[u], 16)

                def expert(q, w, kq, last):
                    with sp.Fori(0, HG) as r:
                        gate_load(q, 2 * r, 0, HG * q + r)
                        gate_load(q, 2 * r + 1, 1, HG * q + r)

                def weights(q, w):
                    sp.wait_ge(y_out[0], START + HG * (q - 1))
                    sp.wait_ge(y_out[1], START + HG * (q - 1))
                    nc.sync.dma_start(WR[:, w], experts[q]).then_inc(w_loaded[w], 16)

                weights(2, 0)
                with sp.Fori(0, E0 // 2 - 1) as r:
                    expert(2 * r + 1, 1, r, False)
                    weights(2 * r + 3, 1)
                    expert(2 * r + 2, 0, r + 1, False)
                    weights(2 * r + 4, 0)
                expert(E0 - 1, 1, 0, False)
                expert(E0, 0, 0, True)

            @block.tensor
            def _(pe):
                def expert(q, w, kq, last):
                    over_groups(pe, q, lambda b, u, n: w1(pe, q, w, b, u), lambda b, u, n: w2(pe, w, u, n),
                                (lambda: None) if last else (lambda: w1(pe, q + 1, 1 - w, 0, 0)))
                over_experts(pe, expert)

            @block.scalar
            def _(act):
                def expert(q, w, kq, last):
                    act.wait_ge(w_loaded[w], START + 16 * kq + 16)
                    with act.Fori(0, HG) as r:
                        gelus(act, q, w, 2 * r, 0, HG * q + r)
                        gelus(act, q, w, 2 * r + 1, 1, HG * q + r)
                over_experts(act, expert)

            @block.gpsimd
            def _(pool):
                def expert(q, w, kq, last):
                    with pool.Fori(0, HG) as r:
                        add(pool, 2 * r, 0, HG * q + r)
                        add(pool, 2 * r + 1, 1, HG * q + r)
                over_experts(pool, expert)

            @block.vector
            def _(dve):
                split(dve, 1, 0, 0, HG)

                def expert(q, w, kq, last):
                    def last_ahead():
                        if not last:
                            split_weights(dve, q + 1, 1 - w, kq + w)
                            split(dve, q + 1, 0, 0, HG * q + HG)
                    over_groups(dve, q, lambda b, u, n: split(dve, q, b, u, n),
                                lambda b, u, n: gated(dve, w, u, n, False), last_ahead)
                over_experts(dve, expert)


def delay_weights(nc, sem, P, W, X, ctxT, ins, we_dram):
    with ExitStack() as ctx:
        def sb(name, shape, dt):
            return ctx.enter_context(nc.sbuf_tensor(name, shape, dt))

        cg = sb("d_cg", [128, 2, TG], F32)
        xc = sb("d_xc", [128, 2, TG], F32)
        sq = sb("d_sq", [128, 2, TG], F32)
        xn = sb("d_xn", [128, TG], F32)
        sx = sb("sx", [128, NB], F32)
        sc = sb("sc", [128, NB], F32)
        wqT = sb("wq1T", [128, 128], F32)
        wkT = sb("wk1T", [128, 128], F32)
        wv = sb("wv1", [128, 128], F32)
        woT = sb("wo1T", [128, 128], F32)
        bqB = sb("bq1B", [128, 128], F32)
        bkB = sb("bk1B", [128, 128], F32)
        bv = sb("bv1", [128, 1], F32)
        bo = sb("bo1", [128, 1], F32)
        qs = sb("qs", [128, 128], F32)
        ks = sb("ks", [128, 128], F32)
        corr = sb("corr", [128, DH], F32)
        peak = sb("d_peak", [128, 1], F32)
        total = sb("d_total", [128, 1], F32)
        WE = sb("WE", [128, 2 * L], F32)

        w_loaded, c_loaded = sem("d_w_loaded"), [sem("d_c_loaded0"), sem("d_c_loaded1")]
        mean, centred, squared, var = sem("d_mean"), sem("d_centred"), sem("d_squared"), sem("d_var")
        log, rstd, normed, summed, c_summed = sem("d_log"), sem("d_rstd"), sem("d_normed"), sem("d_summed"), sem("d_c_summed")
        multiplied, chain, exped, stored = sem("d_multiplied"), sem("d_chain"), sem("d_exped"), sem("d_stored")
        banks_mean = [P[:, 0, :], P[:, 1, :]]
        banks_var = [P[:, 2, :], P[:, 3, :]]
        with nc.Block() as block:
            @block.sync
            def _(sp):
                for dst, name in ((wqT, "wq1T"), (wkT, "wk1T"), (wv, "L1_xattn_Wv"), (woT, "wo1T")):
                    nc.sync.dma_start(dst[:], ins[name]).then_inc(w_loaded, 16)
                for dst, name in ((bqB, "L1_xattn_bq"), (bkB, "L1_xattn_bk")):
                    nc.sync.dma_start(dst[:], ins[name].partition_broadcast(128)).then_inc(w_loaded, 16)
                for dst, name in ((bv, "L1_xattn_bv"), (bo, "L1_xattn_bo")):
                    nc.sync.dma_start(dst[:], ins[name].rearrange("(p a) -> p a", a=1)).then_inc(w_loaded, 16)
                with sp.Fori(0, G // 2) as r:
                    for p in range(2):
                        sp.wait_ge(c_summed, START + 2 * r)
                        nc.sync.dma_start(cg[:, p, :], ctxT[:, group(2 * r + p)]).then_inc(c_loaded[p], 16)
                sp.wait_ge(chain, START + 1)
                nc.sync.dma_start(we_dram, WE[:]).then_inc(stored, 16)
                sp.wait_ge(stored, START + 16)

            @block.tensor
            def _(pe):
                def lead(i, p):
                    need(pe, centred, START + (i - 1))
                    nc.tensor.matmul(banks_mean[p], W["mean"][:], X[:, group(i)],
                                     start=True, stop=True).then_inc(mean, 1)

                def lag(i, p):
                    pe.wait_ge(squared, START + i + 1)
                    nc.tensor.matmul(banks_var[p], W["mean"][:], sq[:, p, :],
                                     start=True, stop=True).then_inc(var, 1)

                skewed(pe, lead, lag)
                pe.wait_ge(w_loaded, START + 128)
                nc.tensor.matmul(P[:, 6, 0:128], wv[:], woT[:], start=True, stop=True).then_inc(multiplied, 1)
                nc.tensor.matmul(P[:, 7, 0:1], woT[:], bv[:], start=True, stop=True).then_inc(multiplied, 1)
                pe.wait_ge(summed, START + G)
                pe.wait_ge(c_summed, START + G)
                nc.tensor.matmul(P[:, 4, 0:128], sx[:], wqT[:], start=True, stop=True).then_inc(multiplied, 1)
                nc.tensor.matmul(P[:, 5, 0:128], sc[:], wkT[:], start=True, stop=True).then_inc(multiplied, 1)

            @block.scalar
            def _(act):
                def lead(i, p):
                    act.wait_ge(centred, START + i + 1)
                    need(act, normed, START + (i - 1))
                    nc.scalar.activation(sq[:, p, :], xc[:, p, :], ACT.Square).then_inc(squared, 1)

                def lag(i, p):
                    act.wait_ge(var, START + i + 1)
                    nc.scalar.activation(sq[:, p, :], banks_var[p], ACT.Ln, bias=W["eps"][:, 0:1]).then_inc(log, 1)
                    act.wait_ge(log, START + i + 1)
                    nc.scalar.activation(sq[:, p, :], sq[:, p, :], ACT.Exp, scale=-0.5).then_inc(rstd, 1)

                nc.scalar.preload_act_table_set(TABLES)
                skewed(act, lead, lag)
                act.wait_ge(exped, START + 1)
                nc.scalar.activation(corr[:], corr[:], ACT.Exp, accum_out=total[:]).then_inc(exped, 1)

            @block.vector
            def _(dve):
                def lead(i, p):
                    dve.wait_ge(mean, START + i + 1)
                    need(dve, normed, START + (i - 1))
                    nc.vector.tensor_tensor(xc[:, p, :], X[:, group(i)], banks_mean[p],
                                            ALU.subtract).then_inc(centred, 1)

                def lag(i, p):
                    dve.wait_ge(rstd, START + i + 1)
                    need(dve, summed, START + (i))
                    nc.vector.tensor_tensor(xn[:], xc[:, p, :], sq[:, p, :], ALU.mult).then_inc(normed, 1)
                    if isinstance(i, int):
                        dve.wait_ge(c_loaded[p], START + 16 * (i // 2 + 1))
                    else:
                        dve.wait_ge(c_loaded[p], START + 8 * (i - p) + 16)
                    nc.vector.tensor_reduce(sc[:, bass.ds(i * NBG, NBG)], cg[:, p, :].rearrange("p (n l) -> p n l", l=L),
                                            AX.X, ALU.add).then_inc(c_summed, 1)
                    dve.wait_ge(normed, START + i + 1)
                    nc.vector.tensor_reduce(sx[:, bass.ds(i * NBG, NBG)], xn[:].rearrange("p (n l) -> p n l", l=L),
                                            AX.X, ALU.add).then_inc(summed, 1)

                skewed(dve, lead, lag)
                n = [0]
                steps = sem("d_steps")

                def step(instruction):
                    instruction.then_inc(steps, 1)
                    n[0] += 1
                    dve.wait_ge(steps, START + n[0])

                step(nc.vector.memset(WE[:], 0.0))
                dve.wait_ge(multiplied, START + 2)
                step(nc.vector.tensor_scalar(W["wvo1"][:], P[:, 6, 0:128], W["gx"][:, 1:2], None, ALU.mult))
                step(nc.vector.tensor_tensor(W["bvo1"][:], P[:, 7, 0:1], bo[:], ALU.add))
                step(nc.vector.tensor_scalar(W["bvo1"][:], W["bvo1"][:], W["gx"][:, 1:2], None, ALU.mult))
                dve.wait_ge(multiplied, START + 4)
                step(nc.vector.scalar_tensor_tensor(out=qs[:], in0=bqB[:], scalar=float(L), in1=P[:, 4, 0:128],
                                                    op0=ALU.mult, op1=ALU.add))
                step(nc.vector.scalar_tensor_tensor(out=ks[:], in0=bkB[:], scalar=float(L), in1=P[:, 5, 0:128],
                                                    op0=ALU.mult, op1=ALU.add))
                step(nc.vector.tensor_tensor(qs[:], qs[:], ks[:], ALU.mult))
                step(nc.vector.tensor_reduce(corr[:], qs[:].rearrange("p (h c) -> p c h", h=H), AX.X, ALU.add))
                step(nc.vector.tensor_scalar(corr[:], corr[:], 1.0 / (H * L), None, ALU.mult))
                step(nc.vector.tensor_reduce(peak[:], corr[:], AX.X, ALU.max))
                nc.vector.tensor_scalar(corr[:], corr[:], peak[:], None, ALU.subtract).then_inc(exped, 1)
                dve.wait_ge(exped, START + 2)
                step(nc.vector.reciprocal(total[:], total[:]))
                step(nc.vector.tensor_scalar(corr[:], corr[:], total[:], None, ALU.mult))
                for d in range(DH):
                    step(nc.vector.tensor_copy(WE[:, L - d:L - d + 1], corr[:, d:d + 1]))
                    if d:
                        step(nc.vector.tensor_copy(WE[:, 2 * L - d:2 * L - d + 1], corr[:, d:d + 1]))
                nc.vector.tensor_copy(peak[:], total[:]).then_inc(chain, 1)


def delays_and_routes(nc, sem, P, W, X, XH, XL, WFH, WFL, ins, we_dram, c_dram):
    with ExitStack() as ctx:
        def sb(name, shape, dt):
            return ctx.enter_context(nc.sbuf_tensor(name, shape, dt))

        WRAW = sb("WRAW", [128, 2, 3 * 128], F32)
        cn = sb("cn", [128, 2, TPG, 128], F32)
        CM = sb("CM", [128, 2, TPG, 128], F32)
        ag = sb("ag", [128, TG], F32)
        xc = sb("e_xc", [128, 2, TG], F32)
        sq = sb("e_sq", [128, 2, TG], F32)
        xn = sb("e_xn", [128, TG], F32)
        ident = sb("ident", [128, 128], F32)
        biasB = sb("biasB", [128, E1], F32)
        gw = sb("gw1", [128, E1], F32)
        seg = [sb("seg_g", [128, TPG, NG1], F32), sb("seg_e", [128, TPG, E1], F32)]
        R = {n: sb("r_" + n, [128, TPG, k], F32) for n, k in {
            "exp": E1, "score": E1, "choice": E1, "group": NG1, "top": 8, "above": E1, "on": E1,
            "rank": E1, "count": 1, "pick_g": NG1, "pick_e": E1, "weight": E1, "sum": 1, "comb": E1, "idle": 1}.items()}
        ct = sb("ct", [E1, 2, TG], F32)

        w_loaded, raw_loaded = sem("e_w_loaded"), sem("e_raw_loaded")
        wf_hi, wf_lo, ready = sem("e_wf_hi"), sem("e_wf_lo"), sem("e_ready")
        with nc.Block() as block:
            @block.sync
            def _(sp):
                nc.sync.dma_start(gw[:], ins["gate1T"]).then_inc(w_loaded, 16)
                nc.sync.dma_start(biasB[:], ins["L1_ffn_e_score_correction_bias"].partition_broadcast(128)
                                  ).then_inc(w_loaded, 16)
                with sp.Fori(0, PAIRS) as r:
                    sp.wait_ge(wf_lo, START + r)
                    nc.sync.dma_start(WRAW[:, 0], ins["experts1"][:, r]).then_inc(raw_loaded, 16)

            @block.vector
            def _(dve):
                nc.vector.memset(CM[:], 0.0).then_inc(ready, 1)
                for s in seg:
                    nc.vector.memset(s[:], 1.0).then_inc(ready, 1)
                dve.wait_ge(ready, START + 3)
                for s in seg:
                    nc.vector.memset(s[:, :, 0:1], 0.0).then_inc(ready, 1)
                with dve.Fori(0, PAIRS) as r:
                    dve.wait_ge(raw_loaded, START + 16 * r + 16)
                    nc.vector.tensor_copy(WFH[:, r], WRAW[:, 0]).then_inc(wf_hi, 1)
                    dve.wait_ge(wf_hi, START + r + 1)
                    nc.vector.tensor_tensor(WFL[:, r], WRAW[:, 0], WFH[:, r].bitcast(F32),
                                            ALU.subtract).then_inc(wf_lo, 1)
                dve.wait_ge(ready, START + 5)

            @block.gpsimd
            def _(pool):
                made = sem("e_ident")
                nc.gpsimd.memset(ident[:], 1.0).then_inc(made, 1)
                pool.wait_ge(made, START + 1)
                nc.gpsimd.affine_select(out=ident[:], in_=ident[:], compare_op=ALU.is_equal, fill=0.0, base=0,
                                        pattern=[[1, 128]], channel_multiplier=-1).then_inc(made, 1)
                pool.wait_ge(made, START + 2)

        loaded = [sem("e_loaded0"), sem("e_loaded1")]
        agg, agg_out, projected, x3 = sem("e_agg"), sem("e_agg_out"), sem("e_projected"), sem("e_x3")
        mean, centred, squared, var = sem("e_mean"), sem("e_centred"), sem("e_squared"), sem("e_var")
        log, rstd, normed, hi, lo = sem("e_log"), sem("e_rstd"), sem("e_normed"), sem("e_hi"), sem("e_lo")
        logits, exped, chosen, turned, turned_out = (sem("e_logits"), sem("e_exped"), sem("e_chosen"),
                                                     sem("e_turned"), sem("e_turned_out"))
        stored = [sem("e_stored0"), sem("e_stored1")]
        steps = sem("e_steps")
        BAG, BPR, BL, BTR = P[:, 0, :], P[:, 1, :], P[:, 6, 0:TPG * E1], P[0:E1, 7, :]
        banks_mean, banks_var = [P[:, 2, :], P[:, 3, :]], [P[:, 4, :], P[:, 5, :]]
        block = ctx.enter_context(nc.Block())

        @block.sync
        def _(sp):
            we = we_dram.rearrange("n j -> (n j)")
            ctx_n = ins["ctxN"].rearrange("(g j p) d -> g p j d", j=TPG, p=128)

            def load(i, p):
                need(sp, agg, START + (i - 1))
                nc.sync.dma_start(cn[:, p], ctx_n[i]).then_inc(loaded[p], 16)
                for u in range(2):
                    at = we[bass.ds((i * NBG + u) * 2 * L + 1, 1)]
                    src = bass.AP(at.tensor, at.offset, [[1, L], [4 * L, TPG], [1, L]])
                    nc.sync.dma_start(CM[64 * u:64 * u + 64, p, :, 64 * u:64 * u + 64], src).then_inc(loaded[p], 16)

            def store(i, p):
                sp.wait_ge(turned_out, START + i + 1)
                nc.sync.dma_start(c_dram[:, group(i)], ct[:, p, :]).then_inc(stored[p], 16)

            load(0, 0)
            load(1, 1)
            with sp.Fori(0, G // 2 - 1) as r:
                for p in range(2):
                    load(2 * r + 2 + p, p)
                    store(2 * r + p, p)
            store(G - 2, 0)
            store(G - 1, 1)
            for p in range(2):
                sp.wait_ge(stored[p], START + 8 * G)

        @block.tensor
        def _(pe):
            def lead(i, p):
                if isinstance(i, int):
                    pe.wait_ge(loaded[p], START + 48 * (i // 2 + 1))
                else:
                    pe.wait_ge(loaded[p], START + 24 * (i - p) + 48)
                need(pe, agg_out, START + (i))
                for t in range(TPG):
                    last = nc.tensor.matmul(BAG[:, 128 * t:128 * t + 128], cn[:, p, t, :], CM[:, p, t, :],
                                            start=True, stop=True)
                last.then_inc(agg, 1)
                pe.wait_ge(agg_out, START + i + 1)
                need(pe, x3, START + (i))
                nc.tensor.matmul(BPR, W["wvo1"][:], ag[:], start=True, stop=True).then_inc(projected, 1)
                pe.wait_ge(x3, START + i + 1)
                need(pe, centred, START + (i - 1))
                nc.tensor.matmul(banks_mean[p], W["mean"][:], X[:, group(i)], start=True, stop=True).then_inc(mean, 1)

            def lag(i, p):
                pe.wait_ge(squared, START + i + 1)
                nc.tensor.matmul(banks_var[p], W["mean"][:], sq[:, p, :], start=True, stop=True).then_inc(var, 1)
                pe.wait_ge(normed, START + i + 1)
                need(pe, exped, START + (i))
                for t in range(TPG):
                    last = nc.tensor.matmul(BL[:, E1 * t:E1 * t + E1], xn[:, 128 * t:128 * t + 128], gw[:],
                                            start=True, stop=True)
                last.then_inc(logits, 1)
                pe.wait_ge(chosen, START + i + 1)
                need(pe, turned_out, START + (i))
                for t in range(TPG):
                    last = nc.tensor.transpose(BTR[:, 128 * t:128 * t + 128], R["comb"][:, t, :], ident[:])
                last.then_inc(turned, 1)

            pe.wait_ge(w_loaded, START + 32)
            skewed(pe, lead, lag)

        @block.scalar
        def _(act):
            def lead(i, p):
                act.wait_ge(agg, START + i + 1)
                need(act, projected, START + (i))
                nc.scalar.activation(ag[:], BAG, ACT.Copy).then_inc(agg_out, 1)
                act.wait_ge(centred, START + i + 1)
                need(act, normed, START + (i - 1))
                nc.scalar.activation(sq[:, p, :], xc[:, p, :], ACT.Square).then_inc(squared, 1)

            def lag(i, p):
                act.wait_ge(var, START + i + 1)
                nc.scalar.activation(sq[:, p, :], banks_var[p], ACT.Ln, bias=W["eps"][:, 0:1]).then_inc(log, 1)
                act.wait_ge(log, START + i + 1)
                nc.scalar.activation(sq[:, p, :], sq[:, p, :], ACT.Exp, scale=-0.5).then_inc(rstd, 1)
                act.wait_ge(logits, START + i + 1)
                need(act, chosen, START + (i))
                nc.scalar.activation(R["exp"][:].rearrange("p t e -> p (t e)"), BL, ACT.Exp,
                                     scale=-1.0).then_inc(exped, 1)
                act.wait_ge(turned, START + i + 1)
                if not isinstance(i, int) or i >= 2:
                    act.wait_ge(stored[p], START + 8 * (i - p))
                nc.scalar.activation(ct[:, p, :], BTR, ACT.Copy).then_inc(turned_out, 1)

            nc.scalar.preload_act_table_set(TABLES)
            skewed(act, lead, lag)

        @block.vector
        def _(dve):
            def lead(i, p):
                dve.wait_ge(projected, START + i + 1)
                nc.vector.scalar_tensor_tensor(out=X[:, group(i)], in0=BPR, scalar=W["bvo1"][:, 0:1],
                                               in1=X[:, group(i)], op0=ALU.add, op1=ALU.add).then_inc(x3, 1)
                dve.wait_ge(mean, START + i + 1)
                need(dve, normed, START + (i - 1))
                nc.vector.tensor_tensor(xc[:, p, :], X[:, group(i)], banks_mean[p], ALU.subtract).then_inc(centred, 1)

            def route(i):
                k = [0]

                def step(instruction):
                    instruction.then_inc(steps, 1)
                    k[0] += 1
                    dve.wait_ge(steps, START + NSTEPS * i + k[0])

                flat = {x: R[x][:].rearrange("p t e -> p (t e)") for x in R}

                def top_mask(v, n, keep, pick, start):
                    above = flat["above"][:, 0:TPG * n].rearrange("p (t e) -> p t e", t=TPG)
                    on = flat["on"][:, 0:TPG * n].rearrange("p (t e) -> p t e", t=TPG)
                    rank = flat["rank"][:, 0:TPG * n].rearrange("p (t e) -> p t e", t=TPG)
                    nc.vector.memset(R["idle"][:], 0.0)
                    for t in range(TPG):
                        ins_ = nc.vector.max(R["top"][:, t, :], v[:, t, :])
                        if t < TPG - 1:
                            ins_.then_inc(steps, 1)
                            k[0] += 1
                    step(ins_)
                    least = R["top"][:, :, keep - 1:keep].to_broadcast([128, TPG, n])
                    nc.vector.tensor_tensor(on, v[:], least, ALU.is_equal).then_inc(steps, 1)
                    k[0] += 1
                    step(nc.vector.tensor_tensor(above, v[:], least, ALU.is_gt))
                    nc.vector.tensor_reduce(R["count"][:, :, 0], above, AX.X, ALU.add).then_inc(steps, 1)
                    k[0] += 1
                    step(nc.vector.tensor_tensor_scan(flat["rank"][:, 0:TPG * n],
                                                      start[:].rearrange("p t e -> p (t e)"),
                                                      flat["on"][:, 0:TPG * n], 0.0, ALU.mult, ALU.add))
                    step(nc.vector.tensor_tensor(rank, rank, R["count"][:].to_broadcast([128, TPG, n]), ALU.add))
                    step(nc.vector.scalar_tensor_tensor(out=flat["rank"][:, 0:TPG * n], in0=flat["rank"][:, 0:TPG * n],
                                                        scalar=float(keep), in1=flat["on"][:, 0:TPG * n],
                                                        op0=ALU.is_le, op1=ALU.mult))
                    step(nc.vector.tensor_tensor(pick[:], rank, above, ALU.add))

                dve.wait_ge(exped, START + i + 1)
                step(nc.vector.tensor_scalar(flat["score"], flat["exp"], 1.0, None, ALU.add))
                step(nc.vector.reciprocal(flat["score"], flat["score"]))
                step(nc.vector.tensor_tensor(R["choice"][:], R["score"][:],
                                             biasB[:].unsqueeze(1).to_broadcast([128, TPG, E1]), ALU.add))
                step(nc.vector.tensor_reduce(flat["group"], flat["choice"].rearrange("p (g s) -> p g s", s=GS1),
                                             AX.X, ALU.max))
                top_mask(R["group"], NG1, TOPG1, R["pick_g"], seg[0])
                step(nc.vector.tensor_tensor(flat["choice"].rearrange("p (g s) -> p g s", s=GS1),
                                             flat["choice"].rearrange("p (g s) -> p g s", s=GS1),
                                             flat["pick_g"].unsqueeze(2).to_broadcast([128, TPG * NG1, GS1]),
                                             ALU.mult))
                top_mask(R["choice"], E1, TOPK1, R["pick_e"], seg[1])
                step(nc.vector.tensor_tensor(R["weight"][:], R["score"][:], R["pick_e"][:], ALU.mult))
                step(nc.vector.tensor_reduce(R["sum"][:, :, 0], R["weight"][:], AX.X, ALU.add))
                step(nc.vector.tensor_scalar(flat["sum"], flat["sum"], 1e-20, None, ALU.add))
                step(nc.vector.reciprocal(flat["sum"], flat["sum"]))
                step(nc.vector.tensor_scalar(flat["sum"], flat["sum"], SCALE1, None, ALU.mult))
                need(dve, turned, START + (i))
                nc.vector.tensor_tensor(R["comb"][:], R["weight"][:], R["sum"][:].to_broadcast([128, TPG, E1]),
                                        ALU.mult).then_inc(chosen, 1)
                assert k[0] == NSTEPS, k[0]

            NSTEPS = 32

            def lag(i, p):
                dve.wait_ge(rstd, START + i + 1)
                need(dve, logits, START + (i))
                need(dve, lo, START + (i))
                nc.vector.tensor_tensor(xn[:], xc[:, p, :], sq[:, p, :], ALU.mult).then_inc(normed, 1)
                dve.wait_ge(normed, START + i + 1)
                nc.vector.tensor_copy(XH[:, group(i)], xn[:]).then_inc(hi, 1)
                dve.wait_ge(hi, START + i + 1)
                nc.vector.tensor_tensor(XL[:, group(i)], xn[:], XH[:, group(i)].bitcast(F32),
                                        ALU.subtract).then_inc(lo, 1)
                route(i)

            skewed(dve, lead, lag)


def second_ffn(nc, sem, P, W, X, XH, XL, WFH, WFL, c_dram, out):
    with ExitStack() as ctx:
        def sb(name, shape, dt):
            return ctx.enter_context(nc.sbuf_tensor(name, shape, dt))

        CQ = 4
        NC = (PAIRS - 1) // CQ
        CB = sb("CB", [128, 2, CQ, TG], F32)
        sg = sb("f_silu", [128, 2, TG], F32)
        au = sb("f_au", [128, 2, TG], F32)
        ac = sb("f_ac", [128, 2, TG], F32)
        hh = sb("f_hh", [128, 2, TG], F32R)
        hl = sb("f_hl", [128, 2, TG], F32R)
        o32 = sb("f_out", [128, 2, TG], F32)
        g_done, u_done, silu_done, gated = sem("f_g"), sem("f_u"), sem("f_silu_done"), sem("f_gated")
        weighted, hi, lo, summed = sem("f_weighted"), sem("f_hi"), sem("f_lo"), sem("f_summed")
        y_done, y_out = sem("f_y"), sem("f_y_out")
        c_loaded, stored = [sem("f_c0"), sem("f_c1")], [sem("f_stored0"), sem("f_stored1")]
        BG, BU, BY = [P[:, 0, :], P[:, 1, :]], [P[:, 2, :], P[:, 3, :]], [P[:, 4, :], P[:, 5, :]]
        N2 = 2 * PAIRS
        block = ctx.enter_context(nc.Block())

        def pair(n):
            return n // PAIRS % 2, n % PAIRS

        @block.sync
        def _(sp):
            c_view = c_dram.rearrange("(k e) t -> k e t", e=2)

            def load(r, b, j):
                q = (NC * b + j) % 2
                n = NC * b + j - 2
                done = (n // NC) * (PAIRS - 1) + (n % NC + 1) * CQ
                if done > 0 or not isinstance(r, int):
                    need(sp, weighted, START + (2 * (PAIRS - 1) * r + done))
                for e in range(2):
                    src = c_view[CQ * j:CQ * j + CQ, e, group(2 * r + b)]
                    nc.sync.dma_start(CB[64 * e:64 * e + 64, q], src.partition_broadcast(64)
                                      ).then_inc(c_loaded[q], 16)

            def store(i, b, r):
                sp.wait_ge(y_out, START + i + 1)
                nc.sync.dma_start(out[:, group(i)], o32[:, b, :]).then_inc(stored[b], 16)

            def body(r):
                for b in range(2):
                    for j in range(NC):
                        load(r, b, j)
                    if b == 1:
                        store(2 * r, 0, r)
                    elif not isinstance(r, int):
                        store(2 * r - 1, 1, r)

            body(0)
            with sp.Fori(1, G // 2) as r:
                body(r)
            store(G - 1, 1, 0)
            for b in range(2):
                sp.wait_ge(stored[b], START + 8 * G)

        @block.tensor
        def _(pe):
            def up(r, n):
                b, k = pair(n)
                s = n % 2
                g = group(2 * r + n // PAIRS)
                for bank, col, done, freed in ((BG[s], 0, g_done, silu_done), (BU[s], 128, u_done, gated)):
                    if not (isinstance(r, int) and n < 2 and r == 0):
                        need(pe, freed, START + (N2 * r + n - 1))
                    for m, (w, x) in enumerate(((WFH, XH), (WFL, XH), (WFH, XL))):
                        last = nc.tensor.matmul(bank, w[:, k, col:col + 128], x[:, g],
                                                start=(m == 0), stop=(m == 2))
                    last.then_inc(done, 1)

            def down(r, n):
                b, k = pair(n)
                s = n % 2
                if k == 0:
                    need(pe, y_out, START + (2 * r + b - 1)) if not isinstance(r, int) else None
                pe.wait_ge(lo, START + N2 * r + n + 1)
                for m, (w, h) in enumerate(((WFH, hh), (WFL, hh), (WFH, hl))):
                    last = nc.tensor.matmul(BY[b], w[:, k, 256:384], h[:, s, :],
                                            start=(k == 0 and m == 0), stop=(k == PAIRS - 1 and m == 2))
                last.then_inc(summed, 1)

            def step(r, last):
                for n in range(N2):
                    if n + 2 < N2 or not last:
                        up(r, n + 2)
                    down(r, n)

            up(0, 0)
            up(0, 1)
            step(0, False)
            with pe.Fori(1, G // 2 - 1) as r:
                step(r, False)
            step(G // 2 - 1, True)

        @block.scalar
        def _(act):
            def body(r):
                for n in range(N2):
                    s = n % 2
                    act.wait_ge(g_done, START + N2 * r + n + 1)
                    if not (isinstance(r, int) and n < 2):
                        need(act, gated, START + (N2 * r + n - 1))
                    nc.scalar.activation(sg[:, s, :], BG[s], ACT.Silu).then_inc(silu_done, 1)

            body(0)
            with act.Fori(1, G // 2) as r:
                body(r)

        @block.gpsimd
        def _(pool):
            def body(r):
                m = 0
                for n in range(N2):
                    b, k = pair(n)
                    s = n % 2
                    if k == PAIRS - 1:
                        continue
                    j = NC * b + k // CQ
                    if k % CQ == 0:
                        pool.wait_ge(c_loaded[j % 2], START + 32 * (NC * r + j // 2 + 1))
                    pool.wait_ge(gated, START + N2 * r + n + 1)
                    if not (isinstance(r, int) and n < 2):
                        need(pool, lo, START + (N2 * r + n - 1))
                    nc.gpsimd.tensor_tensor(ac[:, s, :], au[:, s, :], CB[:, j % 2, k % CQ, :],
                                            ALU.mult).then_inc(weighted, 1)

            body(0)
            with pool.Fori(1, G // 2) as r:
                body(r)

        @block.vector
        def _(dve):
            def gate(r, n):
                s = n % 2
                dve.wait_ge(silu_done, START + N2 * r + n + 1)
                dve.wait_ge(u_done, START + N2 * r + n + 1)
                if not (isinstance(r, int) and n < 2):
                    need(dve, lo, START + (N2 * r + n - 1))
                nc.vector.tensor_tensor(au[:, s, :], sg[:, s, :], BU[s], ALU.mult).then_inc(gated, 1)

            def split(r, n):
                b, k = pair(n)
                s = n % 2
                shared = k == PAIRS - 1
                src = au if shared else ac
                if shared:
                    dve.wait_ge(gated, START + N2 * r + n + 1)
                else:
                    dve.wait_ge(weighted, START + 2 * (PAIRS - 1) * r + b * (PAIRS - 1) + k + 1)
                if not (isinstance(r, int) and n < 2):
                    need(dve, summed, START + (N2 * r + n - 1))
                nc.vector.tensor_copy(hh[:, s, :], src[:, s, :]).then_inc(hi, 1)
                dve.wait_ge(hi, START + N2 * r + n + 1)
                nc.vector.tensor_tensor(hl[:, s, :], src[:, s, :], hh[:, s, :].bitcast(F32),
                                        ALU.subtract).then_inc(lo, 1)

            def result(r, b):
                i = 2 * r + b
                dve.wait_ge(summed, START + N2 * r + PAIRS * (b + 1))
                if not isinstance(r, int):
                    dve.wait_ge(stored[b], START + 16 * r)
                nc.vector.scalar_tensor_tensor(out=o32[:, b, :], in0=BY[b], scalar=W["gf"][:, 1:2],
                                               in1=X[:, group(i)], op0=ALU.mult, op1=ALU.add).then_inc(y_out, 1)

            def body(r):
                for n in range(N2):
                    gate(r, n)
                    if n:
                        split(r, n - 1)
                    if n == PAIRS + 3:
                        result(r, 0)
                split(r, N2 - 1)
                result(r, 1)

            body(0)
            with dve.Fori(1, G // 2) as r:
                body(r)


def shared_constants(nc, semaphores, W, ins):
    def start(eng, k):
        for name in SEMAPHORES[k::5]:
            eng.sem_inc(semaphores[name], START)

    with ExitStack() as ctx:
        loaded = ctx.enter_context(nc.semaphore("const_loaded"))
        done = ctx.enter_context(nc.semaphore("const_done"))
        block = ctx.enter_context(nc.Block())
        dmas = []

        @block.sync
        def _(sp):
            def load(dst, src):
                nc.sync.dma_start(dst, src).then_inc(loaded, 16)
                dmas.append(1)

            def column(v):
                return v.rearrange("(p a) -> p a", a=1)

            load(W["wq0"][:], ins["L0_xattn_Wq"])
            load(W["wk0"][:], ins["L0_xattn_Wk"])
            load(W["wv0"][:], ins["L0_xattn_Wv"])
            sp.wait_ge(done, 1)
            for u in range(2):
                load(W["wo0"][64 * u:64 * u + 64, u], ins["L0_xattn_Wo"].rearrange("(a r) d -> r a d", a=2))
            load(W["gw0"][:], ins["gate0T"])
            load(W["bq0"][:], column(ins["L0_xattn_bq"]))
            load(W["bk0"][:], column(ins["L0_xattn_bk"]))
            load(W["bo0"][:], column(ins["L0_xattn_bo"]))
            load(W["bv0"][:], ins["L0_xattn_bv"].partition_broadcast(128))
            load(W["gx"][:], ins["g_xattn"].partition_broadcast(128))
            load(W["gf"][:], ins["g_ffn"].partition_broadcast(128))
            start(sp, 2)

        n_loaded = 16 * len(dmas)

        @block.vector
        def _(dve):
            start(dve, 0)
            nc.vector.memset(W["wo0"][:], 0.0).then_inc(done, 1)
            nc.vector.memset(W["mean"][:], 1.0 / D).then_inc(done, 1)
            nc.vector.memset(W["ones"][:], 1.0).then_inc(done, 1)
            nc.vector.memset(W["one_row"][:], 1.0).then_inc(done, 1)
            nc.vector.memset(W["eps"][:], EPS).then_inc(done, 1)
            dve.wait_ge(done, 7)
            dve.wait_ge(loaded, n_loaded)
            nc.vector.tensor_scalar(W["wo0"][:].rearrange("p u a d -> p (u a d)"),
                                    W["wo0"][:].rearrange("p u a d -> p (u a d)"),
                                    W["gx"][:, 0:1], None, ALU.mult).then_inc(done, 1)
            nc.vector.tensor_scalar(W["bo0"][:], W["bo0"][:], W["gx"][:, 0:1], None, ALU.mult).then_inc(done, 1)

        @block.tensor
        def _(pe):
            start(pe, 3)

        @block.gpsimd
        def _(pool):
            start(pool, 4)

        @block.scalar
        def _(act):
            start(act, 1)
            act.wait_ge(loaded, n_loaded)
            nc.scalar.activation(W["gx"][:], W["gx"][:], ACT.Tanh).then_inc(done, 1)
            nc.scalar.activation(W["gf"][:], W["gf"][:], ACT.Tanh).then_inc(done, 1)


def program(nc, ins, out, stop="all"):
    with ExitStack() as ctx:
        ctx.enter_context(nc.allow_low_precision(reason="operands split in halves"))
        semaphores = {name: ctx.enter_context(nc.semaphore(name)) for name in SEMAPHORES}
        sem = semaphores.__getitem__

        def sb(name, shape, dt):
            return ctx.enter_context(nc.sbuf_tensor(name, shape, dt))

        P = ctx.enter_context(nc.psum_tensor("P", [128, 8, TG], F32))
        W = {n: sb("w_" + n, s, F32) for n, s in {
            "wq0": [128, 128], "wk0": [128, 128], "wv0": [128, 128], "wo0": [128, 2, 2, 128],
            "gw0": [128, E0], "bq0": [128, 1], "bk0": [128, 1], "bo0": [128, 1], "bv0": [128, 128],
            "gx": [128, 2], "gf": [128, 2], "mean": [128, 128], "ones": [128, 128], "eps": [128, 1],
            "one_row": [128, TG], "wvo1": [128, 128], "bvo1": [128, 1],
        }.items()}
        XH = sb("XH", [128, T], F32R)
        XL = sb("XL", [128, T], F32R)
        SC = sb("SC", [128, E0, NT], F32)
        scratch = nc.dram_tensor("qk_scratch", [2, 2, 2, 128, TG], F16)
        x1_dram = nc.dram_tensor("x1_dram", [128, T], F32)
        shared_constants(nc, semaphores, W, ins)
        attention(nc, sem, P, W, XH, XL, SC, ins["xT"], ins["ctxT"], scratch.ap(), x1_dram.ap())
        if stop == "A":
            with nc.Block() as block:
                s = ctx.enter_context(nc.semaphore("dbg"))
                @block.sync
                def _(sp):
                    nc.sync.dma_start(out, x1_dram.ap()).then_inc(s, 16)
                    dbg = nc.dram_tensor("dbg_sc", [128, E0, NT], F32)
                    nc.sync.dma_start(dbg.ap(), SC[:]).then_inc(s, 16)
                    sp.wait_ge(s, 32)
            return
        gate_dram = nc.dram_tensor("gate_dram", [E0, T], F32)
        X = sb("X", [128, T], F32)
        first_ffn(nc, sem, P, W, X, XH, XL, SC, ins["experts0"], x1_dram.ap(), gate_dram.ap())
        if stop == "C":
            with nc.Block() as block:
                s = ctx.enter_context(nc.semaphore("dbg"))
                @block.sync
                def _(sp):
                    nc.sync.dma_start(out, X[:]).then_inc(s, 16)
                    sp.wait_ge(s, 16)
            return
        we_dram = nc.dram_tensor("we_dram", [NB, 2 * L], F32)
        c_dram = nc.dram_tensor("c_dram", [E1, T], F32)
        delay_weights(nc, sem, P, W, X, ins["ctxT"], ins, we_dram.ap())
        WFH = sb("WFH", [128, PAIRS, 3 * 128], F32R)
        WFL = sb("WFL", [128, PAIRS, 3 * 128], F32R)
        delays_and_routes(nc, sem, P, W, X, XH, XL, WFH, WFL, ins, we_dram.ap(), c_dram.ap())
        if stop == "E":
            with nc.Block() as block:
                s = ctx.enter_context(nc.semaphore("dbg"))
                @block.sync
                def _(sp):
                    nc.sync.dma_start(out, X[:]).then_inc(s, 16)
                    dbg = nc.dram_tensor("dbg_a", [E1, T], F32)
                    nc.sync.dma_start(dbg.ap(), c_dram.ap()).then_inc(s, 16)
                    sp.wait_ge(s, 32)
            return
        second_ffn(nc, sem, P, W, X, XH, XL, WFH, WFL, c_dram.ap(), out)


def kernel(**inputs):
    import numpy as np
    import concourse.bacc as bacc
    from concourse.bass_utils import run_bass_kernel_spmd as run

    a = {k: np.asarray(v) for k, v in inputs.items()}
    laid = {k: a[k] for k in ("g_xattn", "g_ffn", "L0_xattn_Wq", "L0_xattn_bq", "L0_xattn_Wk", "L0_xattn_bk",
                              "L0_xattn_Wv", "L0_xattn_bv", "L0_xattn_Wo", "L0_xattn_bo")}
    laid["xT"] = a["x"].reshape(T, D).T
    laid["ctxT"] = a["ctx_1024"].reshape(T, D).T
    laid["gate0T"] = a["L0_ffn_gate_weight"].T
    laid["ctxN"] = a["ctx_1024"][:, ::-1, :].reshape(T, D)
    laid["wq1T"] = a["L1_xattn_Wq"].T
    laid["wk1T"] = a["L1_xattn_Wk"].T
    laid["wo1T"] = a["L1_xattn_Wo"].T
    laid["gate1T"] = a["L1_ffn_gate_weight"].T
    laid.update({k: a[k] for k in ("L1_xattn_Wv", "L1_xattn_bq", "L1_xattn_bk", "L1_xattn_bv", "L1_xattn_bo",
                                   "L1_ffn_e_score_correction_bias")})
    gu = np.concatenate([a["L1_ffn_experts_gate_up"].reshape(E1 // 2, 2, 2, I1, D).transpose(0, 2, 1, 3, 4),
                         np.stack([a["L1_ffn_shared_gate_w"], a["L1_ffn_shared_up_w"]]).reshape(1, 2, 2, I1, D)])
    down = np.concatenate([a["L1_ffn_experts_down"].transpose(0, 2, 1).reshape(E1 // 2, 2 * I1, D),
                           a["L1_ffn_shared_down_w"].T[None]])
    laid["experts1"] = np.concatenate([gu.reshape(PAIRS, 4 * I1, D).transpose(2, 0, 1), down.transpose(1, 0, 2)],
                                      axis=2)

    def rows(w1, b1, w2, b2):
        e = w1.shape[0]
        w2c = w2.reshape(e, FC, 128, D).transpose(0, 2, 1, 3).reshape(e, 128, FC * D)
        b1c = b1.reshape(e, FC, 128).transpose(0, 2, 1)
        return np.concatenate([w1, w2c, b1c, b2[:, :, None]], axis=2)

    laid["experts0"] = np.concatenate([
        rows(a["L0_ffn_Ws1"][None], a["L0_ffn_bs1"][None], a["L0_ffn_Ws2"][None], a["L0_ffn_bs2"][None]),
        rows(a["L0_ffn_W1"], a["L0_ffn_b1"], a["L0_ffn_W2"], a["L0_ffn_b2"])])
    nc = bacc.Bacc("TRN2", target_bir_lowering=False, num_devices=1)
    arrays, ins = {}, {}
    for name, v in laid.items():
        v = np.ascontiguousarray(v)
        arrays[f"in_{name}"] = v
        ins[name] = nc.dram_tensor(f"in_{name}", v.shape, mybir.dt.from_np(v.dtype), kind="ExternalInput").ap()
    out = nc.dram_tensor("out_T", [D, T], F32, kind="ExternalOutput")
    program(nc, ins, out.ap(), STOP)
    r = run(nc, [arrays], core_ids=[0])
    return np.ascontiguousarray(r.results[0]["out_T"].T).reshape(NB, L, D)


STOP = "all"
```

```python
import concourse.bass as bass
from concourse import mybir
from contextlib import ExitStack
import math

F32 = mybir.dt.float32
F32R = mybir.dt.float32r
F16 = mybir.dt.float16
I32 = mybir.dt.int32
ALU = mybir.AluOpType
ACT = mybir.ActivationFunctionType
AX = mybir.AxisListType

NB, L, D = 128, 64, 128
T = NB * L
TG = 512
G = T // TG
TPG = TG // 128
NBG = TG // L
H, DH = 16, 8
QG, HQ = 4, 4
NVAR = 3
EPS = 1e-5
TABLES = "natural_log_exp_and_others"
E0, F0 = 8, 512
FC = F0 // 128
WC0 = F0 + FC * D
RC0 = WC0 + FC + 1
KTOP = 2 * T
NT = T // 128
E1, I1 = 32, 64
PAIRS = E1 // 2 + 1
NG1, GS1, TOPG1, TOPK1 = 8, 4, 4, 6
SCALE1 = 2.5
START = 1
SEMAPHORES = """
x_loaded0 x_loaded1 ctx_loaded0 ctx_loaded1 residual_loaded0 residual_loaded1 zeroed mean1 centred1
squared1 var1 log1 rstd1 normed1 mean2 centred2 squared2 var2 log2 rstd2 normed2 hi2 lo2 q_done
k_done v_done q_out k_out v_out qk_hi qk_lo qk_stored stacked0 stacked1 scored maxed shifted exped
exped16 halved summed inverted v_scaled v_hi v_lo exp_lo pv_done o_out projected x1_done x1_stored0
x1_stored1 routed logits_out scores_ready x_loaded w_loaded0 w_loaded1 w0_hi w0_lo w_hi w_lo h_done
gelu_done h_hi0 act_hi h_hi1 h_lo0 h_lo1 y_done0 y_done1 y_out0 y_out1 added0 added1 gates_loaded0
gates_loaded1 counted totalled stepped chosen gate_masks gates_stored gate_products d_w_loaded
d_c_loaded0 d_c_loaded1 d_centred d_squared d_var d_log d_rstd d_normed d_summed d_c_summed
d_multiplied d_chain d_exped d_stored d_steps e_w_loaded raw_loaded0 raw_loaded1 wf_hi wf_lo e_ready
e_ident e_loaded0 e_loaded1 e_agg e_agg_out e_projected e_x3 e_centred e_squared e_var e_log e_rstd
e_normed e_hi e_lo e_logits e_exped e_chosen e_turned e_turned_out e_stored0 e_stored1 e_steps f_g
f_u f_silu_done f_gated f_weighted f_hi f_lo f_summed f_y f_y_out f_c0 f_c1 f_stored0 f_stored1
""".split()


def need(eng, sem, n):
    if isinstance(n, int) and n <= START:
        return
    eng.wait_ge(sem, n)


def upto(n):
    return min(n, G) if isinstance(n, int) else n


def group(i):
    return bass.ds(i * TG, TG)


def has(j):
    return not isinstance(j, int) or 0 <= j < G


def attention(nc, sem, P, W, XH, XL, SC, xT, ctxT, scratch, x1_dram):
    with ExitStack() as ctx:
        def sb(name, shape, dt):
            return ctx.enter_context(nc.sbuf_tensor(name, shape, dt))

        xg = sb("xg", [128, 2, TG], F32)
        cg = sb("cg", [128, 2, TG], F32)
        xc1 = sb("xc1", [128, TG], F32)
        sq1 = sb("sq1", [128, TG], F32)
        xn1 = sb("xn1", [128, TG], F32)
        xc2 = sb("xc2", [128, TG], F32)
        sq2 = sb("sq2", [128, TG], F32)
        xn2 = sb("xn2", [128, TG], F32)
        x1s = sb("x1s", [128, 2, TG], F32)
        qk32 = sb("qk32", [128, 2, TG], F32)
        qk16 = sb("qk16", [128, 2, 2, TG], F16)
        v32 = sb("v32", [128, 2, TPG, 128], F32)
        QM = sb("QM", [96, 2, QG, HQ, TG], F16)
        KS = sb("KS", [96, 2, QG, TG], F16)
        ES = sb("ES", [128, 2, H, L], F32)
        EH = sb("EH", [128, 2, H, L], F16)
        EL = sb("EL", [128, 2, H, L], F16)
        mx = sb("mx", [128, 2, H], F32)
        zh = sb("zh", [128, 2, H, L // 2], F32)
        zz = sb("zz", [128, 2, H], F32)
        rz = sb("rz", [128, 2, H], F32)
        vz = sb("vz", [128, 2, 128], F32)
        VH = sb("VH", [128, 2, H, 128], F16)
        VL = sb("VL", [128, 2, H, 128], F16)
        OS = sb("OS", [128, TPG, 2, L], F32)

        x_loaded = [sem("x_loaded0"), sem("x_loaded1")]
        c_loaded = [sem("ctx_loaded0"), sem("ctx_loaded1")]
        r_loaded = [sem("residual_loaded0"), sem("residual_loaded1")]
        zeroed = sem("zeroed")
        mean1, centred1, squared1 = sem("mean1"), sem("centred1"), sem("squared1")
        var1, log1, rstd1, normed1 = sem("var1"), sem("log1"), sem("rstd1"), sem("normed1")
        mean2, centred2, squared2 = sem("mean2"), sem("centred2"), sem("squared2")
        var2, log2, rstd2, normed2 = sem("var2"), sem("log2"), sem("rstd2"), sem("normed2")
        hi2, lo2 = sem("hi2"), sem("lo2")
        q_done, k_done, v_done = sem("q_done"), sem("k_done"), sem("v_done")
        q_out, k_out, v_out = sem("q_out"), sem("k_out"), sem("v_out")
        qk_hi, qk_lo, qk_stored = sem("qk_hi"), sem("qk_lo"), sem("qk_stored")
        stacked = [sem("stacked0"), sem("stacked1")]
        scored, maxed, shifted = sem("scored"), sem("maxed"), sem("shifted")
        exped, exped16, halved, summed = sem("exped"), sem("exped16"), sem("halved"), sem("summed")
        inverted, v_scaled, v_hi, v_lo = sem("inverted"), sem("v_scaled"), sem("v_hi"), sem("v_lo")
        e_lo, pv_done, o_out = sem("exp_lo"), sem("pv_done"), sem("o_out")
        projected, x1_done = sem("projected"), sem("x1_done")
        x1_stored = [sem("x1_stored0"), sem("x1_stored1")]
        routed, logits_out = sem("routed"), sem("logits_out")
        STACK = 16 * (NVAR * HQ + NVAR)

        S = [P[:, 0:2, :], P[:, 2:4, :]]
        BO, BA, BB, BC = P[:, 4, 0:128], P[:, 5, :], P[:, 6, :], P[:, 7, :]
        block = ctx.enter_context(nc.Block())

        def groups(eng, body, ahead=2):
            for i in range(-2, 2):
                body(i, i % 2)
            with eng.Fori(1, (G - ahead) // 2) as r:
                body(2 * r, 0)
                body(2 * r + 1, 1)
            for i in range(G - ahead, G + 2):
                body(i, i % 2)

        def back(i, p, t, k):
            return (i, p, t - k) if t >= k else (i - 1, 1 - p, t - k + TPG)

        @block.sync
        def _(sp):
            def load_ctx(j, p):
                need(sp, v_done, START + j - 1)
                nc.sync.dma_start(cg[:, p, :], ctxT[:, group(j)]).then_inc(c_loaded[p], 16)

            def load_x(j, p):
                need(sp, centred1, START + j - 1)
                nc.sync.dma_start(xg[:, p, :], xT[:, group(j)]).then_inc(x_loaded[p], 16)

            def load_residual(j, p):
                need(sp, x1_stored[p], START + 8 * (j - p))
                nc.sync.dma_start(x1s[:, p, :], xT[:, group(j)]).then_inc(r_loaded[p], 16)

            def store(j, p):
                sp.wait_ge(centred2, START + j + 1)
                nc.sync.dma_start(x1_dram[:, group(j)], x1s[:, p, :]).then_inc(x1_stored[p], 16)

            def stack(j, p):
                for c in range(2):
                    sp.wait_ge(qk_lo, START + 2 * j + 1 + c)
                    nc.sync.dma_start(scratch[p, c].rearrange("h w t -> w h t"), qk16[:, c]
                                      ).then_inc(qk_stored, 16)
                sp.wait_ge(qk_stored, START + 32 * j + 32)
                for var, half in enumerate((0, 1, 0)):
                    src = scratch[p, 0, half].rearrange("(g h d) t -> h d g t", g=QG, h=HQ)
                    for hh in range(HQ):
                        a = 32 * var + DH * hh
                        nc.sync.dma_start(QM[a:a + DH, p, :, hh, :], src[hh]).then_inc(stacked[p], 16)
                for var, half in enumerate((0, 0, 1)):
                    src = scratch[p, 1, half].rearrange("(g r) t -> r g t", g=QG)
                    nc.sync.dma_start(KS[32 * var:32 * var + 32, p, :, :], src).then_inc(stacked[p], 16)

            def body(i, p):
                if has(i + 3):
                    load_x(i + 3, 1 - p)
                if has(i + 2):
                    load_ctx(i + 2, p)
                if has(i):
                    load_residual(i, p)
                if has(i + 1):
                    if not has(i):
                        sp.wait_ge(zeroed, START + 3)
                    stack(i + 1, 1 - p)
                if has(i - 1):
                    store(i - 1, 1 - p)

            body(-3, 1)
            groups(sp, body, 4)
            for p in range(2):
                sp.wait_ge(x1_stored[p], START + 8 * G)

        @block.gpsimd
        def _(pool):
            nc.gpsimd.memset(VH[:], 0.0).then_inc(zeroed, 1)
            nc.gpsimd.memset(VL[:], 0.0).then_inc(zeroed, 1)

            def halves(i, t):
                b, n = t % 2, TPG * i + t
                pool.wait_ge(exped, START + n + 1)
                need(pool, summed, START + n - 1)
                nc.gpsimd.tensor_tensor(zh[:, b], ES[:, b, :, 0:L // 2], ES[:, b, :, L // 2:L],
                                        ALU.add).then_inc(halved, 1)
                pool.wait_ge(exped16, START + n + 1)
                need(pool, pv_done, START + n - 1)
                nc.gpsimd.tensor_tensor(EL[:, b], ES[:, b], EH[:, b], ALU.subtract).then_inc(e_lo, 1)

            def x_low(j):
                pool.wait_ge(hi2, START + j + 1)
                nc.gpsimd.tensor_tensor(XL[:, group(j)], xn2[:], XH[:, group(j)].bitcast(F32),
                                        ALU.subtract).then_inc(lo2, 1)

            def body(i, p):
                for t in range(TPG):
                    if has(i):
                        halves(i, t)
                    if t == 3 and has(i - 2):
                        x_low(i - 2)

            groups(pool, body)

        def v_slot(V, b, u, a):
            flat = V[64 * u:64 * u + 64, b, 8 * a:8 * a + 8, :].rearrange("p h c -> p (h c)")
            return bass.AP(flat.tensor, flat.offset + 64 * u, [list(flat.ap[0]), [136, 8], [1, DH]])

        def v_from(u, b, a):
            return vz[64 * u:64 * u + 64, b, 64 * a:64 * a + 64].rearrange("p (h d) -> p h d", h=8)

        @block.vector
        def _(dve):
            def norm1(j):
                dve.wait_ge(rstd1, START + j + 1)
                need(dve, q_done, START + j)
                nc.vector.tensor_tensor(xn1[:], xc1[:], sq1[:], ALU.mult).then_inc(normed1, 1)

            def split_qk(j, c):
                dve.wait_ge(q_out if c == 0 else k_out, START + j + 1)
                dve.wait_ge(qk_hi, START + 2 * j + 1 + c)
                nc.vector.tensor_tensor(qk16[:, c, 1], qk32[:, c, :], qk16[:, c, 0],
                                        ALU.subtract).then_inc(qk_lo, 1)

            def v_evac(j, p):
                dve.wait_ge(v_done, START + j + 1)
                need(dve, v_scaled, START + (TPG * j - TPG))
                nc.vector.tensor_tensor(v32[:, p], BA.rearrange("p (t c) -> p t c", t=TPG),
                                        W["bv0"][:].unsqueeze(1).to_broadcast([128, TPG, 128]),
                                        ALU.add).then_inc(v_out, 1)

            def peaks(i, t):
                b, n = t % 2, TPG * i + t
                s = S[b].rearrange("p a (h l) -> p (a h) l", l=L)
                dve.wait_ge(scored, START + n + 1)
                nc.vector.tensor_reduce(mx[:, b], s, AX.X, ALU.max).then_inc(maxed, 1)

            def shift(i, t):
                b, n = t % 2, TPG * i + t
                s = S[b].rearrange("p a (h l) -> p (a h) l", l=L)
                dve.wait_ge(maxed, START + n + 1)
                nc.vector.tensor_tensor(s, s, mx[:, b].unsqueeze(2).to_broadcast([128, H, L]),
                                        ALU.subtract).then_inc(shifted, 1)

            def sums(j, t):
                b, n = t % 2, TPG * j + t
                dve.wait_ge(halved, START + n + 1)
                nc.vector.tensor_reduce(zz[:, b], zh[:, b], AX.X, ALU.add).then_inc(summed, 1)

            def scale_v(j, p, t):
                b, n = t % 2, TPG * j + t
                dve.wait_ge(summed, START + n + 1)
                nc.vector.reciprocal(rz[:, b], zz[:, b]).then_inc(inverted, 1)
                dve.wait_ge(inverted, START + n + 1)
                dve.wait_ge(v_out, START + j + 1)
                nc.vector.tensor_tensor(vz[:, b].rearrange("p (h d) -> p h d", h=H),
                                        v32[:, p, t].rearrange("p (h d) -> p h d", h=H),
                                        rz[:, b].unsqueeze(2).to_broadcast([128, H, DH]),
                                        ALU.mult).then_inc(v_scaled, 1)

            def v_low(j, t):
                b, n = t % 2, TPG * j + t
                dve.wait_ge(v_hi, START + 4 * n + 4)
                for u in range(2):
                    for a in range(2):
                        nc.vector.tensor_tensor(v_slot(VL, b, u, a), v_from(u, b, a), v_slot(VH, b, u, a),
                                                ALU.subtract).then_inc(v_lo, 1)

            def x1(j, p):
                dve.wait_ge(projected, START + j + 1)
                dve.wait_ge(r_loaded[p], START + 8 * (j - p) + 16)
                nc.vector.scalar_tensor_tensor(out=x1s[:, p, :], in0=BC, scalar=W["bo0"][:, 0:1],
                                               in1=x1s[:, p, :], op0=ALU.add,
                                               op1=ALU.add).then_inc(x1_done, 1)

            def norm2(j):
                dve.wait_ge(rstd2, START + j + 1)
                need(dve, routed, START + j)
                need(dve, lo2, START + j)
                nc.vector.tensor_tensor(xn2[:], xc2[:], sq2[:], ALU.mult).then_inc(normed2, 1)

            def split2(j):
                dve.wait_ge(normed2, START + j + 1)
                nc.vector.tensor_copy(XH[:, group(j)], xn2[:]).then_inc(hi2, 1)

            def body(i, p):
                for t in range(TPG):
                    j, pj, tj = back(i, p, t, 1)
                    if t == 1 and has(i + 1):
                        v_evac(i + 1, 1 - p)
                    if has(i):
                        peaks(i, t)
                    if has(j):
                        sums(j, tj)
                        scale_v(j, pj, tj)
                    if has(i):
                        shift(i, t)
                    if t == 3 and has(i - 1):
                        x1(i - 1, 1 - p)
                    if t == 3 and has(i + 2):
                        norm1(i + 2)
                    if t == 0 and has(i + 1):
                        split_qk(i + 1, 0)
                        split_qk(i + 1, 1)
                    if t == 1 and has(i - 2):
                        norm2(i - 2)
                    if t == 3 and has(i - 2):
                        split2(i - 2)
                    if has(j):
                        v_low(j, tj)

            flat = QM[:].rearrange("p a b c d -> p (a b c d)").bitcast(I32)
            nc.vector.memset(flat, 0).then_inc(zeroed, 1)
            groups(dve, body)

        @block.scalar
        def _(act):
            def square(j, bank, xc, sq, mean, centred, squared, normed):
                act.wait_ge(mean, START + j + 1)
                need(act, normed, START + j)
                nc.scalar.activation(xc[:], bank, ACT.Copy).then_inc(centred, 1)
                nc.scalar.activation(sq[:], bank, ACT.Square).then_inc(squared, 1)

            def rstd(j, bank, sq, var, log, rst):
                act.wait_ge(var, START + j + 1)
                nc.scalar.activation(sq[:], bank, ACT.Ln, bias=W["eps"][:, 0:1]).then_inc(log, 1)
                act.wait_ge(log, START + j + 1)
                nc.scalar.activation(sq[:], sq[:], ACT.Exp, scale=-0.5).then_inc(rst, 1)

            def exps(i, t):
                b, n = t % 2, TPG * i + t
                s = S[b].rearrange("p a (h l) -> p (a h) l", l=L)
                act.wait_ge(shifted, START + n + 1)
                need(act, e_lo, START + n - 1)
                nc.scalar.activation(ES[:, b], s, ACT.Exp, scale=DH ** -0.5).then_inc(exped, 1)
                need(act, pv_done, START + n - 1)
                nc.scalar.activation(EH[:, b], s, ACT.Exp, scale=DH ** -0.5).then_inc(exped16, 1)

            def v_high(j, t):
                b, n = t % 2, TPG * j + t
                act.wait_ge(v_scaled, START + n + 1)
                if isinstance(j, int) and j == 0 and t == 0:
                    act.wait_ge(zeroed, START + 3)
                need(act, pv_done, START + n - 1)
                for u in range(2):
                    for a in range(2):
                        nc.scalar.activation(v_slot(VH, b, u, a), v_from(u, b, a),
                                             ACT.Copy).then_inc(v_hi, 1)

            def o_evac(j, t):
                act.wait_ge(pv_done, START + TPG * j + t + 1)
                need(act, projected, START + j)
                nc.scalar.activation(OS[:, t].rearrange("p a l -> p (a l)"), BO,
                                     ACT.Copy).then_inc(o_out, 1)

            def qk_evac(j, c):
                act.wait_ge(k_done if c else q_done, START + j + 1)
                need(act, qk_lo, START + (2 * j - 1 + c))
                bias = W["bk0" if c else "bq0"][:, 0:1]
                nc.scalar.activation(qk32[:, c, :], BC if c else BA, ACT.Identity,
                                     bias=bias).then_inc(k_out if c else q_out, 1)
                need(act, qk_stored, START + 32 * j)
                nc.scalar.activation(qk16[:, c, 0], BC if c else BA, ACT.Identity, bias=bias).then_inc(qk_hi, 1)

            def logit_evac(j):
                act.wait_ge(routed, START + j + 1)
                nc.scalar.activation(SC[:, :, bass.ds(j * TPG, TPG)].rearrange("p e t -> p t e"),
                                     BC[:, 0:TPG * E0].rearrange("p (t e) -> p t e", e=E0),
                                     ACT.Copy).then_inc(logits_out, 1)

            first = (BA, xc1, sq1, mean1, centred1, squared1, normed1)
            second = (BB, xc2, sq2, mean2, centred2, squared2, normed2)
            root1 = (BA, sq1, var1, log1, rstd1)
            root2 = (BB, sq2, var2, log2, rstd2)
            nc.scalar.preload_act_table_set(TABLES)

            def body(i, p):
                for t in range(TPG):
                    if t == 2 and has(i + 2):
                        square(i + 2, *first)
                    if t == 0 and has(i - 2):
                        square(i - 2, *second)
                    j, _, tj = back(i, p, t, 1)
                    if has(j):
                        v_high(j, tj)
                    if has(i):
                        exps(i, t)
                    j, _, tj = back(i, p, t, 2)
                    if has(j):
                        o_evac(j, tj)
                    if t == 2 and has(i + 2):
                        rstd(i + 2, *root1)
                    if t == 3 and has(i + 2):
                        qk_evac(i + 2, 0)
                        qk_evac(i + 2, 1)
                    if t == 0 and has(i - 2):
                        rstd(i - 2, *root2)
                    if t == 1 and has(i - 2):
                        logit_evac(i - 2)

            groups(act, body)

        @block.tensor
        def _(pe):
            def centre_1(j, p):
                pe.wait_ge(x_loaded[p], START + 8 * (j - p) + 16)
                need(pe, v_out, START + j)
                nc.tensor.matmul(BA, W["centre"][:], xg[:, p, :], start=True, stop=True).then_inc(mean1, 1)

            def var_1(j):
                pe.wait_ge(centred1, START + j + 1)
                pe.wait_ge(squared1, START + j + 1)
                nc.tensor.matmul(BA, W["mean"][:], sq1[:], start=True, stop=True).then_inc(var1, 1)

            def centre_2(j, p):
                pe.wait_ge(x1_done, START + j + 1)
                need(pe, log2, START + j)
                nc.tensor.matmul(BB, W["centre"][:], x1s[:, p, :], start=True, stop=True).then_inc(mean2, 1)

            def var_2(j):
                pe.wait_ge(centred2, START + j + 1)
                pe.wait_ge(squared2, START + j + 1)
                nc.tensor.matmul(BB, W["mean"][:], sq2[:], start=True, stop=True).then_inc(var2, 1)

            def q_proj(j):
                pe.wait_ge(normed1, START + j + 1)
                nc.tensor.matmul(BA, W["wq0"][:], xn1[:], start=True, stop=True).then_inc(q_done, 1)

            def k_proj(j, p):
                pe.wait_ge(c_loaded[p], START + 8 * (j - p) + 16)
                need(pe, x1_done, START + j - 2)
                nc.tensor.matmul(BC, W["wk0"][:], cg[:, p, :], start=True, stop=True).then_inc(k_done, 1)

            def v_proj(j, p):
                pe.wait_ge(qk_hi, START + 2 * j + 1)
                for t in range(TPG):
                    last = nc.tensor.matmul(BA[:, 128 * t:128 * t + 128], cg[:, p, 128 * t:128 * t + 128],
                                            W["wv0"][:], start=True, stop=True)
                last.then_inc(v_done, 1)

            def score(i, p, t):
                b, n = t % 2, TPG * i + t
                if t == 0:
                    pe.wait_ge(stacked[p], START + STACK // 2 * (i - p) + STACK)
                need(pe, exped16, START + n - 1)
                for u in range(2):
                    c0 = 128 * t + 64 * u
                    for g in range(QG):
                        last = nc.tensor.matmul(
                            S[b][64 * u:64 * u + 64, g // 2, 256 * (g % 2):256 * (g % 2) + 256],
                            KS[:, p, g, c0:c0 + 64], QM[:, p, g, :, c0:c0 + 64], start=True, stop=True)
                last.then_inc(scored, 1)

            def pv(j, t):
                b, n = t % 2, TPG * j + t
                pe.wait_ge(v_lo, START + 4 * n + 4)
                pe.wait_ge(e_lo, START + n + 1)
                need(pe, o_out, START + n)
                for a in range(2):
                    for h in range(8):
                        for k, (v, e) in enumerate(((VH, EH), (VL, EH), (VH, EL))):
                            last = nc.tensor.matmul(BO[:, 64 * a:64 * a + 64], v[:, b, 8 * a + h, :],
                                                    e[:, b, 8 * a + h, :],
                                                    start=(h == 0 and k == 0), stop=(h == 7 and k == 2))
                last.then_inc(pv_done, 1)

            def project(j):
                pe.wait_ge(o_out, START + TPG * j + TPG)
                pe.wait_ge(qk_hi, START + 2 * upto(j + 3))
                need(pe, logits_out, START + j)
                out = BC.rearrange("p (t u l) -> p u t l", t=TPG, u=2)
                for u in range(2):
                    for a in range(2):
                        last = nc.tensor.matmul(out[:, u], W["wo0"][:, u, a, :], OS[:, :, a, :],
                                                start=(a == 0), stop=(a == 1))
                last.then_inc(projected, 1)

            def logits(j):
                pe.wait_ge(normed2, START + j + 1)
                pe.wait_ge(qk_hi, START + 2 * upto(j + 4))
                for t in range(TPG):
                    last = nc.tensor.matmul(BC[:, E0 * t:E0 * t + E0], xn2[:, 128 * t:128 * t + 128],
                                            W["gw0"][:], start=True, stop=True)
                last.then_inc(routed, 1)

            def body(i, p):
                for t in range(TPG):
                    j, _, tj = back(i, p, t, 2)
                    if has(j):
                        pv(j, tj)
                    if t < TPG - 1 and has(i):
                        score(i, p, t + 1)
                    if t == TPG - 1 and has(i + 1):
                        score(i + 1, 1 - p, 0)
                    if t == 0 and has(i + 1):
                        v_proj(i + 1, 1 - p)
                    if t == 0 and has(i - 2):
                        var_2(i - 2)
                    if t == 1 and has(i + 2):
                        centre_1(i + 2, p)
                    if t == 1 and has(i - 2):
                        logits(i - 2)
                    if t == 2 and has(i - 1):
                        project(i - 1)
                    if t == 2 and has(i + 2):
                        var_1(i + 2)
                    if t == 3 and has(i - 1):
                        centre_2(i - 1, 1 - p)
                    if t == 3 and has(i + 2):
                        q_proj(i + 2)
                        k_proj(i + 2, p)

            groups(pe, body)


def first_ffn(nc, sem, P, W, X, XH, XL, SC, experts, x1_dram, gate_dram):
    with ExitStack() as ctx:
        def sb(name, shape, dt):
            return ctx.enter_context(nc.sbuf_tensor(name, shape, dt))

        WR = sb("WR", [128, 2, RC0], F32)
        WH = sb("WH", [128, 2, WC0], F32R)
        WL = sb("WL", [128, 2, WC0], F32R)
        HS = sb("HS", [128, 2, FC, TG], F32)
        HH = sb("HH", [128, 2, FC, TG], F32R)
        HL = sb("HL", [128, 2, FC, TG], F32R)
        GB = sb("GB", [128, 2, TG], F32)
        YB = sb("YB", [128, 2, TG], F32)
        cmp_ = sb("cmp_", [128, E0 * NT], F32)
        cnt = sb("cnt", [128, 1], F32)
        thr = sb("thr", [128, 1], I32)
        bit = sb("bit", [128, 1], I32)
        trial = sb("trial", [128, 1], I32)
        idle = sb("idle", [128, 1], F32)
        keep = sb("keep", [128, 1], I32)

        scores_ready = sem("scores_ready")
        x_loaded = sem("x_loaded")
        w_loaded = [sem("w_loaded0"), sem("w_loaded1")]
        w0_hi, w0_lo = sem("w0_hi"), sem("w0_lo")
        w_hi, w_lo = sem("w_hi"), sem("w_lo")
        h_done, gelu_done = sem("h_done"), sem("gelu_done")
        h_hi, h_lo = [sem("h_hi0"), sem("h_hi1")], [sem("h_lo0"), sem("h_lo1")]
        act_hi = sem("act_hi")
        y_done, y_out = [sem("y_done0"), sem("y_done1")], [sem("y_out0"), sem("y_out1")]
        added = [sem("added0"), sem("added1")]
        gates_loaded = [sem("gates_loaded0"), sem("gates_loaded1")]
        counted, totalled, stepped = sem("counted"), sem("totalled"), sem("stepped")
        BT, BY = P[:, 6, 0:1], [P[:, 4, :], P[:, 5, :]]
        HG = G // 2

        flat = SC[:].rearrange("p e j -> p (e j)")
        by_token = SC[:].rearrange("p e j -> p j e")
        peak = cmp_[:, 0:NT]
        with nc.Block() as block:
            @block.vector
            def _(dve):
                nc.vector.tensor_reduce(peak, by_token, AX.X, ALU.max).then_inc(scores_ready, 1)
                dve.wait_ge(scores_ready, START + 1)
                nc.vector.tensor_tensor(SC[:], SC[:], peak.unsqueeze(1).to_broadcast([128, E0, NT]),
                                        ALU.subtract).then_inc(scores_ready, 1)
                dve.wait_ge(scores_ready, START + 3)
                nc.vector.tensor_reduce(peak, by_token, AX.X, ALU.add).then_inc(scores_ready, 1)
                dve.wait_ge(scores_ready, START + 4)
                nc.vector.reciprocal(peak, peak).then_inc(scores_ready, 1)
                dve.wait_ge(scores_ready, START + 5)
                nc.vector.tensor_tensor(SC[:], SC[:], peak.unsqueeze(1).to_broadcast([128, E0, NT]),
                                        ALU.mult).then_inc(scores_ready, 1)
                nc.vector.memset(thr[:], 0).then_inc(scores_ready, 1)
                nc.vector.memset(bit[:], 1 << 29).then_inc(scores_ready, 1)
                nc.vector.memset(trial[:], 1 << 29).then_inc(scores_ready, 1)

            @block.scalar
            def _(act):
                act.wait_ge(scores_ready, START + 2)
                nc.scalar.activation(flat, flat, ACT.Exp).then_inc(scores_ready, 1)

            @block.sync
            def _(sp):
                nc.sync.dma_start(WR[:, 0], experts[0]).then_inc(w_loaded[0], 16)
                nc.sync.dma_start(WR[:, 1], experts[1]).then_inc(w_loaded[1], 16)
                nc.sync.dma_start(X[:], x1_dram).then_inc(x_loaded, 16)

        def w1(pe, q, w, b, u):
            if not (isinstance(q, int) and q == 0):
                pe.wait_ge(w_lo, START + q)
            for c in range(FC):
                need(pe, gelu_done, START + FC * (G * q + b - 1) + c + 1)
                wc = slice(128 * c, 128 * c + 128)
                for k, (a, x) in enumerate(((WH, XH), (WL, XH), (WH, XL))):
                    last = nc.tensor.matmul(P[:, c, :], a[:, w, wc], x[:, group(b)],
                                            start=(k == 0), stop=(k == 2))
                last.then_inc(h_done, 1)

        def total(pe, n):
            pe.wait_ge(counted, START + n + 1)
            nc.tensor.matmul(BT, W["ones"][:], cnt[:], start=True, stop=True).then_inc(totalled, 1)

        def w2(pe, w, u, n):
            need(pe, y_out[u], START + n)
            for half in range(2):
                pe.wait_ge(h_lo[u], START + 2 * n + half + 1)
                for c in (2 * half, 2 * half + 1):
                    wc = slice(F0 + 128 * c, F0 + 128 * c + 128)
                    for k, (a, h) in enumerate(((WH, HH), (WL, HH), (WH, HL))):
                        last = nc.tensor.matmul(BY[u], a[:, w, wc], h[:, u, c, :],
                                                start=(c == 0 and k == 0), stop=(c == FC - 1 and k == 2))
            last.then_inc(y_done[u], 1)

        def gelus(act, q, w, b, u, n):
            for c in range(FC):
                act.wait_ge(h_done, START + FC * (G * q + b) + c + 1)
                if c % 2 == 0:
                    need(act, h_lo[u], START + (2 * n))
                nc.scalar.activation(HS[:, u, c, :], P[:, c, :], ACT.Gelu_apprx_tanh,
                                     bias=WR[:, w, WC0 + c:WC0 + c + 1]).then_inc(gelu_done, 1)

        def split_half(dve, q, b, u, n, half, n_hi):
            hs = slice(2 * half, 2 * half + 2)
            dve.wait_ge(gelu_done, START + FC * (G * q + b) + 2 * half + 2)
            need(dve, y_done[u], START + n)
            nc.vector.tensor_copy(HH[:, u, hs], HS[:, u, hs]).then_inc(h_hi[u], 1)
            dve.wait_ge(h_hi[u], START + n_hi + 1)
            nc.vector.tensor_tensor(HL[:, u, hs], HS[:, u, hs], HH[:, u, hs].bitcast(F32),
                                    ALU.subtract).then_inc(h_lo[u], 1)

        def split(dve, q, b, u, n):
            for half in range(2):
                split_half(dve, q, b, u, n, half, 2 * n + half - HG)

        def gated(dve, w, u, n, shared):
            dve.wait_ge(y_done[u], START + n + 1)
            need(dve, added[u], START + n)
            b2 = WR[:, w, WC0 + FC:WC0 + FC + 1]
            if shared:
                nc.vector.tensor_scalar(YB[:, u, :], BY[u], b2, W["gf"][:, 0:1], ALU.add,
                                        ALU.mult).then_inc(y_out[u], 1)
            else:
                dve.wait_ge(gates_loaded[u], START + 16 * (n + 1) - 16 * HG)
                nc.vector.scalar_tensor_tensor(out=YB[:, u, :], in0=BY[u], scalar=b2, in1=GB[:, u, :],
                                               op0=ALU.add, op1=ALU.mult).then_inc(y_out[u], 1)

        def split_weights(eng, q, w, kq, w_hi=w_hi, w_lo=w_lo):
            eng.wait_ge(w_loaded[w], START + 16 * kq + 16)
            if not isinstance(q, int):
                eng.tensor_tensor(idle[:], W["eps"][:], W["eps"][:], ALU.add)
            eng.tensor_copy(WH[:, w], WR[:, w, 0:WC0]).then_inc(w_hi, 1)
            eng.wait_ge(w_hi, START + (max(q, 1) if isinstance(q, int) else q))
            eng.tensor_tensor(WL[:, w], WR[:, w, 0:WC0], WH[:, w].bitcast(F32),
                              ALU.subtract).then_inc(w_lo, 1)

        def add(pool, b, u, n):
            pool.wait_ge(y_out[u], START + n + 1)
            need(pool, added[1 - u], START + n + u)
            nc.gpsimd.tensor_tensor(X[:, group(b)], X[:, group(b)], YB[:, u, :],
                                    ALU.add).then_inc(added[u], 1)

        def over_groups(eng, q, ahead, here, last_ahead):
            with eng.Fori(0, HG - 1) as r:
                ahead(2 * r + 1, 1, HG * q + r)
                here(2 * r, 0, HG * q + r)
                ahead(2 * r + 2, 0, HG * q + r + 1)
                here(2 * r + 1, 1, HG * q + r)
            ahead(G - 1, 1, HG * q + HG - 1)
            here(G - 2, 0, HG * q + HG - 1)
            last_ahead()
            here(G - 1, 1, HG * q + HG - 1)

        def over_experts(eng, expert):
            with eng.Fori(0, E0 // 2 - 1) as r:
                expert(2 * r + 1, 1, r, False)
                expert(2 * r + 2, 0, r + 1, False)
            expert(E0 - 1, 1, E0 // 2 - 1, False)
            expert(E0, 0, E0 // 2, True)

        with nc.Block() as block:
            @block.tensor
            def _(pe):
                pe.wait_ge(w0_lo, START + 1)
                w1(pe, 0, 0, 0, 0)

                def ahead(b, u, n):
                    w1(pe, 0, 0, b, u)

                def here(b, u, n):
                    total(pe, 2 * b)
                    w2(pe, 0, u, n)
                    total(pe, 2 * b + 1)

                over_groups(pe, 0, ahead, here, lambda: w1(pe, 1, 1, 0, 0))

            @block.scalar
            def _(act):
                def gelus_and_high(b, u, n):
                    for c in range(FC):
                        bias = WR[:, 0, WC0 + c:WC0 + c + 1]
                        act.wait_ge(h_done, START + FC * b + c + 1)
                        if c >= FC // 2:
                            need(act, y_done[u], START + n)
                            nc.scalar.activation(HH[:, u, c, :], P[:, c, :], ACT.Gelu_apprx_tanh,
                                                 bias=bias).then_inc(act_hi, 1)
                        if c % 2 == 0:
                            need(act, h_lo[u], START + 2 * n)
                        nc.scalar.activation(HS[:, u, c, :], P[:, c, :], ACT.Gelu_apprx_tanh,
                                             bias=bias).then_inc(gelu_done, 1)

                with act.Fori(0, HG) as r:
                    gelus_and_high(2 * r, 0, r)
                    gelus_and_high(2 * r + 1, 1, r)

            @block.gpsimd
            def _(pool):
                def low(b, u, n):
                    hs = slice(FC // 2, FC)
                    pool.wait_ge(gelu_done, START + FC * b + FC)
                    pool.wait_ge(act_hi, START + 2 * b + 2)
                    pool.wait_ge(h_lo[u], START + 2 * n + 1)
                    nc.gpsimd.tensor_tensor(HL[:, u, hs], HS[:, u, hs], HH[:, u, hs].bitcast(F32),
                                            ALU.subtract).then_inc(h_lo[u], 1)

                split_weights(nc.gpsimd, 1, 1, 0)
                low(0, 0, 0)
                pool.wait_ge(x_loaded, START + 16)

                def ahead(b, u, n):
                    low(b, u, n)

                def here(b, u, n):
                    add(pool, b, u, n)

                over_groups(pool, 0, ahead, here, lambda: None)

            @block.vector
            def _(dve):
                split_weights(nc.vector, 0, 0, 0, w0_hi, w0_lo)
                split_half(dve, 0, 0, 0, 0, 0, 0)

                def count(n):
                    dve.wait_ge(stepped, START + 4 * n)
                    need(dve, totalled, START + n)
                    nc.vector.tensor_scalar(cmp_[:], flat, trial[:].bitcast(F32), 0.0, ALU.is_ge, ALU.add,
                                            accum_out=cnt[:]).then_inc(counted, 1)

                def step(n):
                    dve.wait_ge(totalled, START + n + 1)
                    nc.vector.scalar_tensor_tensor(out=keep[:], in0=BT, scalar=float(KTOP), in1=bit[:],
                                                   op0=ALU.is_ge, op1=ALU.mult).then_inc(stepped, 1)
                    dve.wait_ge(stepped, START + 4 * n + 1)
                    nc.vector.tensor_scalar(bit[:], bit[:], 1, None,
                                            ALU.logical_shift_right).then_inc(stepped, 1)
                    nc.vector.tensor_tensor(thr[:], thr[:], keep[:], ALU.bitwise_or).then_inc(stepped, 1)
                    dve.wait_ge(stepped, START + 4 * n + 3)
                    nc.vector.tensor_tensor(trial[:], thr[:], bit[:], ALU.bitwise_or).then_inc(stepped, 1)

                count(0)

                def ahead(b, u, n):
                    split_half(dve, 0, b, u, n, 0, n)

                def here(b, u, n):
                    step(2 * b)
                    count(2 * b + 1)
                    gated(dve, 0, u, n, True)
                    step(2 * b + 1)
                    if not (isinstance(b, int) and b == G - 1):
                        count(2 * b + 2)

                over_groups(dve, 0, ahead, here, lambda: None)

        above = HS[:, 0, 0, :]
        on = HS[:, 0, 1, :]
        rank = HS[:, 0, 3, :]
        gates = HS[:, 1, 0, :]
        gt = YB[:, 0, :]
        left = cnt
        TRI = GB[:, 0, 0:128]
        ident = GB[:, 0, 128:256]
        chosen, made, stored = sem("chosen"), sem("gate_masks"), sem("gates_stored")
        gt_sems = sem("gate_products")
        with nc.Block() as block:
            @block.gpsimd
            def _(pool):
                nc.gpsimd.memset(TRI, 0.0)
                nc.gpsimd.memset(ident, 1.0).then_inc(made, 1)
                pool.wait_ge(made, START + 1)
                nc.gpsimd.affine_select(out=TRI, in_=TRI, compare_op=ALU.is_gt, fill=-1.0, base=0,
                                        pattern=[[1, 128]], channel_multiplier=-1).then_inc(made, 1)
                nc.gpsimd.affine_select(out=ident, in_=ident, compare_op=ALU.is_equal, fill=0.0, base=0,
                                        pattern=[[1, 128]], channel_multiplier=-1).then_inc(made, 1)

            @block.vector
            def _(dve):
                n = [0]

                def step(instruction):
                    instruction.then_inc(chosen, 1)
                    n[0] += 1
                    dve.wait_ge(chosen, START + n[0])

                t32 = thr[:].bitcast(F32)
                step(nc.vector.tensor_scalar(on, flat, t32, None, ALU.is_equal))
                step(nc.vector.tensor_scalar(above, flat, t32, 0.0, ALU.is_gt, ALU.add, accum_out=cnt[:]))
                dve.wait_ge(gt_sems, START + 1)
                step(nc.vector.tensor_scalar(left[:], BT, -1.0, float(KTOP), ALU.mult, ALU.add))
                dve.wait_ge(gt_sems, START + 2)
                step(nc.vector.tensor_tensor_scan(rank, W["one_row"][:], P[:, 5, :], 0.0, ALU.mult, ALU.add))
                dve.wait_ge(gt_sems, START + 3)
                step(nc.vector.tensor_tensor(rank, rank, P[:, 4, :], ALU.add))
                step(nc.vector.scalar_tensor_tensor(out=rank, in0=rank, scalar=left[:], in1=on,
                                                    op0=ALU.is_lt, op1=ALU.mult))
                step(nc.vector.tensor_tensor(rank, rank, above, ALU.add))
                nc.vector.scalar_tensor_tensor(out=gates, in0=flat, scalar=W["gf"][:, 0:1], in1=rank,
                                               op0=ALU.mult, op1=ALU.mult).then_inc(made, 1)
                dve.wait_ge(gt_sems, START + 4)
                nc.vector.tensor_copy(gt, P[:, 7, :]).then_inc(made, 1)

            @block.tensor
            def _(pe):
                pe.wait_ge(chosen, START + 2)
                nc.tensor.matmul(BT, W["ones"][:], cnt[:], start=True, stop=True).then_inc(gt_sems, 1)
                pe.wait_ge(made, START + 3)
                nc.tensor.matmul(P[:, 5, :], W["ones"][:], on, start=True, stop=True).then_inc(gt_sems, 1)
                nc.tensor.matmul(P[:, 4, :], TRI, on, start=True, stop=True).then_inc(gt_sems, 1)
                pe.wait_ge(made, START + 4)
                for k in range(4):
                    last = nc.tensor.transpose(P[:, 7, 128 * k:128 * k + 128], gates[:, 128 * k:128 * k + 128],
                                               ident)
                last.then_inc(gt_sems, 1)

            @block.sync
            def _(sp):
                sp.wait_ge(made, START + 5)
                nc.sync.dma_start(gate_dram.rearrange("(k e) (j p) -> (e j) k p", e=2, p=128),
                                  gt.rearrange("r (k p) -> r k p", k=4)).then_inc(stored, 16)

        with nc.Block() as block:
            @block.sync
            def _(sp):
                def gate_load(q, b, u, n):
                    sp.wait_ge(y_out[u], START + n)
                    nc.sync.dma_start(GB[:, u, :], gate_dram[q - 1, group(b)].partition_broadcast(128)
                                      ).then_inc(gates_loaded[u], 16)

                def expert(q, w, kq, last):
                    with sp.Fori(0, HG) as r:
                        gate_load(q, 2 * r, 0, HG * q + r)
                        gate_load(q, 2 * r + 1, 1, HG * q + r)

                def weights(q, w):
                    sp.wait_ge(y_out[0], START + HG * (q - 1))
                    sp.wait_ge(y_out[1], START + HG * (q - 1))
                    nc.sync.dma_start(WR[:, w], experts[q]).then_inc(w_loaded[w], 16)

                weights(2, 0)
                sp.wait_ge(stored, START + 16)
                with sp.Fori(0, E0 // 2 - 1) as r:
                    expert(2 * r + 1, 1, r, False)
                    weights(2 * r + 3, 1)
                    expert(2 * r + 2, 0, r + 1, False)
                    weights(2 * r + 4, 0)
                expert(E0 - 1, 1, 0, False)
                expert(E0, 0, 0, True)

            @block.tensor
            def _(pe):
                def expert(q, w, kq, last):
                    over_groups(pe, q, lambda b, u, n: w1(pe, q, w, b, u), lambda b, u, n: w2(pe, w, u, n),
                                (lambda: None) if last else (lambda: w1(pe, q + 1, 1 - w, 0, 0)))
                over_experts(pe, expert)

            @block.scalar
            def _(act):
                def expert(q, w, kq, last):
                    act.wait_ge(w_loaded[w], START + 16 * kq + 16)
                    with act.Fori(0, HG) as r:
                        gelus(act, q, w, 2 * r, 0, HG * q + r)
                        gelus(act, q, w, 2 * r + 1, 1, HG * q + r)
                over_experts(act, expert)

            @block.gpsimd
            def _(pool):
                def expert(q, w, kq, last):
                    with pool.Fori(0, HG // 2) as r:
                        add(pool, 2 * r, 0, HG * q + r)
                        add(pool, 2 * r + 1, 1, HG * q + r)
                    if not last:
                        split_weights(nc.gpsimd, q + 1, 1 - w, kq + w)
                    with pool.Fori(HG // 2, HG) as r:
                        add(pool, 2 * r, 0, HG * q + r)
                        add(pool, 2 * r + 1, 1, HG * q + r)
                over_experts(pool, expert)

            @block.vector
            def _(dve):
                split(dve, 1, 0, 0, HG)

                def expert(q, w, kq, last):
                    def last_ahead():
                        if not last:
                            split(dve, q + 1, 0, 0, HG * q + HG)
                    over_groups(dve, q, lambda b, u, n: split(dve, q, b, u, n),
                                lambda b, u, n: gated(dve, w, u, n, False), last_ahead)
                over_experts(dve, expert)


def delay_weights(nc, sem, P, W, X, WFH, WFL, ctxT, ins, we_dram):
    with ExitStack() as ctx:
        def sb(name, shape, dt):
            return ctx.enter_context(nc.sbuf_tensor(name, shape, dt))

        TU = 2 * TG
        NU, NBU = T // TU, TU // L
        cg = sb("d_cg", [128, 2, TU], F32)
        sq = sb("d_sq", [128, 2, TU], F32)
        xn = sb("d_xn", [128, TU], F32)
        chunks = [slice(k, min(k + 4, PAIRS)) for k in range(0, PAIRS, 4)]
        raw = sb("d_raw", [128, 2, 4, 3 * 128], F32)
        sx = sb("sx", [128, NB], F32)
        sc = sb("sc", [128, NB], F32)
        wqT = sb("wq1T", [128, 128], F32)
        wkT = sb("wk1T", [128, 128], F32)
        wv = sb("wv1", [128, 128], F32)
        woT = sb("wo1T", [128, 128], F32)
        bqB = sb("bq1B", [128, 128], F32)
        bkB = sb("bk1B", [128, 128], F32)
        bv = sb("bv1", [128, 1], F32)
        bo = sb("bo1", [128, 1], F32)
        qs = sb("qs", [128, 128], F32)
        ks = sb("ks", [128, 128], F32)
        corr = sb("corr", [128, DH], F32)
        peak = sb("d_peak", [128, 1], F32)
        total = sb("d_total", [128, 1], F32)
        WE = sb("WE", [128, 2 * L], F32)

        w_loaded, c_loaded = sem("d_w_loaded"), [sem("d_c_loaded0"), sem("d_c_loaded1")]
        centred, squared, var = sem("d_centred"), sem("d_squared"), sem("d_var")
        log, rstd, normed, summed, c_summed = sem("d_log"), sem("d_rstd"), sem("d_normed"), sem("d_summed"), sem("d_c_summed")
        multiplied, chain, exped, stored = sem("d_multiplied"), sem("d_chain"), sem("d_exped"), sem("d_stored")
        raw_loaded, wf_hi, wf_lo = [sem("raw_loaded0"), sem("raw_loaded1")], sem("wf_hi"), sem("wf_lo")
        banks_x = [P[:, 0:2, :], P[:, 2:4, :]]
        banks_var = [P[:, 4:6, :], P[:, 6:8, :]]

        def unit(i):
            return bass.ds(i * TU, TU)

        def banked(v):
            return v.rearrange("p (a t) -> p a t", a=2)

        def units(eng, body):
            for i in range(-2, 0):
                body(i, i % 2, i + 2 < NU, i + 1 >= 0, i >= 0)
            with eng.Fori(0, NU // 2 - 1) as r:
                body(2 * r, 0, True, True, True)
                body(2 * r + 1, 1, True, True, True)
            for i in range(NU - 2, NU):
                body(i, i % 2, False, i + 1 < NU, True)

        with nc.Block() as block:
            @block.sync
            def _(sp):
                def load_weights(k):
                    pairs = chunks[k]
                    nc.sync.dma_start(raw[:, k % 2, 0:pairs.stop - pairs.start], ins["experts1"][:, pairs]
                                      ).then_inc(raw_loaded[k % 2], 16)

                for dst, name in ((wqT, "wq1T"), (wkT, "wk1T"), (wv, "L1_xattn_Wv"), (woT, "wo1T")):
                    nc.sync.dma_start(dst[:], ins[name]).then_inc(w_loaded, 16)
                for dst, name in ((bqB, "L1_xattn_bq"), (bkB, "L1_xattn_bk")):
                    nc.sync.dma_start(dst[:], ins[name].partition_broadcast(128)).then_inc(w_loaded, 16)
                for dst, name in ((bv, "L1_xattn_bv"), (bo, "L1_xattn_bo")):
                    nc.sync.dma_start(dst[:], ins[name].rearrange("(p a) -> p a", a=1)).then_inc(w_loaded, 16)
                for k in range(2):
                    nc.sync.dma_start(cg[:, k, :], ctxT[:, unit(k)]).then_inc(c_loaded[k], 16)
                load_weights(0)
                load_weights(1)
                for k in range(2, NU):
                    sp.wait_ge(c_summed, START + k - 1)
                    nc.sync.dma_start(cg[:, k % 2, :], ctxT[:, unit(k)]).then_inc(c_loaded[k % 2], 16)
                    chunk = k // 2 + 1
                    if k % 2 and chunk < len(chunks):
                        sp.wait_ge(wf_lo, START + chunk - 1)
                        load_weights(chunk)
                sp.wait_ge(chain, START + 2 * DH - 1)
                nc.sync.dma_start(we_dram, WE[:]).then_inc(stored, 16)
                sp.wait_ge(stored, START + 16)

            @block.tensor
            def _(pe):
                def body(i, p, first, second, last):
                    if second:
                        pe.wait_ge(squared, START + i + 2)
                        for k in range(2):
                            done = nc.tensor.matmul(banks_var[1 - p][:, k], W["mean"][:],
                                                    sq[:, 1 - p, k * TG:(k + 1) * TG], start=True, stop=True)
                        done.then_inc(var, 1)
                    if first:
                        need(pe, normed, START + i + 1)
                        for k in range(2):
                            done = nc.tensor.matmul(banks_x[p][:, k], W["centre"][:],
                                                    X[:, bass.ds((i + 2) * TU + k * TG, TG)], start=True, stop=True)
                        done.then_inc(centred, 1)

                units(pe, body)
                pe.wait_ge(normed, START + NU)
                pe.wait_ge(w_loaded, START + 128)
                nc.tensor.matmul(P[:, 6, 0:128], wv[:], woT[:], start=True, stop=True).then_inc(multiplied, 1)
                nc.tensor.matmul(P[:, 7, 0:1], woT[:], bv[:], start=True, stop=True).then_inc(multiplied, 1)
                pe.wait_ge(summed, START + NU)
                pe.wait_ge(c_summed, START + NU)
                nc.tensor.matmul(P[:, 4, 0:128], sx[:], wqT[:], start=True, stop=True).then_inc(multiplied, 1)
                nc.tensor.matmul(P[:, 5, 0:128], sc[:], wkT[:], start=True, stop=True).then_inc(multiplied, 1)

            @block.scalar
            def _(act):
                nc.scalar.preload_act_table_set(TABLES)

                def body(i, p, first, second, last):
                    j, q = i + 1, 1 - p
                    if second:
                        act.wait_ge(centred, START + j + 1)
                        need(act, normed, START + j - 1)
                        nc.scalar.activation(banked(sq[:, q, :]), banks_x[q], ACT.Square).then_inc(squared, 1)
                        act.wait_ge(var, START + j + 1)
                        nc.scalar.activation(banked(sq[:, q, :]), banks_var[q], ACT.Ln,
                                             bias=W["eps"][:, 0:1]).then_inc(log, 1)
                        act.wait_ge(log, START + j + 1)
                        nc.scalar.activation(sq[:, q, :], sq[:, q, :], ACT.Exp, scale=-0.5).then_inc(rstd, 1)

                units(act, body)
                act.wait_ge(exped, START + 1)
                nc.scalar.activation(corr[:], corr[:], ACT.Exp, accum_out=total[:]).then_inc(exped, 1)

            @block.vector
            def _(dve):
                def body(i, p, first, second, last):
                    if last:
                        dve.wait_ge(c_loaded[p], START + 8 * (i - p) + 16)
                        nc.vector.tensor_reduce(sc[:, bass.ds(i * NBU, NBU)],
                                                cg[:, p, :].rearrange("p (n l) -> p n l", l=L),
                                                AX.X, ALU.add).then_inc(c_summed, 1)
                        dve.wait_ge(rstd, START + i + 1)
                        need(dve, summed, START + i)
                        nc.vector.tensor_tensor(banked(xn[:]), banks_x[p], banked(sq[:, p, :]),
                                                ALU.mult).then_inc(normed, 1)
                        dve.wait_ge(normed, START + i + 1)
                        nc.vector.tensor_reduce(sx[:, bass.ds(i * NBU, NBU)],
                                                xn[:].rearrange("p (n l) -> p n l", l=L),
                                                AX.X, ALU.add).then_inc(summed, 1)

                units(dve, body)
                n = [0]
                steps = sem("d_steps")

                def step(instruction):
                    instruction.then_inc(steps, 1)
                    n[0] += 1
                    dve.wait_ge(steps, START + n[0])

                step(nc.vector.memset(WE[:], 0.0))
                dve.wait_ge(multiplied, START + 2)
                step(nc.vector.tensor_scalar(W["wvo1"][:], P[:, 6, 0:128], W["gx"][:, 1:2], None, ALU.mult))
                step(nc.vector.tensor_tensor(W["bvo1"][:], P[:, 7, 0:1], bo[:], ALU.add))
                step(nc.vector.tensor_scalar(W["bvo1"][:], W["bvo1"][:], W["gx"][:, 1:2], None, ALU.mult))
                dve.wait_ge(multiplied, START + 4)
                step(nc.vector.scalar_tensor_tensor(out=qs[:], in0=bqB[:], scalar=float(L), in1=P[:, 4, 0:128],
                                                    op0=ALU.mult, op1=ALU.add))
                step(nc.vector.scalar_tensor_tensor(out=ks[:], in0=bkB[:], scalar=float(L), in1=P[:, 5, 0:128],
                                                    op0=ALU.mult, op1=ALU.add))
                step(nc.vector.tensor_tensor(qs[:], qs[:], ks[:], ALU.mult))
                step(nc.vector.tensor_reduce(corr[:], qs[:].rearrange("p (h c) -> p c h", h=H), AX.X, ALU.add))
                step(nc.vector.tensor_scalar(corr[:], corr[:], 1.0 / (H * L), None, ALU.mult))
                step(nc.vector.tensor_reduce(peak[:], corr[:], AX.X, ALU.max))
                nc.vector.tensor_scalar(corr[:], corr[:], peak[:], None, ALU.subtract).then_inc(exped, 1)
                dve.wait_ge(exped, START + 2)
                step(nc.vector.reciprocal(total[:], total[:]))
                step(nc.vector.tensor_scalar(corr[:], corr[:], total[:], None, ALU.mult))
                for d in range(DH):
                    nc.vector.tensor_copy(WE[:, L - d:L - d + 1], corr[:, d:d + 1]).then_inc(chain, 1)
                    if d:
                        nc.vector.tensor_copy(WE[:, 2 * L - d:2 * L - d + 1], corr[:, d:d + 1]).then_inc(chain, 1)

            @block.gpsimd
            def _(pool):
                for k, pairs in enumerate(chunks):
                    n = pairs.stop - pairs.start
                    pool.wait_ge(raw_loaded[k % 2], START + 16 * (k // 2 + 1))
                    nc.gpsimd.tensor_copy(WFH[:, pairs], raw[:, k % 2, 0:n]).then_inc(wf_hi, 1)
                    pool.wait_ge(wf_hi, START + k + 1)
                    nc.gpsimd.tensor_tensor(WFL[:, pairs], raw[:, k % 2, 0:n], WFH[:, pairs].bitcast(F32),
                                            ALU.subtract).then_inc(wf_lo, 1)


def delays_and_routes(nc, sem, P, W, X, XH, XL, ins, we_dram, c_dram):
    with ExitStack() as ctx:
        def sb(name, shape, dt):
            return ctx.enter_context(nc.sbuf_tensor(name, shape, dt))

        TR = 2 * TPG
        cn = sb("cn", [128, 2, TPG, 128], F32)
        CM = sb("CM", [128, 2, TPG, 128], F32)
        ag = sb("ag", [128, TG], F32)
        sq = sb("e_sq", [128, 2, TG], F32)
        xn = sb("e_xn", [128, TG], F32)
        ident = sb("ident", [128, 128], F32)
        biasB = sb("biasB", [128, E1], F32)
        gw = sb("gw1", [128, E1], F32)
        seg = [sb("seg_g", [128, TPG, NG1], F32), sb("seg_e", [128, TPG, E1], F32)]
        R = {n: sb("r_" + n, [128, TR, k], F32) for n, k in {
            "exp": E1, "score": E1, "choice": E1, "group": NG1, "top": 8, "above": E1, "on": E1,
            "rank": E1, "count": 1, "pick_g": NG1, "pick_e": E1, "weight": E1, "sum": 1, "comb": E1, "idle": 1}.items()}
        ct = sb("ct", [E1, 2, TG], F32)

        w_loaded, ready = sem("e_w_loaded"), sem("e_ready")
        with nc.Block() as block:
            @block.sync
            def _(sp):
                nc.sync.dma_start(gw[:], ins["gate1T"]).then_inc(w_loaded, 16)
                nc.sync.dma_start(biasB[:], ins["L1_ffn_e_score_correction_bias"].partition_broadcast(128)
                                  ).then_inc(w_loaded, 16)

            @block.vector
            def _(dve):
                nc.vector.memset(CM[:], 0.0).then_inc(ready, 1)
                for s in seg:
                    nc.vector.memset(s[:], 1.0).then_inc(ready, 1)
                dve.wait_ge(ready, START + 3)
                for s in seg:
                    nc.vector.memset(s[:, :, 0:1], 0.0).then_inc(ready, 1)
                dve.wait_ge(ready, START + 5)

            @block.gpsimd
            def _(pool):
                made = sem("e_ident")
                nc.gpsimd.memset(ident[:], 1.0).then_inc(made, 1)
                pool.wait_ge(made, START + 1)
                nc.gpsimd.affine_select(out=ident[:], in_=ident[:], compare_op=ALU.is_equal, fill=0.0, base=0,
                                        pattern=[[1, 128]], channel_multiplier=-1).then_inc(made, 1)
                pool.wait_ge(made, START + 2)

        loaded = [sem("e_loaded0"), sem("e_loaded1")]
        agg, agg_out, projected, x3 = sem("e_agg"), sem("e_agg_out"), sem("e_projected"), sem("e_x3")
        centred, squared, var = sem("e_centred"), sem("e_squared"), sem("e_var")
        log, rstd, normed, hi, lo = sem("e_log"), sem("e_rstd"), sem("e_normed"), sem("e_hi"), sem("e_lo")
        logits, exped, chosen, turned, turned_out = (sem("e_logits"), sem("e_exped"), sem("e_chosen"),
                                                     sem("e_turned"), sem("e_turned_out"))
        stored = [sem("e_stored0"), sem("e_stored1")]
        steps = sem("e_steps")
        ALL = 4 * (TPG + 12)

        def groups(eng, body, ahead=4):
            for i in range(-ahead, 4):
                body(i, i % 2)
            with eng.Fori(2, (G - ahead) // 2) as r:
                body(2 * r, 0)
                body(2 * r + 1, 1)
            for i in range(G - ahead, G + 4):
                body(i, i % 2)

        BAG, BPR, BL, BTR = P[:, 0, :], P[:, 1, :], P[:, 6, 0:TR * E1], P[0:E1, 7, :]
        banks_x, banks_var = [P[:, 2, :], P[:, 3, :]], [P[:, 4, :], P[:, 5, :]]
        block = ctx.enter_context(nc.Block())

        @block.sync
        def _(sp):
            we = we_dram.rearrange("n j -> (n j)")
            ctx_n = ins["ctxN"].rearrange("(g j p) d -> g p j d", j=TPG, p=128)

            def load(i, p):
                need(sp, agg, START + i - 1)
                nc.sync.dma_start(cn[:, p], ctx_n[i]).then_inc(loaded[p], 16)
                for u in range(2):
                    at = we[bass.ds((i * NBG + u) * 2 * L + 1, 1)]
                    src = bass.AP(at.tensor, at.offset, [[1, L], [4 * L, TPG], [1, L]])
                    nc.sync.dma_start(CM[64 * u:64 * u + 64, p, :, 64 * u:64 * u + 64], src).then_inc(loaded[p], 16)

            def store(i, p):
                sp.wait_ge(turned_out, START + i + 1)
                nc.sync.dma_start(c_dram[:, group(i)], ct[:, p, :]).then_inc(stored[p], 16)

            def body(i, p):
                if has(i + 5):
                    load(i + 5, 1 - p)
                if has(i - 3):
                    store(i - 3, 1 - p)

            groups(sp, body, 6)
            for p in range(2):
                sp.wait_ge(stored[p], START + 8 * G)

        @block.tensor
        def _(pe):
            def aggregate(j, p):
                pe.wait_ge(loaded[p], START + 24 * (j - p) + 48)
                need(pe, agg_out, START + j)
                for t in range(TPG):
                    last = nc.tensor.matmul(BAG[:, 128 * t:128 * t + 128], cn[:, p, t, :], CM[:, p, t, :],
                                            start=True, stop=True)
                last.then_inc(agg, 1)

            def project(j):
                pe.wait_ge(agg_out, START + j + 1)
                need(pe, x3, START + j)
                nc.tensor.matmul(BPR, W["wvo1"][:], ag[:], start=True, stop=True).then_inc(projected, 1)

            def centre(j, p):
                pe.wait_ge(x3, START + j + 1)
                need(pe, normed, START + j - 1)
                nc.tensor.matmul(banks_x[p], W["centre"][:], X[:, group(j)], start=True,
                                 stop=True).then_inc(centred, 1)

            def var_of(j, p):
                pe.wait_ge(squared, START + j + 1)
                nc.tensor.matmul(banks_var[p], W["mean"][:], sq[:, p, :], start=True, stop=True).then_inc(var, 1)

            def route(j, p):
                pe.wait_ge(normed, START + j + 1)
                need(pe, exped, START + j)
                for t in range(TPG):
                    at = E1 * (TPG * p + t)
                    last = nc.tensor.matmul(BL[:, at:at + E1], xn[:, 128 * t:128 * t + 128], gw[:],
                                            start=True, stop=True)
                last.then_inc(logits, 1)

            def turn(j, p):
                pe.wait_ge(chosen, START + j - p + 2)
                need(pe, turned_out, START + j)
                for t in range(TPG):
                    last = nc.tensor.transpose(BTR[:, 128 * t:128 * t + 128], R["comb"][:, TPG * p + t, :], ident[:])
                last.then_inc(turned, 1)

            def body(i, p):
                if has(i + 4):
                    aggregate(i + 4, p)
                if has(i + 3):
                    centre(i + 3, 1 - p)
                if has(i + 4):
                    project(i + 4)
                if has(i + 2):
                    var_of(i + 2, p)
                if has(i + 1):
                    route(i + 1, 1 - p)
                if has(i - 3):
                    turn(i - 3, 1 - p)

            pe.wait_ge(w_loaded, START + 32)
            groups(pe, body)

        @block.scalar
        def _(act):
            def body(i, p):
                j = i + 4
                if has(j):
                    act.wait_ge(agg, START + j + 1)
                    need(act, projected, START + j)
                    nc.scalar.activation(ag[:], BAG, ACT.Copy).then_inc(agg_out, 1)
                j = i + 2
                if has(j):
                    act.wait_ge(centred, START + j + 1)
                    need(act, normed, START + j - 1)
                    nc.scalar.activation(sq[:, p, :], banks_x[p], ACT.Square).then_inc(squared, 1)
                    act.wait_ge(var, START + j + 1)
                    nc.scalar.activation(sq[:, p, :], banks_var[p], ACT.Ln, bias=W["eps"][:, 0:1]).then_inc(log, 1)
                    act.wait_ge(log, START + j + 1)
                    nc.scalar.activation(sq[:, p, :], sq[:, p, :], ACT.Exp, scale=-0.5).then_inc(rstd, 1)
                j = i + 1
                if has(j):
                    act.wait_ge(logits, START + j + 1)
                    if has(j - 2):
                        act.wait_ge(steps, START + ALL // 2 * (j - (1 - p) - 2) + 2)
                    half = slice(TPG * (1 - p), TPG * (2 - p))
                    nc.scalar.activation(R["exp"][:, half].rearrange("p t e -> p (t e)"),
                                         BL[:, E1 * half.start:E1 * half.stop], ACT.Exp,
                                         scale=-1.0).then_inc(exped, 1)
                j = i - 3
                if has(j):
                    act.wait_ge(turned, START + j + 1)
                    need(act, stored[1 - p], START + 8 * (j - (1 - p)))
                    nc.scalar.activation(ct[:, 1 - p, :], BTR, ACT.Copy).then_inc(turned_out, 1)

            nc.scalar.preload_act_table_set(TABLES)
            groups(act, body)

        @block.gpsimd
        def _(pool):
            def body(i, p):
                if has(i + 1):
                    pool.wait_ge(hi, START + i + 2)
                    nc.gpsimd.tensor_tensor(XL[:, group(i + 1)], xn[:], XH[:, group(i + 1)].bitcast(F32),
                                            ALU.subtract).then_inc(lo, 1)

            groups(pool, body)

        @block.vector
        def _(dve):
            def attend(j):
                dve.wait_ge(projected, START + j + 1)
                nc.vector.scalar_tensor_tensor(out=X[:, group(j)], in0=BPR, scalar=W["bvo1"][:, 0:1],
                                               in1=X[:, group(j)], op0=ALU.add, op1=ALU.add).then_inc(x3, 1)

            def norm(j, p):
                dve.wait_ge(rstd, START + j + 1)
                need(dve, logits, START + j)
                need(dve, lo, START + j)
                nc.vector.tensor_tensor(xn[:], banks_x[p], sq[:, p, :], ALU.mult).then_inc(normed, 1)
                dve.wait_ge(normed, START + j + 1)
                nc.vector.tensor_copy(XH[:, group(j)], xn[:]).then_inc(hi, 1)

            def alternate(base, part):
                done, n = [0, 0], 0
                parts = [part(0), part(1)]
                for _ in range(STEPS[part]):
                    for h in range(2):
                        dve.wait_ge(steps, START + base + done[h])
                        for instruction in next(parts[h]):
                            instruction.then_inc(steps, 1)
                            n += 1
                        done[h] = n
                assert n == COUNTS[part], n
                return n

            def of(name, h, k=None):
                v = R[name][:, TPG * h:TPG * (h + 1)]
                if k:
                    v = v.rearrange("p t e -> p (t e)")[:, 0:TPG * k].rearrange("p (t e) -> p t e", t=TPG)
                return v, v.rearrange("p t e -> p (t e)")

            def top_mask(h, v, n, keep, pick, start):
                (above, _), (on, on_flat), (rank, rank_flat) = (of(x, h, n) for x in ("above", "on", "rank"))
                top, count = R["top"][:, TPG * h:TPG * (h + 1)], R["count"][:, TPG * h:TPG * (h + 1)]
                nc.vector.memset(R["idle"][:, h], 0.0)
                yield [nc.vector.max(top[:, t, :], v[:, t, :]) for t in range(TPG)]
                least = top[:, :, keep - 1:keep].to_broadcast([128, TPG, n])
                yield [nc.vector.tensor_tensor(on, v, least, ALU.is_equal),
                       nc.vector.tensor_tensor(above, v, least, ALU.is_gt)]
                yield [nc.vector.tensor_reduce(count[:, :, 0], above, AX.X, ALU.add),
                       nc.vector.tensor_tensor_scan(rank_flat, start[:].rearrange("p t e -> p (t e)"),
                                                    on_flat, 0.0, ALU.mult, ALU.add)]
                yield [nc.vector.tensor_tensor(rank, rank, count.to_broadcast([128, TPG, n]), ALU.add)]
                yield [nc.vector.scalar_tensor_tensor(out=rank_flat, in0=rank_flat, scalar=float(keep), in1=on_flat,
                                                      op0=ALU.is_le, op1=ALU.mult)]
                yield [nc.vector.tensor_tensor(pick, rank, above, ALU.add)]

            def choose_groups(h):
                (score, score_flat), (_, exp_flat) = of("score", h), of("exp", h)
                (choice, choice_flat), (group_, group_flat) = of("choice", h), of("group", h)
                by_group = choice_flat.rearrange("p (g s) -> p g s", s=GS1)
                pick, pick_flat = of("pick_g", h)
                yield [nc.vector.tensor_scalar(score_flat, exp_flat, 1.0, None, ALU.add)]
                yield [nc.vector.reciprocal(score_flat, score_flat)]
                yield [nc.vector.tensor_tensor(choice, score, biasB[:].unsqueeze(1).to_broadcast([128, TPG, E1]),
                                               ALU.add)]
                yield [nc.vector.tensor_reduce(group_flat, by_group, AX.X, ALU.max)]
                yield from top_mask(h, group_, NG1, TOPG1, pick, seg[0])
                yield [nc.vector.tensor_tensor(by_group, by_group,
                                               pick_flat.unsqueeze(2).to_broadcast([128, TPG * NG1, GS1]),
                                               ALU.mult)]

            def choose_experts(h):
                (score, _), (weight, _), (pick, _) = of("score", h), of("weight", h), of("pick_e", h)
                total, total_flat = of("sum", h)
                yield from top_mask(h, of("choice", h)[0], E1, TOPK1, pick, seg[1])
                yield [nc.vector.tensor_tensor(weight, score, pick, ALU.mult)]
                yield [nc.vector.tensor_reduce(total[:, :, 0], weight, AX.X, ALU.add)]
                yield [nc.vector.tensor_scalar(total_flat, total_flat, 1e-20, None, ALU.add)]
                yield [nc.vector.reciprocal(total_flat, total_flat)]
                yield [nc.vector.tensor_scalar(total_flat, total_flat, SCALE1, None, ALU.mult)]

            MASK = 6
            MASK_COUNT = TPG + 2 + 2 + 3
            STEPS = {choose_groups: MASK + 5, choose_experts: MASK + 5}
            COUNTS = {part: 2 * (MASK_COUNT + 5) for part in STEPS}
            assert ALL == sum(COUNTS.values())

            def body(i, p):
                if has(i + 3):
                    attend(i + 3)
                if has(i + 1):
                    norm(i + 1, 1 - p)
                if p == 1 and has(i):
                    dve.wait_ge(exped, START + i + 1)
                    alternate(ALL // 2 * (i - 1), choose_groups)
                if p == 0 and has(i - 1):
                    n = alternate(ALL // 2 * (i - 2) + COUNTS[choose_groups], choose_experts)
                    dve.wait_ge(steps, START + ALL // 2 * (i - 2) + COUNTS[choose_groups] + n)
                    need(dve, turned, START + i - 2)
                    nc.vector.tensor_tensor(R["comb"][:], R["weight"][:],
                                            R["sum"][:].to_broadcast([128, TR, E1]), ALU.mult).then_inc(chosen, 2)

            groups(dve, body)


def second_ffn(nc, sem, P, W, X, XH, XL, WFH, WFL, c_dram, out):
    with ExitStack() as ctx:
        def sb(name, shape, dt):
            return ctx.enter_context(nc.sbuf_tensor(name, shape, dt))

        CQ = 4
        NC = (PAIRS - 1) // CQ
        CB = sb("CB", [128, 2, CQ, TG], F32)
        sg = sb("f_silu", [128, 2, TG], F32)
        au = sb("f_au", [128, 2, TG], F32)
        ac = sb("f_ac", [128, 2, TG], F32)
        hh = sb("f_hh", [128, 2, TG], F32R)
        hl = sb("f_hl", [128, 2, TG], F32R)
        o32 = sb("f_out", [128, 2, TG], F32)
        g_done, u_done, silu_done, gated = sem("f_g"), sem("f_u"), sem("f_silu_done"), sem("f_gated")
        weighted, hi, lo, summed = sem("f_weighted"), sem("f_hi"), sem("f_lo"), sem("f_summed")
        y_done, y_out = sem("f_y"), sem("f_y_out")
        c_loaded, stored = [sem("f_c0"), sem("f_c1")], [sem("f_stored0"), sem("f_stored1")]
        BG, BU, BY = [P[:, 0, :], P[:, 1, :]], [P[:, 2, :], P[:, 3, :]], [P[:, 4, :], P[:, 5, :]]
        N2 = 2 * PAIRS
        LEAD = 3
        block = ctx.enter_context(nc.Block())

        def pair(n):
            return n // PAIRS % 2, n % PAIRS

        @block.sync
        def _(sp):
            c_view = c_dram.rearrange("(k e) t -> k e t", e=2)

            def load(r, b, j):
                q = (NC * b + j) % 2
                n = NC * b + j - 2
                done = (n // NC) * (PAIRS - 1) + (n % NC + 1) * CQ
                need(sp, weighted, START + (2 * (PAIRS - 1) * r + done))
                for e in range(2):
                    src = c_view[CQ * j:CQ * j + CQ, e, group(2 * r + b)]
                    nc.sync.dma_start(CB[64 * e:64 * e + 64, q], src.partition_broadcast(64)
                                      ).then_inc(c_loaded[q], 16)

            def store(i, b, r):
                sp.wait_ge(y_out, START + i + 1)
                nc.sync.dma_start(out[:, group(i)], o32[:, b, :]).then_inc(stored[b], 16)

            def body(r):
                for b in range(2):
                    for j in range(NC):
                        load(r, b, j)
                    if b == 1:
                        store(2 * r, 0, r)
                    elif has(2 * r - 1):
                        store(2 * r - 1, 1, r)

            body(0)
            with sp.Fori(1, G // 2) as r:
                body(r)
            store(G - 1, 1, 0)
            for b in range(2):
                sp.wait_ge(stored[b], START + 8 * G)

        @block.tensor
        def _(pe):
            def up(r, n):
                b, k = pair(n)
                s = n % 2
                g = group(2 * r + n // PAIRS)
                for bank, col, done, freed in ((BG[s], 0, g_done, silu_done), (BU[s], 128, u_done, gated)):
                    need(pe, freed, START + (N2 * r + n - 1))
                    for m, (w, x) in enumerate(((WFH, XH), (WFL, XH), (WFH, XL))):
                        last = nc.tensor.matmul(bank, w[:, k, col:col + 128], x[:, g],
                                                start=(m == 0), stop=(m == 2))
                    last.then_inc(done, 1)

            def down(r, n):
                b, k = pair(n)
                s = n % 2
                if k == 0:
                    need(pe, y_out, START + (2 * r + b - 1))
                pe.wait_ge(lo, START + N2 * r + n + 1)
                for m, (w, h) in enumerate(((WFH, hh), (WFL, hh), (WFH, hl))):
                    last = nc.tensor.matmul(BY[b], w[:, k, 256:384], h[:, s, :],
                                            start=(k == 0 and m == 0), stop=(k == PAIRS - 1 and m == 2))
                last.then_inc(summed, 1)

            def step(r, last):
                for n in range(N2):
                    if n + LEAD < N2 or not last:
                        up(r, n + LEAD)
                    down(r, n)

            for n in range(LEAD):
                up(0, n)
            step(0, False)
            with pe.Fori(1, G // 2 - 1) as r:
                step(r, False)
            step(G // 2 - 1, True)

        @block.scalar
        def _(act):
            def body(r):
                for n in range(N2):
                    s = n % 2
                    act.wait_ge(g_done, START + N2 * r + n + 1)
                    need(act, gated, START + (N2 * r + n - 1))
                    nc.scalar.activation(sg[:, s, :], BG[s], ACT.Silu).then_inc(silu_done, 1)

            body(0)
            with act.Fori(1, G // 2) as r:
                body(r)

        @block.gpsimd
        def _(pool):
            def body(r):
                m = 0
                for n in range(N2):
                    b, k = pair(n)
                    s = n % 2
                    if k == PAIRS - 1:
                        continue
                    j = NC * b + k // CQ
                    if k % CQ == 0:
                        pool.wait_ge(c_loaded[j % 2], START + 32 * (NC * r + j // 2 + 1))
                    pool.wait_ge(gated, START + N2 * r + n + 1)
                    need(pool, lo, START + (N2 * r + n - 1))
                    nc.gpsimd.tensor_tensor(ac[:, s, :], au[:, s, :], CB[:, j % 2, k % CQ, :],
                                            ALU.mult).then_inc(weighted, 1)

            body(0)
            with pool.Fori(1, G // 2) as r:
                body(r)

        @block.vector
        def _(dve):
            def gate(r, n):
                s = n % 2
                dve.wait_ge(silu_done, START + N2 * r + n + 1)
                dve.wait_ge(u_done, START + N2 * r + n + 1)
                need(dve, lo, START + (N2 * r + n - 1))
                nc.vector.tensor_tensor(au[:, s, :], sg[:, s, :], BU[s], ALU.mult).then_inc(gated, 1)

            def split(r, n):
                b, k = pair(n)
                s = n % 2
                shared = k == PAIRS - 1
                src = au if shared else ac
                if shared:
                    dve.wait_ge(gated, START + N2 * r + n + 1)
                else:
                    dve.wait_ge(weighted, START + 2 * (PAIRS - 1) * r + b * (PAIRS - 1) + k + 1)
                need(dve, summed, START + (N2 * r + n - 1))
                nc.vector.tensor_copy(hh[:, s, :], src[:, s, :]).then_inc(hi, 1)
                dve.wait_ge(hi, START + N2 * r + n + 1)
                nc.vector.tensor_tensor(hl[:, s, :], src[:, s, :], hh[:, s, :].bitcast(F32),
                                        ALU.subtract).then_inc(lo, 1)

            def result(r, b):
                i = 2 * r + b
                dve.wait_ge(summed, START + N2 * r + PAIRS * (b + 1))
                need(dve, stored[b], START + 16 * r)
                nc.vector.scalar_tensor_tensor(out=o32[:, b, :], in0=BY[b], scalar=W["gf"][:, 1:2],
                                               in1=X[:, group(i)], op0=ALU.mult, op1=ALU.add).then_inc(y_out, 1)

            def body(r):
                for n in range(N2):
                    gate(r, n)
                    if n:
                        split(r, n - 1)
                    if n == LEAD + 1 and has(2 * r - 1):
                        result(r - 1, 1)
                    if n == PAIRS + LEAD + 1:
                        result(r, 0)
                split(r, N2 - 1)

            body(0)
            with dve.Fori(1, G // 2) as r:
                body(r)
            result(G // 2 - 1, 1)


def shared_constants(nc, semaphores, W, ins):
    def start(eng, k):
        for name in SEMAPHORES[k::5]:
            eng.sem_inc(semaphores[name], START)

    with ExitStack() as ctx:
        loaded = ctx.enter_context(nc.semaphore("const_loaded"))
        done = ctx.enter_context(nc.semaphore("const_done"))
        made = ctx.enter_context(nc.semaphore("centre_made"))
        block = ctx.enter_context(nc.Block())
        dmas = []

        @block.sync
        def _(sp):
            def load(dst, src):
                nc.sync.dma_start(dst, src).then_inc(loaded, 16)
                dmas.append(1)

            def column(v):
                return v.rearrange("(p a) -> p a", a=1)

            load(W["wq0"][:], ins["L0_xattn_Wq"])
            load(W["wk0"][:], ins["L0_xattn_Wk"])
            load(W["wv0"][:], ins["L0_xattn_Wv"])
            sp.wait_ge(done, 1)
            for u in range(2):
                load(W["wo0"][64 * u:64 * u + 64, u], ins["L0_xattn_Wo"].rearrange("(a r) d -> r a d", a=2))
            load(W["gw0"][:], ins["gate0T"])
            load(W["bq0"][:], column(ins["L0_xattn_bq"]))
            load(W["bk0"][:], column(ins["L0_xattn_bk"]))
            load(W["bo0"][:], column(ins["L0_xattn_bo"]))
            load(W["bv0"][:], ins["L0_xattn_bv"].partition_broadcast(128))
            load(W["gx"][:], ins["g_xattn"].partition_broadcast(128))
            load(W["gf"][:], ins["g_ffn"].partition_broadcast(128))
            start(sp, 2)

        n_loaded = 16 * len(dmas)

        @block.vector
        def _(dve):
            start(dve, 0)
            nc.vector.memset(W["wo0"][:], 0.0).then_inc(done, 1)
            nc.vector.memset(W["mean"][:], 1.0 / D).then_inc(done, 1)
            nc.vector.memset(W["ones"][:], 1.0).then_inc(done, 1)
            nc.vector.memset(W["one_row"][:], 1.0).then_inc(done, 1)
            nc.vector.memset(W["eps"][:], EPS).then_inc(done, 1)
            dve.wait_ge(done, 7)
            dve.wait_ge(loaded, n_loaded)
            nc.vector.tensor_scalar(W["wo0"][:].rearrange("p u a d -> p (u a d)"),
                                    W["wo0"][:].rearrange("p u a d -> p (u a d)"),
                                    W["gx"][:, 0:1], None, ALU.mult).then_inc(done, 1)
            nc.vector.tensor_scalar(W["bo0"][:], W["bo0"][:], W["gx"][:, 0:1], None, ALU.mult).then_inc(done, 1)

        @block.tensor
        def _(pe):
            start(pe, 3)

        @block.gpsimd
        def _(pool):
            start(pool, 4)
            nc.gpsimd.memset(W["centre"][:], 1.0 - 1.0 / D).then_inc(made, 1)
            pool.wait_ge(made, 1)
            nc.gpsimd.affine_select(out=W["centre"][:], in_=W["centre"][:], compare_op=ALU.is_equal,
                                    fill=-1.0 / D, base=0, pattern=[[1, 128]],
                                    channel_multiplier=-1).then_inc(made, 1)
            pool.wait_ge(made, 2)

        @block.scalar
        def _(act):
            start(act, 1)
            act.wait_ge(loaded, n_loaded)
            nc.scalar.activation(W["gx"][:], W["gx"][:], ACT.Tanh).then_inc(done, 1)
            nc.scalar.activation(W["gf"][:], W["gf"][:], ACT.Tanh).then_inc(done, 1)


def program(nc, ins, out):
    with ExitStack() as ctx:
        ctx.enter_context(nc.allow_low_precision(reason="operands split in halves"))
        semaphores = {name: ctx.enter_context(nc.semaphore(name)) for name in SEMAPHORES}
        sem = semaphores.__getitem__

        def sb(name, shape, dt):
            return ctx.enter_context(nc.sbuf_tensor(name, shape, dt))

        P = ctx.enter_context(nc.psum_tensor("P", [128, 8, TG], F32))
        W = {n: sb("w_" + n, s, F32) for n, s in {
            "wq0": [128, 128], "wk0": [128, 128], "wv0": [128, 128], "wo0": [128, 2, 2, 128],
            "gw0": [128, E0], "bq0": [128, 1], "bk0": [128, 1], "bo0": [128, 1], "bv0": [128, 128],
            "gx": [128, 2], "gf": [128, 2], "mean": [128, 128], "centre": [128, 128], "ones": [128, 128], "eps": [128, 1],
            "one_row": [128, TG], "wvo1": [128, 128], "bvo1": [128, 1],
        }.items()}
        XH = sb("XH", [128, T], F32R)
        XL = sb("XL", [128, T], F32R)
        SC = sb("SC", [128, E0, NT], F32)
        scratch = nc.dram_tensor("qk_scratch", [2, 2, 2, 128, TG], F16)
        x1_dram = nc.dram_tensor("x1_dram", [128, T], F32)
        shared_constants(nc, semaphores, W, ins)
        attention(nc, sem, P, W, XH, XL, SC, ins["xT"], ins["ctxT"], scratch.ap(), x1_dram.ap())
        gate_dram = nc.dram_tensor("gate_dram", [E0, T], F32)
        X = sb("X", [128, T], F32)
        first_ffn(nc, sem, P, W, X, XH, XL, SC, ins["experts0"], x1_dram.ap(), gate_dram.ap())
        we_dram = nc.dram_tensor("we_dram", [NB, 2 * L], F32)
        c_dram = nc.dram_tensor("c_dram", [E1, T], F32)
        WFH = sb("WFH", [128, PAIRS, 3 * 128], F32R)
        WFL = sb("WFL", [128, PAIRS, 3 * 128], F32R)
        delay_weights(nc, sem, P, W, X, WFH, WFL, ins["ctxT"], ins, we_dram.ap())
        delays_and_routes(nc, sem, P, W, X, XH, XL, ins, we_dram.ap(), c_dram.ap())
        second_ffn(nc, sem, P, W, X, XH, XL, WFH, WFL, c_dram.ap(), out)


def kernel(**inputs):
    import numpy as np
    import concourse.bacc as bacc
    from concourse.bass_utils import run_bass_kernel_spmd as run

    a = {k: np.asarray(v) for k, v in inputs.items()}
    laid = {k: a[k] for k in ("g_xattn", "g_ffn", "L0_xattn_Wq", "L0_xattn_bq", "L0_xattn_Wk", "L0_xattn_bk",
                              "L0_xattn_Wv", "L0_xattn_bv", "L0_xattn_Wo", "L0_xattn_bo")}
    laid["xT"] = a["x"].reshape(T, D).T
    laid["ctxT"] = a["ctx_1024"].reshape(T, D).T
    laid["gate0T"] = a["L0_ffn_gate_weight"].T
    laid["ctxN"] = a["ctx_1024"][:, ::-1, :].reshape(T, D)
    laid["wq1T"] = a["L1_xattn_Wq"].T
    laid["wk1T"] = a["L1_xattn_Wk"].T
    laid["wo1T"] = a["L1_xattn_Wo"].T
    laid["gate1T"] = a["L1_ffn_gate_weight"].T
    laid.update({k: a[k] for k in ("L1_xattn_Wv", "L1_xattn_bq", "L1_xattn_bk", "L1_xattn_bv", "L1_xattn_bo",
                                   "L1_ffn_e_score_correction_bias")})
    gu = np.concatenate([a["L1_ffn_experts_gate_up"].reshape(E1 // 2, 2, 2, I1, D).transpose(0, 2, 1, 3, 4),
                         np.stack([a["L1_ffn_shared_gate_w"], a["L1_ffn_shared_up_w"]]).reshape(1, 2, 2, I1, D)])
    down = np.concatenate([a["L1_ffn_experts_down"].transpose(0, 2, 1).reshape(E1 // 2, 2 * I1, D),
                           a["L1_ffn_shared_down_w"].T[None]])
    laid["experts1"] = np.concatenate([gu.reshape(PAIRS, 4 * I1, D).transpose(2, 0, 1), down.transpose(1, 0, 2)],
                                      axis=2)

    def rows(w1, b1, w2, b2):
        e = w1.shape[0]
        w2c = w2.reshape(e, FC, 128, D).transpose(0, 2, 1, 3).reshape(e, 128, FC * D)
        b1c = b1.reshape(e, FC, 128).transpose(0, 2, 1)
        return np.concatenate([w1, w2c, b1c, b2[:, :, None]], axis=2)

    laid["experts0"] = np.concatenate([
        rows(a["L0_ffn_Ws1"][None], a["L0_ffn_bs1"][None], a["L0_ffn_Ws2"][None], a["L0_ffn_bs2"][None]),
        rows(a["L0_ffn_W1"], a["L0_ffn_b1"], a["L0_ffn_W2"], a["L0_ffn_b2"])])
    nc = bacc.Bacc("TRN2", target_bir_lowering=False, num_devices=1)
    arrays, ins = {}, {}
    for name, v in laid.items():
        v = np.ascontiguousarray(v)
        arrays[f"in_{name}"] = v
        ins[name] = nc.dram_tensor(f"in_{name}", v.shape, mybir.dt.from_np(v.dtype), kind="ExternalInput").ap()
    out = nc.dram_tensor("out_T", [D, T], F32, kind="ExternalOutput")
    program(nc, ins, out.ap())
    r = run(nc, [arrays], core_ids=[0])
    return np.ascontiguousarray(r.results[0]["out_T"].T).reshape(NB, L, D)
```
